# Optimizing a Trainium2 kernel written in Bass

```python
import numpy as np
import jax
import jax.numpy as jnp

def _softmax(x, axis=-1):
    return jax.nn.softmax(x, axis=axis)

def _gelu(x):
    return jax.nn.gelu(x, approximate=True)

def _silu(x):
    return jax.nn.silu(x)

def _sigmoid(x):
    return jax.nn.sigmoid(x)

def _layernorm(x, axis=-1, eps=1e-05):
    m = jnp.mean(x, axis=axis, keepdims=True)
    v = jnp.var(x, axis=axis, keepdims=True)
    return (x - m) / jnp.sqrt(v + eps)

def _scatter_add(tgt, idx, src, axis=0):
    return tgt.at[idx].add(src)

def _segment_sum(src, seg, n):
    return jax.ops.segment_sum(src, seg, n)
kernel_name = 'mk_decoder_postln_d1_seqx_r8_22f5be'

def setup_inputs(seed: int=0):
    np.random.seed(seed)
    _w = jnp.asarray

    def _rec_inputs():
        import jax
        import jax.numpy as jnp
        _rk = jax.random.key(seed)
        x = -0.0003929 + 0.9999 * jax.random.normal(jax.random.fold_in(_rk, 1), (4, 256, 256), jnp.float32)
        _lenS = 256 - jax.random.randint(jax.random.fold_in(_rk, 7), (4,), 0, max(1, 256 // 4) + 1, jnp.int32)
        _lenS2 = 64 - jax.random.randint(jax.random.fold_in(_rk, 8), (4,), 0, max(1, 64 // 4) + 1, jnp.int32)
        _ctx_1024P = jax.random.normal(jax.random.fold_in(_rk, 11), (4, 16, 128), jnp.float32)
        _ctx_1024c = jax.random.dirichlet(jax.random.fold_in(_rk, 511), 0.3 * jnp.ones((16,), jnp.float32), (4, 64))
        _ctx_1024t = jnp.einsum('bsk,bkd->bsd', _ctx_1024c, _ctx_1024P)
        _ctx_1024t = _ctx_1024t * jax.lax.rsqrt(jnp.mean(jnp.square(_ctx_1024t)) + 1e-12) * 0.953939
        ctx_1024 = 0.000227908 + 0.99994 * (_ctx_1024t + 0.3 * jax.random.normal(jax.random.fold_in(_rk, 611), (4, 64, 128), jnp.float32))
        return (x, ctx_1024)
    x, ctx_1024 = _rec_inputs()

    def _L0_attn_setup():
        import jax, jax.numpy as jnp
        import numpy as np
        EPS = 1e-06

        def rmsnorm(x, w):
            var = jnp.mean(x * x, axis=-1, keepdims=True)
            return x * jax.lax.rsqrt(var + EPS) * w

        def _reference_tuple_inner(hidden_states, ln_in_w, in_proj_w, conv_w, conv_b, x_proj_w, dt_ln_w, b_ln_w, c_ln_w, dt_proj_w, dt_proj_b, A_log, D_param, out_proj_w, ln_ff_w, router_w, w1, w3, w2):
            Bb, L, D = hidden_states.shape
            Di = in_proj_w.shape[0] // 2
            N = b_ln_w.shape[0]
            R = dt_ln_w.shape[0]
            K = conv_w.shape[1]
            E = router_w.shape[0]
            TOP_K = 2
            residual = hidden_states
            hs = rmsnorm(hidden_states, ln_in_w)
            xz = hs @ in_proj_w.T
            x, z = jnp.split(xz, 2, axis=-1)
            xt = jnp.moveaxis(x, 1, 2)
            xc = jax.lax.conv_general_dilated(xt, conv_w[:, None, :], (1,), [(K - 1, 0)], dimension_numbers=('NCH', 'OIH', 'NCH'), feature_group_count=Di)
            xc = jax.nn.silu(xc + conv_b[None, :, None])
            xc = jnp.moveaxis(xc, 1, 2)
            xdb = xc @ x_proj_w.T
            dt, Bm, Cm = jnp.split(xdb, [R, R + N], axis=-1)
            dt = rmsnorm(dt, dt_ln_w)
            Bm = rmsnorm(Bm, b_ln_w)
            Cm = rmsnorm(Cm, c_ln_w)
            dt = jax.nn.softplus(dt @ dt_proj_w.T + dt_proj_b)
            A = -jnp.exp(A_log)

            def step(h, inps):
                dt_t, x_t, B_t, C_t = inps
                dA = jnp.exp(dt_t[..., None] * A)
                h = h * dA + (dt_t * x_t)[..., None] * B_t[:, None, :]
                y = jnp.einsum('bdn,bn->bd', h, C_t)
                return (h, y)
            h0 = jnp.zeros((Bb, Di, N), hs.dtype)
            xs = (jnp.moveaxis(dt, 0, 1), jnp.moveaxis(xc, 0, 1), jnp.moveaxis(Bm, 0, 1), jnp.moveaxis(Cm, 0, 1))
            _, ys = jax.lax.scan(step, h0, xs)
            y = jnp.moveaxis(ys, 0, 1)
            y = y + xc * D_param
            y = y * jax.nn.silu(z)
            mamba_out = y @ out_proj_w.T
            residual = mamba_out + residual
            hs = rmsnorm(residual, ln_ff_w)
            T = Bb * L
            flat = hs.reshape(T, D)
            logits = flat @ router_w.T
            probs = jax.nn.softmax(logits, axis=-1)
            topv, topi = jax.lax.top_k(probs, TOP_K)
            gate_w = jnp.sum(jax.nn.one_hot(topi, E, dtype=flat.dtype) * topv[..., None], axis=1)
            g = jnp.einsum('td,eid->tei', flat, w1)
            u = jnp.einsum('td,eid->tei', flat, w3)
            yexp = jnp.einsum('tei,edi->ted', jax.nn.silu(g) * u, w2)
            moe_out = jnp.einsum('ted,te->td', yexp, gate_w).reshape(Bb, L, D)
            return (moe_out, residual)
        key = jax.random.key(seed)
        ks = jax.random.split(key, 16)
        B, L, D = (1, 128, 256)
        Di, N, K, R = (512, 16, 4, 128)
        I, E = (704, 8)
        s = 0.02
        inp = {}
        inp['hidden_states'] = jax.random.normal(ks[0], (B, L, D), jnp.float32)
        inp['ln_in_w'] = jnp.ones((D,), jnp.float32)
        inp['in_proj_w'] = jax.random.normal(ks[1], (2 * Di, D), jnp.float32) * s
        inp['conv_w'] = jax.random.normal(ks[2], (Di, K), jnp.float32) * 0.1
        inp['conv_b'] = jnp.zeros((Di,), jnp.float32)
        inp['x_proj_w'] = jax.random.normal(ks[3], (R + 2 * N, Di), jnp.float32) * s
        inp['dt_ln_w'] = jnp.ones((R,), jnp.float32)
        inp['b_ln_w'] = jnp.ones((N,), jnp.float32)
        inp['c_ln_w'] = jnp.ones((N,), jnp.float32)
        inp['dt_proj_w'] = jax.random.normal(ks[4], (Di, R), jnp.float32) * s
        inp['dt_proj_b'] = jax.random.uniform(ks[5], (Di,), jnp.float32, -4.0, -2.0)
        inp['A_log'] = jnp.log(jnp.broadcast_to(jnp.arange(1, N + 1, dtype=jnp.float32), (Di, N)))
        inp['D_param'] = jnp.ones((Di,), jnp.float32)
        inp['out_proj_w'] = jax.random.normal(ks[6], (D, Di), jnp.float32) * s
        inp['ln_ff_w'] = jnp.ones((D,), jnp.float32)
        inp['router_w'] = jax.random.normal(ks[7], (E, D), jnp.float32) * s
        inp['w1'] = jax.random.normal(ks[8], (E, I, D), jnp.float32) * s
        inp['w3'] = jax.random.normal(ks[9], (E, I, D), jnp.float32) * s
        inp['w2'] = jax.random.normal(ks[10], (E, D, I), jnp.float32) * s
        return inp
    _L0_attn_all = _L0_attn_setup()
    _L0_attn_in = {k: v for k, v in _L0_attn_all.items() if k in ('ln_in_w', 'in_proj_w', 'conv_w', 'conv_b', 'x_proj_w', 'dt_ln_w', 'b_ln_w', 'c_ln_w', 'dt_proj_w', 'dt_proj_b', 'A_log', 'D_param', 'out_proj_w', 'ln_ff_w', 'router_w', 'w1', 'w3', 'w2')}
    del _L0_attn_all

    def _L0_xattn_setup():
        import jax, jax.numpy as jnp
        import numpy as np
        EPS = 1e-05

        def rmsnorm(x, g, eps=EPS):
            var = jnp.mean(jnp.square(x), axis=-1, keepdims=True)
            return x * jax.lax.rsqrt(var + eps) * g
        key = jax.random.key(seed)
        ks = jax.random.split(key, 8)
        B, Sq, Skv = (2, 512, 64)
        dim, cdim, H, D = (256, 128, 16, 128)
        inner = H * D
        s = lambda f: 1.0 / np.sqrt(f)
        return {'hidden_states': jax.random.normal(ks[0], (B, Sq, dim), jnp.float32), 'encoder_hidden_states': jax.random.normal(ks[1], (B, Skv, cdim), jnp.float32), 'Wq': jax.random.normal(ks[2], (dim, inner), jnp.float32) * s(dim), 'Wk': jax.random.normal(ks[3], (cdim, inner), jnp.float32) * s(cdim), 'Wv': jax.random.normal(ks[4], (cdim, inner), jnp.float32) * s(cdim), 'Wo': jax.random.normal(ks[5], (inner, dim), jnp.float32) * s(inner), 'gq': jnp.ones((D,), jnp.float32), 'gk': jnp.ones((D,), jnp.float32)}
    _L0_xattn_all = _L0_xattn_setup()
    _L0_xattn_in = {k: v for k, v in _L0_xattn_all.items() if k in ('Wq', 'Wk', 'Wv', 'Wo', 'gq', 'gk')}
    del _L0_xattn_all

    def _L0_ffn_setup():
        import jax, jax.numpy as jnp
        import numpy as np
        FP8_MAX = 448.0
        GLOBAL_DIV = 448.0 * 6.0

        def _fp8(x):
            return x.astype(jnp.float8_e4m3fn).astype(jnp.float32)

        def _reorder_quantize_x(x, idx):
            scale = jnp.max(jnp.abs(x)) / GLOBAL_DIV
            xr = (x / scale)[:, idx]
            scale_x = jnp.max(jnp.abs(xr), axis=1, keepdims=True) / FP8_MAX
            qx = _fp8(xr / scale_x)
            return (qx, scale_x, scale)

        def _qlinear(qx, scale_x, scale, W, idx, out_idx=None):
            Wr = W[:, idx]
            w_scale = jnp.max(jnp.abs(Wr), axis=1, keepdims=True) / FP8_MAX
            qw = _fp8(Wr / w_scale)
            y = qx * scale_x @ (qw * w_scale).T * scale
            if out_idx is not None:
                y = y[:, out_idx]
            return y
        key = jax.random.key(seed)
        ks = jax.random.split(key, 6)
        B, S, H, I = (2, 128, 256, 704)
        return {'x': jax.random.normal(ks[0], (B, S, H), jnp.float32), 'w_gate': jax.random.normal(ks[1], (I, H), jnp.float32) * 0.02, 'w_up': jax.random.normal(ks[2], (I, H), jnp.float32) * 0.02, 'w_down': jax.random.normal(ks[3], (H, I), jnp.float32) * 0.02, 'up_reorder_index': jax.random.permutation(ks[4], jnp.arange(H, dtype=jnp.int64)), 'down_reorder_index': jax.random.permutation(ks[5], jnp.arange(I, dtype=jnp.int64))}
    _L0_ffn_all = _L0_ffn_setup()
    _L0_ffn_in = {k: v for k, v in _L0_ffn_all.items() if k in ('w_gate', 'w_up', 'w_down', 'up_reorder_index', 'down_reorder_index')}
    del _L0_ffn_all
    return {'x': x, 'ctx_1024': ctx_1024, 'L0_attn_ln_in_w': _L0_attn_in['ln_in_w'], 'L0_attn_in_proj_w': _L0_attn_in['in_proj_w'], 'L0_attn_conv_w': _L0_attn_in['conv_w'], 'L0_attn_conv_b': _L0_attn_in['conv_b'], 'L0_attn_x_proj_w': _L0_attn_in['x_proj_w'], 'L0_attn_dt_ln_w': _L0_attn_in['dt_ln_w'], 'L0_attn_b_ln_w': _L0_attn_in['b_ln_w'], 'L0_attn_c_ln_w': _L0_attn_in['c_ln_w'], 'L0_attn_dt_proj_w': _L0_attn_in['dt_proj_w'], 'L0_attn_dt_proj_b': _L0_attn_in['dt_proj_b'], 'L0_attn_A_log': _L0_attn_in['A_log'], 'L0_attn_D_param': _L0_attn_in['D_param'], 'L0_attn_out_proj_w': _L0_attn_in['out_proj_w'], 'L0_attn_ln_ff_w': _L0_attn_in['ln_ff_w'], 'L0_attn_router_w': _L0_attn_in['router_w'], 'L0_attn_w1': _L0_attn_in['w1'], 'L0_attn_w3': _L0_attn_in['w3'], 'L0_attn_w2': _L0_attn_in['w2'], 'L0_xattn_Wq': _L0_xattn_in['Wq'], 'L0_xattn_Wk': _L0_xattn_in['Wk'], 'L0_xattn_Wv': _L0_xattn_in['Wv'], 'L0_xattn_Wo': _L0_xattn_in['Wo'], 'L0_xattn_gq': _L0_xattn_in['gq'], 'L0_xattn_gk': _L0_xattn_in['gk'], 'L0_ffn_w_gate': _L0_ffn_in['w_gate'], 'L0_ffn_w_up': _L0_ffn_in['w_up'], 'L0_ffn_w_down': _L0_ffn_in['w_down'], 'L0_ffn_up_reorder_index': _L0_ffn_in['up_reorder_index'], 'L0_ffn_down_reorder_index': _L0_ffn_in['down_reorder_index']}

def reference(x, ctx_1024, L0_attn_ln_in_w, L0_attn_in_proj_w, L0_attn_conv_w, L0_attn_conv_b, L0_attn_x_proj_w, L0_attn_dt_ln_w, L0_attn_b_ln_w, L0_attn_c_ln_w, L0_attn_dt_proj_w, L0_attn_dt_proj_b, L0_attn_A_log, L0_attn_D_param, L0_attn_out_proj_w, L0_attn_ln_ff_w, L0_attn_router_w, L0_attn_w1, L0_attn_w3, L0_attn_w2, L0_xattn_Wq, L0_xattn_Wk, L0_xattn_Wv, L0_xattn_Wo, L0_xattn_gq, L0_xattn_gk, L0_ffn_w_gate, L0_ffn_w_up, L0_ffn_w_down, L0_ffn_up_reorder_index, L0_ffn_down_reorder_index):
    import jax
    import jax.numpy as jnp

    def _L0_attn_ref(hidden_states, ln_in_w, in_proj_w, conv_w, conv_b, x_proj_w, dt_ln_w, b_ln_w, c_ln_w, dt_proj_w, dt_proj_b, A_log, D_param, out_proj_w, ln_ff_w, router_w, w1, w3, w2):
        import jax, jax.numpy as jnp
        import numpy as np
        EPS = 1e-06

        def rmsnorm(x, w):
            var = jnp.mean(x * x, axis=-1, keepdims=True)
            return x * jax.lax.rsqrt(var + EPS) * w

        def _reference_tuple_inner(hidden_states, ln_in_w, in_proj_w, conv_w, conv_b, x_proj_w, dt_ln_w, b_ln_w, c_ln_w, dt_proj_w, dt_proj_b, A_log, D_param, out_proj_w, ln_ff_w, router_w, w1, w3, w2):
            Bb, L, D = hidden_states.shape
            Di = in_proj_w.shape[0] // 2
            N = b_ln_w.shape[0]
            R = dt_ln_w.shape[0]
            K = conv_w.shape[1]
            E = router_w.shape[0]
            TOP_K = 2
            residual = hidden_states
            hs = rmsnorm(hidden_states, ln_in_w)
            xz = hs @ in_proj_w.T
            x, z = jnp.split(xz, 2, axis=-1)
            xt = jnp.moveaxis(x, 1, 2)
            xc = jax.lax.conv_general_dilated(xt, conv_w[:, None, :], (1,), [(K - 1, 0)], dimension_numbers=('NCH', 'OIH', 'NCH'), feature_group_count=Di)
            xc = jax.nn.silu(xc + conv_b[None, :, None])
            xc = jnp.moveaxis(xc, 1, 2)
            xdb = xc @ x_proj_w.T
            dt, Bm, Cm = jnp.split(xdb, [R, R + N], axis=-1)
            dt = rmsnorm(dt, dt_ln_w)
            Bm = rmsnorm(Bm, b_ln_w)
            Cm = rmsnorm(Cm, c_ln_w)
            dt = jax.nn.softplus(dt @ dt_proj_w.T + dt_proj_b)
            A = -jnp.exp(A_log)

            def step(h, inps):
                dt_t, x_t, B_t, C_t = inps
                dA = jnp.exp(dt_t[..., None] * A)
                h = h * dA + (dt_t * x_t)[..., None] * B_t[:, None, :]
                y = jnp.einsum('bdn,bn->bd', h, C_t)
                return (h, y)
            h0 = jnp.zeros((Bb, Di, N), hs.dtype)
            xs = (jnp.moveaxis(dt, 0, 1), jnp.moveaxis(xc, 0, 1), jnp.moveaxis(Bm, 0, 1), jnp.moveaxis(Cm, 0, 1))
            _, ys = jax.lax.scan(step, h0, xs)
            y = jnp.moveaxis(ys, 0, 1)
            y = y + xc * D_param
            y = y * jax.nn.silu(z)
            mamba_out = y @ out_proj_w.T
            residual = mamba_out + residual
            hs = rmsnorm(residual, ln_ff_w)
            T = Bb * L
            flat = hs.reshape(T, D)
            logits = flat @ router_w.T
            probs = jax.nn.softmax(logits, axis=-1)
            topv, topi = jax.lax.top_k(probs, TOP_K)
            gate_w = jnp.sum(jax.nn.one_hot(topi, E, dtype=flat.dtype) * topv[..., None], axis=1)
            g = jnp.einsum('td,eid->tei', flat, w1)
            u = jnp.einsum('td,eid->tei', flat, w3)
            yexp = jnp.einsum('tei,edi->ted', jax.nn.silu(g) * u, w2)
            moe_out = jnp.einsum('ted,te->td', yexp, gate_w).reshape(Bb, L, D)
            return (moe_out, residual)
        return _reference_tuple_inner(hidden_states, ln_in_w, in_proj_w, conv_w, conv_b, x_proj_w, dt_ln_w, b_ln_w, c_ln_w, dt_proj_w, dt_proj_b, A_log, D_param, out_proj_w, ln_ff_w, router_w, w1, w3, w2)[0]

    def _L0_xattn_ref(hidden_states, encoder_hidden_states, Wq, Wk, Wv, Wo, gq, gk):
        import jax, jax.numpy as jnp
        import numpy as np
        EPS = 1e-05

        def rmsnorm(x, g, eps=EPS):
            var = jnp.mean(jnp.square(x), axis=-1, keepdims=True)
            return x * jax.lax.rsqrt(var + eps) * g
        B, Sq, _ = hidden_states.shape
        Skv = encoder_hidden_states.shape[1]
        D = gq.shape[0]
        H = Wq.shape[1] // D
        scale = 1.0 / np.sqrt(D)
        q = (hidden_states @ Wq).reshape(B, Sq, H, D)
        k = (encoder_hidden_states @ Wk).reshape(B, Skv, H, D)
        v = (encoder_hidden_states @ Wv).reshape(B, Skv, H, D)
        q = rmsnorm(q, gq)
        k = rmsnorm(k, gk)
        scores = jnp.einsum('bqhd,bkhd->bhqk', q, k) * scale
        attn = jax.nn.softmax(scores, axis=-1)
        out = jnp.einsum('bhqk,bkhd->bqhd', attn, v)
        out = out.reshape(B, Sq, H * D)
        return out @ Wo

    def _L0_ffn_ref(x, w_gate, w_up, w_down, up_reorder_index, down_reorder_index):
        import jax, jax.numpy as jnp
        import numpy as np
        FP8_MAX = 448.0
        GLOBAL_DIV = 448.0 * 6.0

        def _fp8(x):
            return x.astype(jnp.float8_e4m3fn).astype(jnp.float32)

        def _reorder_quantize_x(x, idx):
            scale = jnp.max(jnp.abs(x)) / GLOBAL_DIV
            xr = (x / scale)[:, idx]
            scale_x = jnp.max(jnp.abs(xr), axis=1, keepdims=True) / FP8_MAX
            qx = _fp8(xr / scale_x)
            return (qx, scale_x, scale)

        def _qlinear(qx, scale_x, scale, W, idx, out_idx=None):
            Wr = W[:, idx]
            w_scale = jnp.max(jnp.abs(Wr), axis=1, keepdims=True) / FP8_MAX
            qw = _fp8(Wr / w_scale)
            y = qx * scale_x @ (qw * w_scale).T * scale
            if out_idx is not None:
                y = y[:, out_idx]
            return y
        B, S, H = x.shape
        xf = x.reshape(B * S, H)
        qx, sx, sc = _reorder_quantize_x(xf, up_reorder_index)
        g = _qlinear(qx, sx, sc, w_gate, up_reorder_index, out_idx=down_reorder_index)
        u = _qlinear(qx, sx, sc, w_up, up_reorder_index, out_idx=down_reorder_index)
        t = jax.nn.silu(g) * u
        qt, st, sct = _reorder_quantize_x(t, down_reorder_index)
        y = _qlinear(qt, st, sct, w_down, down_reorder_index)
        return y.reshape(B, S, H)
    x = _layernorm(x + _L0_attn_ref(x, L0_attn_ln_in_w, L0_attn_in_proj_w, L0_attn_conv_w, L0_attn_conv_b, L0_attn_x_proj_w, L0_attn_dt_ln_w, L0_attn_b_ln_w, L0_attn_c_ln_w, L0_attn_dt_proj_w, L0_attn_dt_proj_b, L0_attn_A_log, L0_attn_D_param, L0_attn_out_proj_w, L0_attn_ln_ff_w, L0_attn_router_w, L0_attn_w1, L0_attn_w3, L0_attn_w2), axis=-1)
    x = _layernorm(x + _L0_xattn_ref(x, ctx_1024, L0_xattn_Wq, L0_xattn_Wk, L0_xattn_Wv, L0_xattn_Wo, L0_xattn_gq, L0_xattn_gk), axis=-1)
    x = _layernorm(x + _L0_ffn_ref(x, L0_ffn_w_gate, L0_ffn_w_up, L0_ffn_w_down, L0_ffn_up_reorder_index, L0_ffn_down_reorder_index), axis=-1)
    return x

_drawn_inputs = setup_inputs


def setup_inputs(seed=0):
    import zlib

    import numpy as np

    out = dict(_drawn_inputs(seed))
    spreads = {'L0_attn_ln_in_w': (1.0, 0.6),
     'L0_attn_conv_b': (0.0, 0.8),
     'L0_attn_dt_ln_w': (1.0, 0.6),
     'L0_attn_b_ln_w': (1.0, 0.6),
     'L0_attn_c_ln_w': (1.0, 0.6),
     'L0_attn_D_param': (1.0, 0.6),
     'L0_attn_ln_ff_w': (1.0, 0.6),
     'L0_xattn_gq': (1.0, 0.2),
     'L0_xattn_gk': (1.0, 0.2)}
    factors = {'L0_attn_in_proj_w': 8.0,
     'L0_attn_conv_w': 8.0,
     'L0_attn_x_proj_w': 8.0,
     'L0_attn_dt_proj_w': 8.0,
     'L0_attn_dt_proj_b': 8.0,
     'L0_attn_A_log': 8.0,
     'L0_attn_out_proj_w': 8.0,
     'L0_attn_router_w': 8.0,
     'L0_attn_w1': 7.962,
     'L0_attn_w3': 7.891,
     'L0_attn_w2': 7.881}
    for name, (base, spread) in spreads.items():
        noise = np.random.default_rng([zlib.crc32(name.encode()), seed]).standard_normal(out[name].shape)
        drawn = base * np.exp(spread * noise) if base else spread * noise
        out[name] = jnp.asarray(drawn.astype(out[name].dtype))
    for name, factor in factors.items():
        out[name] = (out[name] * factor).astype(out[name].dtype)
    return out
```

```python
from contextlib import ExitStack

import numpy as np

import concourse.bass as bass
from concourse import mybir

F32, BF16 = mybir.dt.float32, mybir.dt.bfloat16
I32, U32 = mybir.dt.int32, mybir.dt.uint32
ALU, ACT, AX = mybir.AluOpType, mybir.ActivationFunctionType, mybir.AxisListType

P = 128
BATCH, SEQ, D = 4, 256, 256
T = BATCH * SEQ
TILES = T // P
KD = D // P
HALF = 512
DI, NS, DR, TAPS = 512, 16, 128, 4
CI = DI // P
XP = DR + 2 * NS
UNITS = CI * NS
LANES = (("conv_w", TAPS), ("conv_b", 1), ("dt_b", 1), ("d_param", 1), ("a_log", NS))
E, FF = 8, 704
FCH = -(-FF // P)
MOE_W = 3 * FCH * D
OUT_TILES = 2 * TILES + E - 1
IN_TILES = OUT_TILES - 1 + TILES
HEADS, DH, KV, CTX = 16, 128, 64, 128
PAIRS = HEADS // 2
KVT = BATCH * KV
FPAD = FCH * P
FP8_MAX = 448.0
ROUND_AT = 1.5 * 2.0 ** 20
LEAST_NORMAL = 2.0 ** -6
EXPONENT = 0x7F800000
ARENA_KB = 181
LANE_AT = {}
for _name, _n in LANES:
    LANE_AT[_name] = sum(n for _, n in LANES[:len(LANE_AT)])
LANE_W = sum(n for _, n in LANES)
LOG1P = (0.9999999705406564, -0.4999950151678747, 0.33319271342510387, -0.24844369892549822,
         0.19111431080914837, -0.13674769706244683, 0.07836166802698068, -0.02958850739778893,
         0.0052534577981952985)


def build(nc, inp, out):
    with ExitStack() as ctx:
        def sb(name, shape, dt=F32):
            return ctx.enter_context(nc.sbuf_tensor(name, shape, dt))

        def sem(name):
            return ctx.enter_context(nc.semaphore(name))

        arena = sb("arena", [P, ARENA_KB * 256])

        def view(at_kb, shape, dt=F32, rows=P):
            size = int(np.prod(shape)) * (2 if dt == BF16 else 4)
            assert at_kb * 1024 + size <= ARENA_KB * 1024 and size % 4 == 0
            at = int(at_kb * 256)
            v = arena[0:rows, at:at + size // 4]
            if dt != F32:
                v = v.bitcast(dt)
            dims = ["a", "b", "c"][:len(shape)]
            if len(shape) > 1:
                v = v.rearrange(f"p ({' '.join(dims)}) -> p {' '.join(dims)}", **dict(zip(dims[1:], shape[1:])))
            return v

        x = sb("x", [P, TILES, D])
        cols = sb("cols", [P, 7])
        bc_ln = sb("bc_ln", [2 * NS, 1])
        lane = sb("lane", [P, CI, LANE_W])
        a_neg = sb("a_neg", [P, CI, NS])
        ident = sb("ident", [P, P])
        ones = sb("ones", [P, P])
        before = sb("before", [P, P])
        ln_ff_row = sb("ln_ff_row", [P, D])
        zero = sb("zero", [P, D])
        neg_half = sb("neg_half", [P, P])
        ms = sb("ms", [P, P])
        rs = sb("rs", [P, P])
        xpad = view(0, [CI, BATCH, SEQ + TAPS - 1])
        u, rv = view(0, [2, T]), view(8, [2, T])
        w_in, hT, conv = view(16.5, [KD, 2 * DI]), view(24.5, [KD, T]), view(32.5, [2, T])
        zs, xc, dt, dtx = (view(40.5 + 16 * k, [CI, T]) for k in range(4))
        xdb, junk = view(104.5, [TILES, XP]), view(109.5, [TILES, XP])
        dBx, h = view(104.5, [T]), view(108.5, [T])
        dtnT = view(114.5, [T])
        bcf, bc_rest = view(118.5, [T], rows=2 * NS), view(122.5, [T], rows=2 * NS)
        bc_mid, bc3 = view(126.5, [T], BF16, rows=2 * NS), view(128.5, [T], BF16, rows=96)
        hC, dA = view(130.5, [2, T]), view(138.5, [2, T])
        xn = view(130.5, [TILES, D])
        w_x, w_dt, w_out = view(146.5, [CI, XP]), view(149, [DI]), view(151, [CI, D])
        row_of = view(155, [2 * NS, P], BF16, rows=96)
        w_moe = [view(163, [MOE_W]), view(16.5, [MOE_W])]
        res, hn = view(0, [TILES, D]), view(8, [TILES, D])
        x_rows = [view(40.5, [TILES, D]), view(48.5, [TILES, D])]
        hfT = view(56.5, [KD, T])
        row_in, xT, hid = view(64.5, [D]), view(65.5, [KD, P]), view(66.5, [FCH, P])
        act_g3, y_row = view(69.5, [3, 2 * P]), view(72.5, [D])
        y_got = [view(73.5, [TILES, D]), view(81.5, [TILES, D])]
        w_router = sb("w_router", [P, KD, E])
        logit = sb("logit", [P, TILES, E])
        prob = sb("prob", [P, TILES, E])
        best = sb("best", [P, TILES, 8])
        best_at = sb("best_at", [P, TILES, 8], U32)
        best_f = sb("best_f", [P, TILES, 8])
        picked = [sb(f"picked{k}", [P, TILES, E]) for k in range(2)]
        both = sb("both", [P, TILES, E])
        earlier = sb("earlier", [P, TILES, E])
        iota_e = sb("iota_e", [P, E])
        place = sb("place", [P, TILES, E])
        stat = sb("stat", [P, 4, TILES])
        count = sb("count", [P, 4, E])
        count_i = sb("count_i", [P, E], I32)
        n_tiles = sb("n_tiles", [P, E], I32)
        bounds = sb("bounds", [P, E + 1], I32)
        slot_f = sb("slot_f", [P, 2, TILES])
        slot = sb("slot", [P, 2, TILES], U32)
        bn = sb("bn", [P, TILES, 6])
        mv = sb("mv", [P, TILES, 2])
        ctxT = view(90, [KVT])
        vw = view(91, [PAIRS, BATCH, D])
        w_v, vT, w_o = view(123, [HEADS * DH]), view(131, [HEADS, KVT]), view(147, [HEADS, D])
        w_k, k_raw, k_sq = view(123, [HEADS * DH]), view(131, [2, HEADS * DH]), view(147, [2, HEADS * DH])
        kT = view(147, [HEADS, KVT])
        w_q, x1T = view(0, [KD, HEADS * DH]), view(16.5, [KD, T])
        q_sb, q_sq = view(24.5, [2, 2, HALF]), view(32.5, [2, 2, HALF])
        shift, soft, pT = view(40.5, [2, 8, KV]), view(44.5, [2, 8, KV]), view(48.5, [2, HALF])
        gqk = sb("gqk", [P, 1])
        k_ms = sb("k_ms", [P, 2 * HEADS])
        k_rs = sb("k_rs", [P, 2 * HEADS])
        top = sb("top", [P, 2, 8])
        q_ms = sb("q_ms", [P, 2, 8])
        q_rs = sb("q_rs", [P, 2, 8])
        total_e = sb("total_e", [P, 2, 8])
        up_row, down_row = view(53, [D]), view(54, [FF])
        cmp_row = view(57, [FF])
        up_mask, down_mask = view(60, [D]), view(61, [FPAD])
        diag = view(64, [P])
        w_raw = view(65, [FCH, D])
        wq_a, wq_b = view(71, [FCH, D]), view(77, [FCH, D])
        w_q8 = view(83, [FCH, D], BF16)
        w_fp8T = [view(86, [KD, FPAD], BF16), view(89, [KD, FPAD], BF16)]
        w_dT = view(92, [FCH, D], BF16)
        wd_raw, wd_a, wd_b = view(163, [KD, FF]), view(169, [KD, FF]), view(175, [KD, FF])
        wd_q8 = view(113, [KD, FPAD], BF16)
        scale_rows = [view(116, [FPAD]), view(119, [FPAD])]
        scale_d = view(122, [D])
        xm, xv, xr_ = view(123, [TILES, D]), view(131, [TILES, D]), view(139, [TILES, D])
        qx, qxT = view(147, [TILES, D], BF16), view(151, [KD, T], BF16)
        gs, us, ts_, tv, tr = (view(0 + 3 * k, [FF]) for k in range(5))
        qt, qtT = view(15, [FPAD], BF16), view(17, [FCH, P], BF16)
        y_s = view(19, [D])
        up_col = sb("up_col", [P, KD])
        down_col = sb("down_col", [P, FCH])
        iota_p = sb("iota_p", [P, FCH])
        gather_at = sb("gather_at", [P, FCH], I32)
        rmax = sb("rmax", [P, FCH])
        rinv = sb("rinv", [P, FCH])
        rscale = sb("rscale", [P, FCH])
        xmax = sb("xmax", [P, TILES])
        xinv = sb("xinv", [P, TILES])
        xscale = sb("xscale", [P, TILES])
        tmax = sb("tmax", [P, 1])
        tinv = sb("tinv", [P, 1])
        tscale = sb("tscale", [P, TILES])
        ident16 = sb("ident16", [P, P], BF16)
        moe_in = nc.dram_tensor("moe_in", (IN_TILES * P, D), F32).ap()
        moe_out = nc.dram_tensor("moe_out", (OUT_TILES * P, D), F32).ap()
        ps = ctx.enter_context(nc.psum_tensor("ps", [P, 8, HALF], F32))

        names = """ld_x ld_small ld_win ld_wx ld_wd ld_wo consts pads selectors
            sumsq1 ms1 rstd1 xn hs_psum hsT in_psum in_out conv_acc conv_out xproj_psum xdb_sb
            ms2 rstd2 xdbn dtn_psum bc_psum dtn_sb bc_sb dt_psum dt_act softplus a_exp a_ready bc_split
            b_ready c_ready da_ready dbx_done scan_done hc_done y_summed y_drained ym_done
            out_psum dve_chain st_out
            ld_lnff iota tables zero_set moe_zeroed res_done sumsq3 ms3 rstd3 hn_done hn_psum hfT_done logit_psum
            logit_sub logit_exp picked_done prefix_psum slots_done scattered ld_rows0 ld_rows1 ld_w0 ld_w1
            row_ready xT_psum xT_done gu_psum gate_act hid_done y_psum y_ready y_stored gathered x1_sum pool_waited
            bn3 rstd_x1 x1_done
            ld_v ld_o ld_k ld_q kv_psum kv_out k_squared k_ms k_rstd k_normed v_ready vw_ready
            x1T_psum x1T_done q_psum q_copied q_squared s_psum s_ms q_rstd s_shifted s_exp s_soft pT_psum pT_done attn_psum attn_taken
            sum2 bn4 rstd_x2 x2_done
            ld_idx ld_down gathered_w iota_done counted mask_psum mask_done quant_done wT_psum wT_done sc_psum sc_done
            x_quant xT8_psum xT8_done ff_psum ff_read ff_gate ff_in t_done t_psum tT_done y2_psum y2_read
            attn_chain ff_chain bn5 rstd_out out_done stored""".split()
        s = {n: sem(n) for n in names}

        block = ctx.enter_context(nc.Block())
        DA_BUFS, HC_BUFS, HID_BUFS = 2, 2, 3

        @block.sync
        def _(sp):
            def load(dst, src, signal):
                sp.dma_start(dst, src).then_inc(s[signal], 16)
            load(x[:, :, :], inp["x"].rearrange("b s d -> (b s) d").rearrange("(i p) d -> p i d", p=P), "ld_x")
            load(w_in[:, :, :], inp["w_in"], "ld_win")
            load(cols[:, :], inp["cols"], "ld_small")
            load(bc_ln[:, :], inp["bc_ln"], "ld_small")
            load(lane[:, :, :], inp["lane"], "ld_small")
            load(w_x[:, :, :], inp["w_x"], "ld_wx")
            load(w_dt[:, :], inp["w_dt"], "ld_wd")
            load(w_out[:, :, :], inp["w_out"], "ld_wo")
            load(w_router[:, :, :], inp["w_router"], "ld_small")
            load(ln_ff_row[:, :], inp["ln_ff"].partition_broadcast(P), "ld_lnff")
            sp.wait_ge(s["zero_set"], 1)
            load(moe_in.rearrange("(i p) d -> p i d", p=P), zero[:, :].unsqueeze(1).to_broadcast([P, IN_TILES, D]), "moe_zeroed")
            load(moe_out.rearrange("(i p) d -> p i d", p=P), zero[:, :].unsqueeze(1).to_broadcast([P, OUT_TILES, D]), "moe_zeroed")

            def load_weights(e):
                sp.dma_start(w_moe[e % 2], inp["w_moe"][e]).then_inc(s[f"ld_w{e % 2}"], 16)

            def load_rows(e):
                first = sp.value_load(bounds[0:1, e:e + 1], min_val=0, max_val=OUT_TILES - 1)
                sp.dma_start(x_rows[e % 2], moe_in[bass.ds(first * P, TILES * P), :].rearrange("(i p) d -> p i d", p=P))\
                    .then_inc(s[f"ld_rows{e % 2}"], 16)

            load_weights(0)
            sp.wait_ge(s["conv_out"], CI)
            load_weights(1)
            sp.wait_ge(s["scattered"], 2 * TILES * 16)
            load_rows(0)
            load_rows(1)
            load(w_q, inp["w_q"], "ld_q")
            for e in range(E):
                if 1 <= e < E - 1:
                    sp.wait_ge(s["y_stored"], sp.value_load(bounds[0:1, e:e + 1], min_val=1, max_val=OUT_TILES) * 16 + 16)
                    load_weights(e + 1)
                    load_rows(e + 1)
                first = sp.value_load(bounds[0:1, e:e + 1], min_val=0, max_val=OUT_TILES - 1)
                last = sp.value_load(bounds[0:1, e + 1:e + 2], min_val=1, max_val=OUT_TILES)
                with sp.Fori(first, last) as j:
                    sp.wait_ge(s["y_ready"], j + 2)
                    sp.dma_start(moe_out[bass.ds(j * P, P), :], y_row).then_inc(s["y_stored"], 16)
            sp.wait_ge(s["x1_done"], TILES)
            load(up_row.bitcast(I32), inp["up_index"].partition_broadcast(P), "ld_idx")
            load(down_row.bitcast(I32), inp["down_index"].partition_broadcast(P), "ld_idx")
            load(gather_at[:, :], inp["down_at"], "ld_idx")
            load(wd_raw, inp["w_down"], "ld_down")
            o = out.rearrange("b s d -> (b s) d").rearrange("(i p) d -> p i d", p=P)
            for half in range(2):
                tiles = slice(half * TILES // 2, (half + 1) * TILES // 2)
                sp.wait_ge(s["out_done"], (half + 1) * TILES // 2)
                sp.dma_start(o[:, tiles, :], x[:, tiles, :]).then_inc(s["stored"], 16)
            sp.wait_ge(s["stored"], 32)

        @block.gpsimd
        def _(pool):
            pool.memset(ident[:, :], 0.0).then_inc(s["pads"], 1)
            pool.wait_ge(s["pads"], 1)
            pool.affine_select(out=ident[:, :], in_=ident[:, :], compare_op=ALU.not_equal, fill=1.0, base=0,
                               pattern=[[-1, P]], channel_multiplier=1).then_inc(s["consts"], 1)
            pool.memset(zero[:, :], 0.0).then_inc(s["zero_set"], 1)
            pool.memset(ones[:, :], 1.0).then_inc(s["tables"], 1)
            pool.wait_ge(s["tables"], 1)
            pool.affine_select(out=before[:, :], in_=ones[:, :], compare_op=ALU.is_gt, fill=0.0, base=0,
                               pattern=[[1, P]], channel_multiplier=-1).then_inc(s["tables"], 1)
            pool.iota(iota_e[:, :], pattern=[[1, E]], base=0, channel_multiplier=0,
                      allow_small_or_imprecise_dtypes=True).then_inc(s["tables"], 1)
            pool.wait_ge(s["consts"], 1)
            pool.tensor_copy(ident16[:, :], ident[:, :]).then_inc(s["tables"], 1)
            pool.memset(neg_half[:, :], -0.5).then_inc(s["consts"], 1)
            pool.memset(xpad[:, :, :, 0:TAPS - 1], 0.0).then_inc(s["consts"], 1)
            pool.memset(dA[:, :, :].rearrange("p k (b t) -> p k b t", b=BATCH)[:, :, :, 0:1], 0.0).then_inc(s["consts"], 1)
            pool.memset(row_of[:, :, :], 0.0).then_inc(s["selectors"], 1)
            for k in range(3):
                pool.wait_ge(s["selectors"], k + 1)
                pool.affine_select(out=row_of[:, :, :], in_=row_of[:, :, :], compare_op=ALU.not_equal, fill=1.0,
                                   base=-2 * NS * k, pattern=[[-1, 2 * NS], [0, P]], channel_multiplier=1)\
                    .then_inc(s["selectors"], 1)
            pool.wait_ge(s["consts"], 2)
            pool.wait_ge(s["ms1"], 1)
            pool.tensor_tensor(rs[:, 0:TILES], ms[:, 0:TILES], neg_half[:, 0:TILES], ALU.pow).then_inc(s["rstd1"], 1)
            pool.wait_ge(s["ms2"], 3)
            pool.tensor_tensor(rs[:, TILES:4 * TILES], ms[:, TILES:4 * TILES], neg_half[:, 0:3 * TILES], ALU.pow).then_inc(s["rstd2"], 1)

            pool.wait_ge(s["ms3"], 1)
            pool.tensor_tensor(rs[:, 0:TILES], ms[:, 0:TILES], neg_half[:, 0:TILES], ALU.pow).then_inc(s["rstd3"], 1)
            pool.wait_ge(s["slots_done"], 1)
            pool.wait_ge(s["moe_zeroed"], 32)
            pool.wait_ge(s["hn_done"], TILES)
            for k in range(2):
                for i in range(TILES):
                    pool.indirect_dma_start(moe_in[0:OUT_TILES * P, :], bass.IndirectOffsetOnAxis(slot[:, k, i:i + 1], 0), hn[:, i, :], None)\
                        .then_inc(s["scattered"], 16)
            pool.wait_ge(s["k_ms"], 1)
            pool.tensor_tensor(k_rs[:, :], k_ms[:, :], neg_half[:, 0:2 * HEADS], ALU.pow).then_inc(s["k_rstd"], 1)
            for e in range(E):
                first = pool.value_load(bounds[0:1, e:e + 1], min_val=0, max_val=OUT_TILES - 1)
                tiles = pool.value_load(n_tiles[0:1, e:e + 1], min_val=1, max_val=TILES)
                pool.wait_ge(s[f"ld_rows{e % 2}"], 16 * (e // 2 + 1))
                with pool.Fori(0, tiles) as j:
                    pool.wait_ge(s["xT_psum"], first + j + 1)
                    pool.sem_inc(s["pool_waited"], 1)
                    pool.tensor_copy(row_in, x_rows[e % 2][:, j, :]).then_inc(s["row_ready"], 1)
            total = pool.value_load(bounds[0:1, E:E + 1], min_val=E, max_val=OUT_TILES)
            pool.wait_ge(s["xT_psum"], total + 1)
            pool.sem_inc(s["pool_waited"], 1)
            pool.tensor_copy(row_in, x_rows[(E - 1) % 2][:, 0, :]).then_inc(s["row_ready"], 1)
            pool.wait_ge(s["y_stored"], total * 16 + 16)
            pool.sem_inc(s["pool_waited"], 1)
            for k in range(2):
                for i in range(TILES):
                    pool.indirect_dma_start(y_got[k][:, i, :], None, moe_out[:, :], bass.IndirectOffsetOnAxis(slot[:, k, i:i + 1], 0))\
                        .then_inc(s["gathered"], 16)
            pool.wait_ge(s["bn3"], TILES + 1)
            pool.tensor_tensor(rs[:, 0:TILES], ms[:, 0:TILES], neg_half[:, 0:TILES], ALU.pow).then_inc(s["rstd_x1"], 1)

            with pool.Fori(0, 2) as half:
                for n in range(PAIRS):
                    pool.wait_ge(s["s_ms"], half * PAIRS + n + 2)
                    pool.sem_inc(s["pool_waited"], 1)
                    pool.tensor_tensor(q_rs[:, n % 2, :], q_ms[:, n % 2, :], neg_half[:, 0:8], ALU.pow).then_inc(s["q_rstd"], 1)
            pool.wait_ge(s["bn4"], TILES + 1)
            pool.tensor_tensor(rs[:, 0:TILES], ms[:, 0:TILES], neg_half[:, 0:TILES], ALU.pow).then_inc(s["rstd_x2"], 1)
            pool.wait_ge(s["x2_done"], TILES)
            pool.iota(iota_p[:, :], pattern=[[P, FCH]], base=0, channel_multiplier=1, allow_small_or_imprecise_dtypes=True).then_inc(s["iota_done"], 1)
            pool.memset(wd_q8[:, :, FF:], 0.0).then_inc(s["iota_done"], 1)
            pool.memset(qt[:, FF:], 0.0).then_inc(s["iota_done"], 1)
            pool.wait_ge(s["ld_idx"], 48)
            for m, name in enumerate(("w_gate", "w_up")):
                if m:
                    pool.wait_ge(s["quant_done"], 1)
                for c in range(FCH):
                    pool.indirect_dma_start(w_raw[:, c, :], None, inp[name], bass.IndirectOffsetOnAxis(gather_at[:, c:c + 1].bitcast(U32), 0))\
                        .then_inc(s["gathered_w"], 16)
            pool.wait_ge(s["bn5"], TILES + 1)
            pool.tensor_tensor(rs[:, 0:TILES], ms[:, 0:TILES], neg_half[:, 0:TILES], ALU.pow).then_inc(s["rstd_out"], 1)

        @block.scalar
        def _(act):
            act.wait_ge(s["ld_x"], 16)
            for i in range(TILES):
                nc.scalar.activation(xn[:, i, :], x[:, i, :], ACT.Square,
                                     accum_out=ms[:, i:i + 1]).then_inc(s["sumsq1"], 1)
            act.wait_ge(s["ld_small"], 64)
            nc.scalar.activation(a_neg[:, :, :], lane[:, :, LANE_AT["a_log"]:LANE_AT["a_log"] + NS], ACT.Exp).then_inc(s["a_exp"], 1)
            act.wait_ge(s["hs_psum"], 2)
            nc.scalar.activation(hT[:, 1, :], ps[:, 2:4, :].rearrange("p a b -> p (a b)"), ACT.Identity,
                                 scale=cols[:, 1:2]).then_inc(s["hsT"], 1)
            act.wait_ge(s["consts"], 4)
            for n in range(4 * CI):
                c, half = divmod(n, 2)
                act.wait_ge(s["in_psum"], n + 1)
                src = ps[:, 4 + n % 4, :]
                if c < CI:
                    nc.scalar.activation(xpad[:, c, 2 * half:2 * half + 2, TAPS - 1:], src.rearrange("p (b t) -> p b t", b=2),
                                         ACT.Identity).then_inc(s["in_out"], 1)
                else:
                    nc.scalar.activation(zs[:, c - CI, half * HALF:(half + 1) * HALF], src, ACT.Silu).then_inc(s["in_out"], 1)
            for c in range(CI):
                act.wait_ge(s["conv_acc"], c + 1)
                nc.scalar.activation(xc[:, c, :], conv[:, c % 2, :], ACT.Silu,
                                     bias=lane[:, c, LANE_AT["conv_b"]:LANE_AT["conv_b"] + 1]).then_inc(s["conv_out"], 1)
            act.wait_ge(s["xproj_psum"], TILES)
            nc.scalar.activation(xdb[:, :, :].rearrange("p (a b) c -> p a b c", b=2),
                                 ps[:, 0:4, :].rearrange("p a (b c) -> p a b c", b=2)[:, :, :, 0:XP], ACT.Identity).then_inc(s["xdb_sb"], 1)
            for c in range(CI):
                act.wait_ge(s["dt_psum"], 2 * c + 2)
                if c >= 2:
                    act.wait_ge(s["softplus"], c - 1)
                v = ps[:, 4 + 2 * (c % 2):6 + 2 * (c % 2), :].rearrange("p a b -> p (a b)")
                bias = lane[:, c, LANE_AT["dt_b"]:LANE_AT["dt_b"] + 1]
                nc.scalar.activation(rv[:, c % 2, :], v, ACT.Relu, bias=bias).then_inc(s["dt_act"], 1)
                nc.scalar.activation(u[:, c % 2, :], v, ACT.Abs, bias=bias).then_inc(s["dt_act"], 1)
                act.wait_ge(s["dt_act"], 3 * c + 2)
                nc.scalar.activation(u[:, c % 2, :], u[:, c % 2, :], ACT.Exp, scale=-1.0).then_inc(s["dt_act"], 1)
            act.wait_ge(s["a_ready"], 1)
            act.wait_ge(s["softplus"], CI)
            dt_b = dt[:, :, :].rearrange("p c (b t) -> p c b t", b=BATCH)
            dA_b = dA[:, :, :].rearrange("p k (b t) -> p k b t", b=BATCH)
            with act.Fori(0, CI) as c:
                for n in range(NS):
                    unit = c * NS + n
                    act.wait_ge(s["scan_done"], unit + 1)
                    nc.scalar.activation(dA_b[:, n % 2, :, 1:], dt_b[:, c, :, 1:], ACT.Exp,
                                         scale=a_neg[:, c, n:n + 1]).then_inc(s["da_ready"], 1)

            act.wait_ge(s["out_psum"], TILES)
            act.dma_start(ctxT, inp["ctxT"]).then_inc(s["ld_v"], 16)
            act.dma_start(w_v, inp["w_v"]).then_inc(s["ld_v"], 16)
            act.dma_start(w_o, inp["w_o"]).then_inc(s["ld_o"], 16)
            act.wait_ge(s["res_done"], 4)
            for i in range(TILES):
                nc.scalar.activation(hn[:, i, :], res[:, i, :], ACT.Square, accum_out=ms[:, i:i + 1]).then_inc(s["sumsq3"], 1)
            act.wait_ge(s["hn_psum"], KD)
            nc.scalar.activation(hfT[:, 1, :], ps[:, 6:8, :].rearrange("p a b -> p (a b)"), ACT.Identity).then_inc(s["hfT_done"], 1)
            act.wait_ge(s["logit_sub"], 1)
            nc.scalar.activation(prob[:, :, :], logit[:, :, :], ACT.Exp).then_inc(s["logit_exp"], 1)
            step = 0
            for n in range(PAIRS):
                act.wait_ge(s["kv_psum"], step + 1)
                nc.scalar.activation(vT[:, 2 * n:2 * n + 2, :], ps[:, 2 + step % 6, :].rearrange("p (a b) -> p a b", a=2), ACT.Identity).then_inc(s["kv_out"], 1)
                step += 1
            for n in range(2 * PAIRS):
                act.wait_ge(s["kv_psum"], step + 1)
                nc.scalar.activation(vw[:, n // 2, 2 * (n % 2):2 * (n % 2) + 2, :], ps[:, 2 + step % 6, :].rearrange("p (a b) -> p a b", a=2),
                                     ACT.Identity).then_inc(s["kv_out"], 1)
                step += 1
                if n == 0:
                    act.dma_start(w_k, inp["w_k"]).then_inc(s["ld_k"], 16)
            for n in range(8):
                act.wait_ge(s["kv_psum"], step + 1)
                src = ps[:, 2 + step % 6, :]
                at = slice((n % 4) * HALF, (n % 4 + 1) * HALF)
                nc.scalar.activation(k_raw[:, n // 4, at], src, ACT.Identity).then_inc(s["k_squared"], 1)
                nc.scalar.activation(k_sq[:, n // 4, at], src, ACT.Square).then_inc(s["kv_out"], 1)
                step += 1
            for n in range(PAIRS):
                act.wait_ge(s["kv_psum"], step + 1)
                nc.scalar.activation(kT[:, 2 * n:2 * n + 2, :], ps[:, 2 + step % 6, :].rearrange("p (a b) -> p a b", a=2), ACT.Identity,
                                     scale=gqk[:, 0:1]).then_inc(s["kv_out"], 1)
                step += 1
            act.wait_ge(s["slots_done"], 1)
            total = act.value_load(bounds[0:1, E:E + 1], min_val=E, max_val=OUT_TILES)
            with act.Fori(0, total) as j:
                for q in range(FCH // 2):
                    act.wait_ge(s["gu_psum"], j * (FCH // 2) + q + 1)
                    act.wait_ge(s["hid_done"], j * (FCH // 2) + q + 1)
                    nc.scalar.activation(act_g3[:, q, :], ps[:, 2 * q, 0:2 * P], ACT.Silu).then_inc(s["gate_act"], 1)

            act.wait_ge(s["x1T_psum"], 2)
            nc.scalar.activation(x1T[:, 1, :], ps[:, 2:4, :].rearrange("p a b -> p (a b)"), ACT.Identity).then_inc(s["x1T_done"], 1)
            with act.Fori(0, 2) as half:
                base = half * PAIRS
                for m in range(PAIRS + 2):
                    if m < PAIRS:
                        for hd in range(2):
                            act.wait_ge(s["q_copied"], 2 * (base + m) + hd + 3)
                            if hd == 0:
                                act.wait_ge(s["s_psum"], base + m + 1)
                            nc.scalar.activation(q_sq[:, m % 2, hd, :], q_sb[:, m % 2, hd, :], ACT.Square).then_inc(s["q_squared"], 1)
                    if m >= 1 and m - 1 < PAIRS:
                        n = m - 1
                        act.wait_ge(s["s_shifted"], base + n + 3)
                        nc.scalar.activation(shift[:, n % 2, :, :], shift[:, n % 2, :, :], ACT.Exp).then_inc(s["s_exp"], 1)
                    if m >= 2:
                        n = m - 2
                        act.wait_ge(s["pT_psum"], base + n + 3)
                        act.wait_ge(s["attn_psum"], base + n + 1)
                        nc.scalar.activation(pT[:, n % 2, :], ps[:, 4, :], ACT.Identity).then_inc(s["pT_done"], 1)
            act.wait_ge(s["xT8_psum"], 2)
            nc.scalar.activation(qxT[:, 1, :], ps[:, 2, :].bitcast(BF16), ACT.Identity).then_inc(s["xT8_done"], 1)
            with act.Fori(0, TILES) as i:
                act.wait_ge(s["ff_in"], i + 1)
                nc.scalar.activation(gs, gs, ACT.Silu, scale=xscale[:, bass.ds(i, 1)]).then_inc(s["ff_gate"], 1)
                act.wait_ge(s["t_psum"], i + 1)
                nc.scalar.activation(qtT, ps[:, 4, 0:FPAD // 2].bitcast(BF16).rearrange("p (a b) -> p a b", b=P), ACT.Identity).then_inc(s["tT_done"], 1)

        @block.vector
        def _(dve):
            chain = [0]

            def link(ins):
                chain[0] += 1
                ins.then_inc(s["dve_chain"], 1)
                dve.wait_ge(s["dve_chain"], chain[0])

            loops = {"count": 0, "base": 0}

            def link_loop(ins, turn):
                loops["count"] += 1
                ins.then_inc(s[loops["sem"]], 1)
                dve.wait_ge(s[loops["sem"]], turn * loops["per_turn"] + loops["count"])

            dve.sem_inc(s["scan_done"], DA_BUFS)
            dve.sem_inc(s["y_summed"], HC_BUFS)
            for name in ("dbx_done", "hc_done", "y_drained"):
                dve.sem_inc(s[name], 1)
            dve.wait_ge(s["sumsq1"], TILES)
            nc.vector.tensor_scalar(ms[:, 0:TILES], ms[:, 0:TILES], 1.0 / D, 1e-6, ALU.mult, ALU.add).then_inc(s["ms1"], 1)
            dve.wait_ge(s["rstd1"], 1)
            for i in range(TILES):
                nc.vector.tensor_scalar(xn[:, i, :], x[:, i, :], rs[:, i:i + 1], None, ALU.mult).then_inc(s["xn"], 1)
            dve.wait_ge(s["a_exp"], 1)
            nc.vector.tensor_scalar(a_neg[:, :, :], a_neg[:, :, :], -1.0, None, ALU.mult).then_inc(s["a_ready"], 1)
            dve.wait_ge(s["hs_psum"], 1)
            dve.wait_ge(s["ld_small"], 64)
            nc.vector.tensor_scalar(hT[:, 0, :], ps[:, 0:2, :].rearrange("p a b -> p (a b)"), cols[:, 0:1], None, ALU.mult).then_inc(s["hsT"], 1)
            for c in range(CI):
                dve.wait_ge(s["in_out"], 2 * c + 2)
                if c >= 2:
                    dve.wait_ge(s["conv_out"], c - 1)
                acc = conv[:, c % 2, :].rearrange("p (b t) -> p b t", b=BATCH)
                tap = lambda k: lane[:, c, LANE_AT["conv_w"] + k:LANE_AT["conv_w"] + k + 1]
                link(nc.vector.tensor_scalar(acc, xpad[:, c, :, 0:SEQ], tap(0), None, ALU.mult))
                for k in range(1, TAPS):
                    ins = nc.vector.scalar_tensor_tensor(acc, xpad[:, c, :, k:k + SEQ], tap(k), acc, ALU.mult, ALU.add)
                    if k < TAPS - 1:
                        link(ins)
                    else:
                        ins.then_inc(s["conv_acc"], 1)
            dve.wait_ge(s["xdb_sb"], 1)
            sq = junk
            link(nc.vector.tensor_tensor(sq, xdb[:, :, :], xdb[:, :, :], ALU.mult))
            groups = ((0, DR), (DR, NS), (DR + NS, NS))
            for g, (at, width) in enumerate(groups):
                dst = ms[:, (g + 1) * TILES:(g + 2) * TILES]
                link(nc.vector.tensor_reduce(dst, sq[:, :, at:at + width], axis=AX.X, op=ALU.add))
                nc.vector.tensor_scalar(dst, dst, 1.0 / width, 1e-6, ALU.mult, ALU.add).then_inc(s["ms2"], 1)
            dve.wait_ge(s["rstd2"], 1)
            for g, (at, width) in enumerate(groups):
                part = xdb[:, :, at:at + width]
                rstd = rs[:, (g + 1) * TILES:(g + 2) * TILES].unsqueeze(2).to_broadcast([P, TILES, width])
                nc.vector.tensor_tensor(part, part, rstd, ALU.mult).then_inc(s["xdbn"], 1)
            dve.wait_ge(s["dtn_psum"], 1)
            nc.vector.tensor_scalar(dtnT, ps[:, 0:2, :].rearrange("p a b -> p (a b)"), cols[:, 2:3], None, ALU.mult).then_inc(s["dtn_sb"], 1)
            dve.wait_ge(s["bc_psum"], 1)
            R = 2 * NS
            link(nc.vector.tensor_scalar(bcf, ps[0:R, 2:4, :].rearrange("p a b -> p (a b)"), bc_ln[:, 0:1], None, ALU.mult))
            link(nc.vector.tensor_copy(bc3[0:R, :], bcf))
            link(nc.vector.tensor_tensor(bc_rest, bcf, bc3[0:R, :], ALU.subtract))
            link(nc.vector.tensor_copy(bc_mid, bc_rest))
            nc.vector.tensor_copy(bc3[R:2 * R, :], bc_mid).then_inc(s["bc_split"], 1)
            nc.vector.tensor_tensor(bc3[2 * R:3 * R, :], bc_rest, bc_mid, ALU.subtract).then_inc(s["bc_split"], 1)
            for c in range(CI):
                dve.wait_ge(s["dt_act"], 3 * c + 3)
                acc = dt[:, c, :]
                uu = u[:, c % 2, :]
                link(nc.vector.tensor_scalar(acc, uu, LOG1P[-1], None, ALU.mult))
                for k in range(len(LOG1P) - 2, -1, -1):
                    link(nc.vector.scalar_tensor_tensor(acc, acc, LOG1P[k], uu, ALU.add, ALU.mult))
                nc.vector.tensor_tensor(acc, acc, rv[:, c % 2, :], ALU.add).then_inc(s["softplus"], 1)
                dve.wait_ge(s["softplus"], c + 1)
                dve.wait_ge(s["conv_out"], c + 1)
                link(nc.vector.tensor_tensor(dtx[:, c, :], acc, xc[:, c, :], ALU.mult))
            pB = ps[:, 0:2, :].rearrange("p a b -> p (a b)")
            pC = ps[:, 2:4, :].rearrange("p a b -> p (a b)")
            pY = ps[:, 4:6, :].rearrange("p a b -> p (a b)")
            with dve.Fori(0, CI) as c:
                for n in range(NS):
                    unit = c * NS + n
                    dve.wait_ge(s["b_ready"], unit + 1)
                    dve.wait_ge(s["scan_done"], unit + DA_BUFS)
                    nc.vector.tensor_tensor(dBx, dtx[:, c, :], pB, ALU.mult).then_inc(s["dbx_done"], 1)
                    dve.wait_ge(s["da_ready"], unit + 1)
                    dve.wait_ge(s["dbx_done"], unit + 2)
                    dve.wait_ge(s["hc_done"], unit + 1)
                    nc.vector.tensor_tensor_scan(h, dA[:, n % 2, :], dBx, 0.0, ALU.mult, ALU.add).then_inc(s["scan_done"], 1)
                    dve.wait_ge(s["c_ready"], unit + 1)
                    dve.wait_ge(s["scan_done"], unit + DA_BUFS + 1)
                    dve.wait_ge(s["y_summed"], unit + 1)
                    nc.vector.tensor_tensor(hC[:, n % 2, :], h, pC, ALU.mult).then_inc(s["hc_done"], 1)
                dve.wait_ge(s["y_summed"], (c + 1) * NS + HC_BUFS)
                dve.wait_ge(s["scan_done"], (c + 1) * NS + DA_BUFS)
                nc.vector.scalar_tensor_tensor(dtx[:, c, :], xc[:, c, :], lane[:, c, LANE_AT["d_param"]:LANE_AT["d_param"] + 1],
                                               pY, ALU.mult, ALU.add).then_inc(s["y_drained"], 1)
                dve.wait_ge(s["y_drained"], c + 2)
                nc.vector.tensor_tensor(dtx[:, c, :], dtx[:, c, :], zs[:, c, :], ALU.mult).then_inc(s["ym_done"], 1)
            for q in range(4):
                dve.wait_ge(s["out_psum"], 2 * q + 2)
                nc.vector.tensor_tensor(res[:, 2 * q:2 * q + 2, :], x[:, 2 * q:2 * q + 2, :],
                                        ps[:, q, :].rearrange("p (a b) -> p a b", b=D), ALU.add).then_inc(s["res_done"], 1)
            dve.wait_ge(s["sumsq3"], TILES)
            nc.vector.tensor_scalar(ms[:, 0:TILES], ms[:, 0:TILES], 1.0 / D, 1e-6, ALU.mult, ALU.add).then_inc(s["ms3"], 1)
            dve.wait_ge(s["rstd3"], 1)
            dve.wait_ge(s["ld_lnff"], 16)
            for i in range(TILES):
                nc.vector.scalar_tensor_tensor(hn[:, i, :], res[:, i, :], rs[:, i:i + 1], ln_ff_row[:, :], ALU.mult, ALU.mult).then_inc(s["hn_done"], 1)
            dve.wait_ge(s["hn_psum"], 1)
            nc.vector.tensor_copy(hfT[:, 0, :], ps[:, 4:6, :].rearrange("p a b -> p (a b)")).then_inc(s["hfT_done"], 1)
            stat_of = lambda k, n=E: stat[:, k, :].unsqueeze(2).to_broadcast([P, TILES, n])
            dve.wait_ge(s["logit_psum"], 1)
            link(nc.vector.tensor_copy(logit[:, :, :], ps[:, 0, 0:TILES * E].rearrange("p (i e) -> p i e", e=E)))
            link(nc.vector.tensor_reduce(stat[:, 0, :], logit[:, :, :], axis=AX.X, op=ALU.max))
            nc.vector.tensor_tensor(logit[:, :, :], logit[:, :, :], stat_of(0), ALU.subtract).then_inc(s["logit_sub"], 1)
            dve.wait_ge(s["logit_exp"], 1)
            link(nc.vector.tensor_reduce(stat[:, 1, :], prob[:, :, :], axis=AX.X, op=ALU.add))
            link(nc.vector.reciprocal(stat[:, 2, :], stat[:, 1, :]))
            link(nc.vector.tensor_tensor(prob[:, :, :], prob[:, :, :], stat_of(2), ALU.mult))
            for i in range(TILES):
                ins = nc.vector.max(best[:, i, :], prob[:, i, :])
            link(ins)
            for i in range(TILES):
                ins = nc.vector.max_index(best_at[:, i, :], best[:, i, :], prob[:, i, :])
            link(ins)
            link(nc.vector.tensor_copy(best_f[:, :, :], best_at[:, :, :]))
            dve.wait_ge(s["tables"], 3)
            for k in range(2):
                nc.vector.tensor_tensor(picked[k][:, :, :], iota_e[:, :].unsqueeze(1).to_broadcast([P, TILES, E]),
                                        best_f[:, :, k:k + 1].to_broadcast([P, TILES, E]), ALU.is_equal).then_inc(s["picked_done"], 1)
            dve.wait_ge(s["picked_done"], 2)
            link(nc.vector.tensor_tensor(both[:, :, :], picked[0][:, :, :], picked[1][:, :, :], ALU.add))
            link(nc.vector.memset(earlier[:, 0, :], 0.0))
            for i in range(1, TILES):
                ins = nc.vector.tensor_tensor(earlier[:, i, :], earlier[:, i - 1, :], both[:, i - 1, :], ALU.add)
                if i < TILES - 1:
                    link(ins)
            ins.then_inc(s["picked_done"], 1)
            dve.wait_ge(s["prefix_psum"], 1)
            link(nc.vector.tensor_scalar(count_i[:, :], ps[:, 1, 0:E], float(P - 1), None, ALU.add))
            link(nc.vector.tensor_scalar(count_i[:, :], count_i[:, :], 7, None, ALU.logical_shift_right))
            link(nc.vector.tensor_scalar(count[:, 0, :], count_i[:, :], 1.0, None, ALU.max))
            link(nc.vector.tensor_tensor_scan(count[:, 1, :], ones[:, 0:E], count[:, 0, :], 0.0, ALU.mult, ALU.add))
            link(nc.vector.tensor_copy(n_tiles[:, :], count[:, 0, :]))
            link(nc.vector.memset(bounds[:, 0:1], 0))
            link(nc.vector.tensor_copy(bounds[:, 1:E + 1], count[:, 1, :]))
            link(nc.vector.tensor_tensor(count[:, 2, :], count[:, 1, :], count[:, 0, :], ALU.subtract))
            link(nc.vector.tensor_scalar(count[:, 3, :], count[:, 2, :], float(P), None, ALU.mult))
            link(nc.vector.tensor_tensor(place[:, :, :], ps[:, 1, E:E + TILES * E].rearrange("p (i e) -> p i e", e=E),
                                         count[:, 3, :].unsqueeze(1).to_broadcast([P, TILES, E]), ALU.add))
            for k in range(2):
                link(nc.vector.tensor_tensor(picked[k][:, :, :], picked[k][:, :, :], place[:, :, :], ALU.mult))
                link(nc.vector.tensor_reduce(slot_f[:, k, :], picked[k][:, :, :], axis=AX.X, op=ALU.add))
            nc.vector.tensor_copy(slot[:, :, :], slot_f[:, :, :]).then_inc(s["slots_done"], 1)
            link(nc.vector.tensor_tensor(gqk[:, :], cols[:, 5:6], cols[:, 6:7], ALU.mult))
            link(nc.vector.tensor_scalar(gqk[:, :], gqk[:, :], float(DH) ** -0.5, None, ALU.mult))
            dve.wait_ge(s["kv_out"], 3 * PAIRS + 8)
            link(nc.vector.tensor_reduce(k_ms[:, :], k_sq.rearrange("p j (h d) -> p (j h) d", d=DH), axis=AX.X, op=ALU.add))
            nc.vector.tensor_scalar(k_ms[:, :], k_ms[:, :], 1.0 / DH, 1e-5, ALU.mult, ALU.add).then_inc(s["k_ms"], 1)
            dve.wait_ge(s["k_rstd"], 1)
            k_heads = k_raw.rearrange("p j (h d) -> p (j h) d", d=DH)
            nc.vector.tensor_tensor(k_heads, k_heads, k_rs[:, :].unsqueeze(2).to_broadcast([P, 2 * HEADS, DH]), ALU.mult).then_inc(s["k_normed"], 1)
            dve.wait_ge(s["slots_done"], 1)
            dve.sem_inc(s["hid_done"], HID_BUFS)
            dve.sem_inc(s["xT_psum"], 1)
            dve.sem_inc(s["y_psum"], 1)
            dve.sem_inc(s["y_ready"], 1)
            dve.sem_inc(s["y_stored"], 16)
            dve.sem_inc(s["xT_done"], 1)
            total = dve.value_load(bounds[0:1, E:E + 1], min_val=E, max_val=OUT_TILES)

            def take_transposed(tile):
                dve.wait_ge(s["xT_psum"], tile + 2)
                nc.vector.tensor_copy(xT, ps[:, 7, 0:D].rearrange("p (k n) -> p k n", k=KD)).then_inc(s["xT_done"], 1)

            take_transposed(0)
            with dve.Fori(0, total) as j:
                for q in range(FCH // 2):
                    dve.wait_ge(s["gate_act"], j * (FCH // 2) + q + 1)
                    dve.wait_ge(s["y_psum"], j + 1)
                    nc.vector.tensor_tensor(hid[:, 2 * q:2 * q + 2, :], act_g3[:, q, :].rearrange("p (a b) -> p a b", b=P),
                                            ps[:, 2 * q + 1, 0:2 * P].rearrange("p (a b) -> p a b", b=P), ALU.mult).then_inc(s["hid_done"], 1)
                take_transposed(j + 1)
                dve.wait_ge(s["y_psum"], j + 2)
                dve.wait_ge(s["y_stored"], j * 16 + 16)
                nc.vector.tensor_copy(y_row, ps[:, 6, 0:D]).then_inc(s["y_ready"], 1)
            for i in range(TILES):
                dve.wait_ge(s["gathered"], 2 * TILES * 16)
                nc.vector.scalar_tensor_tensor(x[:, i, :], y_got[0][:, i, :], best[:, i, 0:1], x[:, i, :], ALU.mult, ALU.add).then_inc(s["x1_sum"], 1)
            for i in range(TILES):
                dve.wait_ge(s["x1_sum"], i + 1)
                nc.vector.scalar_tensor_tensor(x[:, i, :], y_got[1][:, i, :], best[:, i, 1:2], x[:, i, :], ALU.mult, ALU.add).then_inc(s["x1_sum"], 1)
            for i in range(TILES):
                dve.wait_ge(s["x1_sum"], TILES + i + 1)
                nc.vector.bn_stats(bn[:, i, :], x[:, i, :]).then_inc(s["bn3"], 1)
            dve.wait_ge(s["bn3"], TILES)
            for i in range(TILES):
                ins = nc.vector.bn_aggr(mv[:, i, :], bn[:, i, :])
            link(ins)
            nc.vector.tensor_scalar(ms[:, 0:TILES], mv[:, :, 1:2].rearrange("p a b -> p (a b)"), 1e-5, None, ALU.add).then_inc(s["bn3"], 1)
            dve.wait_ge(s["rstd_x1"], 1)
            for i in range(TILES):
                nc.vector.tensor_scalar(x[:, i, :], x[:, i, :], mv[:, i, 0:1], rs[:, i:i + 1], ALU.subtract, ALU.mult).then_inc(s["x1_done"], 1)

            dve.sem_inc(s["s_psum"], 2)
            dve.sem_inc(s["attn_psum"], 2)
            dve.sem_inc(s["pT_psum"], 2)
            dve.sem_inc(s["attn_taken"], 1)
            dve.sem_inc(s["s_soft"], 1)
            dve.sem_inc(s["s_ms"], 1)
            dve.sem_inc(s["pT_done"], 1)
            dve.sem_inc(s["q_copied"], 2)
            dve.sem_inc(s["q_squared"], 2)
            dve.sem_inc(s["s_shifted"], 2)
            dve.wait_ge(s["x1T_psum"], 1)
            nc.vector.tensor_copy(x1T[:, 0, :], ps[:, 0:2, :].rearrange("p a b -> p (a b)")).then_inc(s["x1T_done"], 1)
            loops.update(sem="attn_chain", per_turn=4 * PAIRS, count=0)
            over = lambda t, n: t[:, n % 2, :].unsqueeze(2).to_broadcast([P, 8, KV])
            with dve.Fori(0, 2) as half:
                base = half * PAIRS
                for m in range(PAIRS + 1):
                    if m < PAIRS:
                        for hd in range(2):
                            dve.wait_ge(s["q_psum"], 2 * (base + m) + hd + 1)
                            if hd == 0:
                                dve.wait_ge(s["s_psum"], base + m + 1)
                            nc.vector.tensor_copy(q_sb[:, m % 2, hd, :], ps[:, hd, :]).then_inc(s["q_copied"], 1)
                    if m >= 1:
                        n = m - 1
                        scores = ps[:, 2 + n % 2, :].rearrange("p (a b) -> p a b", b=KV)
                        dve.wait_ge(s["s_psum"], base + n + 3)
                        nc.vector.tensor_scalar(q_ms[:, n % 2, :], ps[:, 5, 0:8], 1.0 / DH, 1e-5, ALU.mult, ALU.add).then_inc(s["s_ms"], 1)
                        link_loop(nc.vector.tensor_reduce(top[:, n % 2, :], scores, axis=AX.X, op=ALU.max), half)
                        dve.wait_ge(s["s_soft"], base + n + 1)
                        link_loop(nc.vector.tensor_tensor(shift[:, n % 2, :, :], scores, over(top, n), ALU.subtract), half)
                        dve.wait_ge(s["q_rstd"], base + n + 1)
                        nc.vector.tensor_tensor(shift[:, n % 2, :, :], shift[:, n % 2, :, :], over(q_rs, n), ALU.mult).then_inc(s["s_shifted"], 1)
                        dve.wait_ge(s["s_exp"], base + n + 1)
                        link_loop(nc.vector.tensor_reduce(total_e[:, n % 2, :], shift[:, n % 2, :, :], axis=AX.X, op=ALU.add), half)
                        link_loop(nc.vector.reciprocal(total_e[:, n % 2, :], total_e[:, n % 2, :]), half)
                        dve.wait_ge(s["pT_psum"], base + n + 1)
                        nc.vector.tensor_tensor(soft[:, n % 2, :, :], shift[:, n % 2, :, :], over(total_e, n), ALU.mult).then_inc(s["s_soft"], 1)
                dve.wait_ge(s["attn_psum"], base + PAIRS + 2)
                for i in range(4):
                    nc.vector.tensor_tensor(x[:, half * 4 + i, :], x[:, half * 4 + i, :], ps[:, 6 + i // 2, (i % 2) * D:(i % 2 + 1) * D], ALU.add).then_inc(s["attn_taken"], 1)

            def layernorm(before, stats, rstd, done):
                for i in range(TILES):
                    dve.wait_ge(*before(i))
                    nc.vector.bn_stats(bn[:, i, :], x[:, i, :]).then_inc(s[stats], 1)
                dve.wait_ge(s[stats], TILES)
                for i in range(TILES):
                    ins = nc.vector.bn_aggr(mv[:, i, :], bn[:, i, :])
                link(ins)
                nc.vector.tensor_scalar(ms[:, 0:TILES], mv[:, :, 1:2].rearrange("p a b -> p (a b)"), 1e-5, None, ALU.add).then_inc(s[stats], 1)
                dve.wait_ge(s[rstd], 1)
                for i in range(TILES):
                    nc.vector.tensor_scalar(x[:, i, :], x[:, i, :], mv[:, i, 0:1], rs[:, i:i + 1], ALU.subtract, ALU.mult).then_inc(s[done], 1)

            layernorm(lambda i: (s["attn_taken"], i + 2), "bn4", "rstd_x2", "x2_done")
            dve.wait_ge(s["x2_done"], TILES)

            dve.wait_ge(s["ld_idx"], 48)
            dve.wait_ge(s["iota_done"], 3)
            for row_i, width, col, chunks in ((up_row, D, up_col, KD), (down_row, FF, down_col, FCH)):
                link(nc.vector.tensor_copy(row_i, row_i.bitcast(I32)))
                for c in range(chunks):
                    link(nc.vector.tensor_scalar(cmp_row[:, 0:width], row_i, iota_p[:, c:c + 1], None, ALU.is_equal))
                    link(nc.vector.tensor_reduce(col[:, c:c + 1], cmp_row[:, 0:width], axis=AX.X, op=ALU.add))
            state = {"diag": 0, "quant": 0}

            def spread_row(col, chunks, finish):
                for c in range(chunks):
                    nc.vector.tensor_scalar(diag, ident[:, :], col[:, c:c + 1], None, ALU.mult).then_inc(s["counted"], 1)
                    state["diag"] += 1
                    dve.wait_ge(s["mask_psum"], state["diag"])
                    finish(c, ps[:, 5, 0:P]).then_inc(s["mask_done"], 1)
                    dve.wait_ge(s["mask_done"], state["diag"])

            spread_row(up_col, KD, lambda c, v: nc.vector.tensor_scalar(up_mask[:, c * P:(c + 1) * P], v, 1.0, None, ALU.min))
            spread_row(down_col, FCH, lambda c, v: nc.vector.tensor_scalar(down_mask[:, c * P:(c + 1) * P], v, 1.0, None, ALU.min))

            def scales(maxima, inverse, scale):
                link(nc.vector.reciprocal(inverse, maxima))
                link(nc.vector.tensor_scalar(scale, maxima, 1.0 / FP8_MAX, None, ALU.mult))

            def round_fp8(v, tmp, result):
                link(nc.vector.tensor_scalar(tmp.bitcast(I32), v.bitcast(I32), EXPONENT, None, ALU.bitwise_and))
                link(nc.vector.tensor_scalar(tmp, tmp, LEAST_NORMAL, ROUND_AT, ALU.max, ALU.mult))
                link(nc.vector.tensor_tensor(v, v, tmp, ALU.add))
                return nc.vector.tensor_tensor(result, v, tmp, ALU.subtract)

            for m in range(2):
                dve.wait_ge(s["gathered_w"], 16 * FCH * (m + 1))
                if m:
                    dve.wait_ge(s["wT_psum"], 2 * m)
                nc.vector.tensor_tensor(wq_a, w_raw, up_mask.unsqueeze(1).to_broadcast([P, FCH, D]), ALU.mult).then_inc(s["quant_done"], 1)
                dve.wait_ge(s["quant_done"], 2 * m + 1)
                link(nc.vector.tensor_reduce(rmax[:, :], wq_a, axis=AX.X, op=ALU.max, apply_absolute_value=True))
                scales(rmax[:, :], rinv[:, :], rscale[:, :])
                for c in range(FCH):
                    ins = nc.vector.tensor_scalar(wq_a[:, c, :], wq_a[:, c, :], rinv[:, c:c + 1], FP8_MAX, ALU.mult, ALU.mult)
                link(ins)
                round_fp8(wq_a, wq_b, w_q8).then_inc(s["quant_done"], 1)
                for k in range(KD):
                    dve.wait_ge(s["wT_psum"], 2 * m + k + 1)
                    nc.vector.tensor_scalar(w_fp8T[m][:, k, :], ps[:, k, 0:FPAD // 2].bitcast(BF16), up_col[:, k:k + 1], None, ALU.mult).then_inc(s["wT_done"], 1)
                if m == 0:
                    spread_row(rscale, FCH, lambda c, v: nc.vector.tensor_copy(scale_rows[0][:, c * P:(c + 1) * P], v))
                else:
                    spread_row(rscale, FCH, lambda c, v: nc.vector.tensor_tensor(scale_rows[1][:, c * P:(c + 1) * P], v, down_mask[:, c * P:(c + 1) * P], ALU.mult))
            dve.wait_ge(s["ld_down"], 16)
            link(nc.vector.tensor_tensor(wd_a, wd_raw, down_mask[:, 0:FF].unsqueeze(1).to_broadcast([P, KD, FF]), ALU.mult))
            link(nc.vector.tensor_reduce(rmax[:, 0:KD], wd_a, axis=AX.X, op=ALU.max, apply_absolute_value=True))
            scales(rmax[:, 0:KD], rinv[:, 0:KD], rscale[:, 0:KD])
            for c in range(KD):
                ins = nc.vector.tensor_scalar(wd_a[:, c, :], wd_a[:, c, :], rinv[:, c:c + 1], FP8_MAX, ALU.mult, ALU.mult)
            link(ins)
            round_fp8(wd_a, wd_b, wd_q8[:, :, 0:FF]).then_inc(s["quant_done"], 1)
            for c in range(FCH):
                dve.wait_ge(s["wT_psum"], 5 + c)
                nc.vector.tensor_scalar(w_dT[:, c, :], ps[:, c % 2, 0:D // 2].bitcast(BF16), down_col[:, c:c + 1], None, ALU.mult).then_inc(s["wT_done"], 1)
            spread_row(rscale, KD, lambda c, v: nc.vector.tensor_copy(scale_d[:, c * P:(c + 1) * P], v))
            link(nc.vector.tensor_tensor(xm, x[:, :, :], up_mask.unsqueeze(1).to_broadcast([P, TILES, D]), ALU.mult))
            link(nc.vector.tensor_reduce(xmax[:, :], xm, axis=AX.X, op=ALU.max, apply_absolute_value=True))
            scales(xmax[:, :], xinv[:, :], xscale[:, :])
            for i in range(TILES):
                ins = nc.vector.tensor_scalar(xv[:, i, :], xm[:, i, :], xinv[:, i:i + 1], FP8_MAX, ALU.mult, ALU.mult)
            link(ins)
            round_fp8(xv, xr_, qx).then_inc(s["x_quant"], 1)
            dve.wait_ge(s["xT8_psum"], 1)
            nc.vector.tensor_copy(qxT[:, 0, :], ps[:, 0, :].bitcast(BF16)).then_inc(s["xT8_done"], 1)
            loops.update(sem="ff_chain", per_turn=9, count=0)
            dve.sem_inc(s["t_done"], 1)
            dve.sem_inc(s["y2_read"], 1)
            dve.sem_inc(s["ff_read"], 1)
            with dve.Fori(0, TILES) as i:
                dve.wait_ge(s["ff_psum"], i + 1)
                gate = ps[:, 0:2, 0:FF // 2]
                up = ps[:, 2:4, 0:FF // 2]
                two = lambda t: t[:, 0:FF].rearrange("p (a b) -> p a b", a=2)
                dve.wait_ge(s["t_done"], i + 1)
                nc.vector.tensor_tensor(two(gs), gate, two(scale_rows[0]), ALU.mult).then_inc(s["ff_in"], 1)
                nc.vector.scalar_tensor_tensor(two(us), up, xscale[:, bass.ds(i, 1)], two(scale_rows[1]), ALU.mult, ALU.mult).then_inc(s["ff_read"], 1)
                dve.wait_ge(s["ff_read"], i + 2)
                dve.wait_ge(s["ff_gate"], i + 1)
                link_loop(nc.vector.tensor_tensor(ts_, gs, us, ALU.mult), i)
                link_loop(nc.vector.tensor_reduce(tmax[:, :], ts_, axis=AX.X, op=ALU.max, apply_absolute_value=True), i)
                link_loop(nc.vector.reciprocal(tinv[:, :], tmax[:, :]), i)
                link_loop(nc.vector.tensor_scalar(tscale[:, bass.ds(i, 1)], tmax[:, :], 1.0 / FP8_MAX, None, ALU.mult), i)
                link_loop(nc.vector.tensor_scalar(tv, ts_, tinv[:, 0:1], FP8_MAX, ALU.mult, ALU.mult), i)
                link_loop(nc.vector.tensor_scalar(tr.bitcast(I32), tv.bitcast(I32), EXPONENT, None, ALU.bitwise_and), i)
                link_loop(nc.vector.tensor_scalar(tr, tr, LEAST_NORMAL, ROUND_AT, ALU.max, ALU.mult), i)
                link_loop(nc.vector.tensor_tensor(tv, tv, tr, ALU.add), i)
                nc.vector.tensor_tensor(qt[:, 0:FF], tv, tr, ALU.subtract).then_inc(s["t_done"], 1)
                dve.wait_ge(s["y2_psum"], i + 1)
                link_loop(nc.vector.scalar_tensor_tensor(y_s, ps[:, 5, 0:D], tscale[:, bass.ds(i, 1)], scale_d, ALU.mult, ALU.mult), i)
                nc.vector.tensor_tensor(x[:, i, :], x[:, i, :], y_s, ALU.add).then_inc(s["y2_read"], 1)
            layernorm(lambda i: (s["y2_read"], i + 2), "bn5", "rstd_out", "out_done")

        @block.tensor
        def _(pe):
            pe.wait_ge(s["consts"], 1)
            for k in range(KD):
                for i in range(TILES):
                    if k == 0:
                        pe.wait_ge(s["xn"], i + 1)
                    ins = nc.tensor.transpose(ps[:, 2 * k + i // 4, (i % 4) * P:(i % 4 + 1) * P],
                                              xn[:, i, k * P:(k + 1) * P], ident[:, :])
                ins.then_inc(s["hs_psum"], 1)
            pe.wait_ge(s["ld_win"], 16)
            pe.wait_ge(s["hsT"], 2)
            for n in range(4 * CI):
                c, half = divmod(n, 2)
                if n >= 4:
                    pe.wait_ge(s["in_out"], n - 3)
                for k in range(KD):
                    ins = nc.tensor.matmul(ps[:, 4 + n % 4, :], w_in[:, k, c * P:(c + 1) * P], hT[:, k, half * HALF:(half + 1) * HALF],
                                           start=(k == 0), stop=(k == KD - 1))
                ins.then_inc(s["in_psum"], 1)
            pe.wait_ge(s["ld_wx"], 16)
            pe.wait_ge(s["conv_out"], CI)
            for i in range(TILES):
                for c in range(CI):
                    ins = nc.tensor.matmul(ps[:, i // 2, (i % 2) * D:(i % 2) * D + XP], xc[:, c, i * P:(i + 1) * P], w_x[:, c, :],
                                           start=(c == 0), stop=(c == CI - 1))
                ins.then_inc(s["xproj_psum"], 1)
            pe.wait_ge(s["xdbn"], 1)
            for i in range(TILES):
                ins = nc.tensor.transpose(ps[:, i // 4, (i % 4) * P:(i % 4 + 1) * P], xdb[:, i, 0:DR], ident[:, :])
            ins.then_inc(s["dtn_psum"], 1)
            pe.wait_ge(s["xdbn"], 3)
            for i in range(TILES):
                ins = nc.tensor.transpose(ps[0:2 * NS, 2 + i // 4, (i % 4) * P:(i % 4 + 1) * P], xdb[:, i, DR:XP], ident[:, :])
            ins.then_inc(s["bc_psum"], 1)
            pe.wait_ge(s["ld_wd"], 16)
            pe.wait_ge(s["dtn_sb"], 1)
            pe.wait_ge(s["in_out"], 4 * CI)
            for c in range(CI):
                if c >= 2:
                    pe.wait_ge(s["dt_act"], 3 * (c - 2) + 2)
                for half in range(2):
                    nc.tensor.matmul(ps[:, 4 + 2 * (c % 2) + half, :], w_dt[:, c * P:(c + 1) * P], dtnT[:, half * HALF:(half + 1) * HALF],
                                     start=True, stop=True).then_inc(s["dt_psum"], 1)
            pe.wait_ge(s["selectors"], 4)
            pe.wait_ge(s["bc_split"], 2)
            pe.wait_ge(s["dt_act"], 3 * CI)

            def spread(bank, row, ready):
                for half in range(2):
                    ins = nc.tensor.matmul(ps[:, bank + half, :], row_of[:, row, :], bc3[:, half * HALF:(half + 1) * HALF],
                                           start=True, stop=True)
                ins.then_inc(s[ready], 1)

            def sum_states(n):
                for half in range(2):
                    ins = nc.tensor.matmul(ps[:, 4 + half, :], ident[:, :], hC[:, n % 2, half * HALF:(half + 1) * HALF],
                                           start=(n == 0), stop=(n == NS - 1))
                ins.then_inc(s["y_summed"], 1)

            with pe.Fori(0, CI) as c:
                for n in range(NS):
                    unit = c * NS + n
                    pe.wait_ge(s["dbx_done"], unit + 1)
                    spread(0, n, "b_ready")
                    pe.wait_ge(s["hc_done"], unit + 1)
                    spread(2, NS + n, "c_ready")
                    if n == 1:
                        pe.wait_ge(s["y_drained"], c + 1)
                    if n:
                        sum_states(n - 1)
                pe.wait_ge(s["hc_done"], (c + 1) * NS + 1)
                sum_states(NS - 1)
            pe.wait_ge(s["ld_wo"], 16)
            pe.wait_ge(s["ym_done"], CI)
            for i in range(TILES):
                for c in range(CI):
                    ins = nc.tensor.matmul(ps[:, i // 2, (i % 2) * D:(i % 2 + 1) * D], dtx[:, c, i * P:(i + 1) * P], w_out[:, c, :],
                                           start=(c == 0), stop=(c == CI - 1))
                ins.then_inc(s["out_psum"], 1)
            for k in range(KD):
                for i in range(TILES):
                    if k == 0:
                        pe.wait_ge(s["hn_done"], i + 1)
                    ins = nc.tensor.transpose(ps[:, 4 + 2 * k + i // 4, (i % 4) * P:(i % 4 + 1) * P], hn[:, i, k * P:(k + 1) * P], ident[:, :])
                ins.then_inc(s["hn_psum"], 1)
            pe.wait_ge(s["hfT_done"], KD)
            pe.wait_ge(s["res_done"], 1)
            pe.wait_ge(s["ld_small"], 64)
            for i in range(TILES):
                for k in range(KD):
                    ins = nc.tensor.matmul(ps[:, 0, i * E:(i + 1) * E], hfT[:, k, i * P:(i + 1) * P], w_router[:, k, :],
                                           start=(k == 0), stop=(k == KD - 1))
            ins.then_inc(s["logit_psum"], 1)
            pe.wait_ge(s["tables"], 3)
            pe.wait_ge(s["picked_done"], 3)
            nc.tensor.matmul(ps[:, 1, 0:E], ones[:, :], earlier[:, TILES - 1, :], start=True, stop=False)
            nc.tensor.matmul(ps[:, 1, 0:E], ones[:, :], both[:, TILES - 1, :], start=False, stop=True)
            flat = lambda t: t[:, :, :].rearrange("p i e -> p (i e)")
            nc.tensor.matmul(ps[:, 1, E:E + TILES * E], ones[:, :], flat(earlier), start=True, stop=False)
            nc.tensor.matmul(ps[:, 1, E:E + TILES * E], before[:, :], flat(both), start=False, stop=True).then_inc(s["prefix_psum"], 1)
            kv = [0]

            def kv_bank():
                if kv[0] >= 6:
                    pe.wait_ge(s["kv_out"], kv[0] - 5)
                kv[0] += 1
                return 2 + (kv[0] - 1) % 6

            pe.wait_ge(s["hfT_done"], KD)
            pe.wait_ge(s["ld_v"], 32)
            for n in range(PAIRS):
                bank = kv_bank()
                for hd in range(2):
                    ins = nc.tensor.matmul(ps[:, bank, hd * KVT:(hd + 1) * KVT], w_v[:, (2 * n + hd) * DH:(2 * n + hd + 1) * DH], ctxT, start=True, stop=True)
                ins.then_inc(s["kv_psum"], 1)
            pe.wait_ge(s["ld_o"], 16)
            for n in range(2 * PAIRS):
                bank = kv_bank()
                if n % 2 == 0:
                    pe.wait_ge(s["kv_out"], n // 2 + 1)
                for b in range(2 * (n % 2), 2 * (n % 2) + 2):
                    for hd in range(2):
                        ins = nc.tensor.matmul(ps[hd * KV:(hd + 1) * KV, bank, (b % 2) * D:(b % 2 + 1) * D], vT[:, 2 * (n // 2) + hd, b * KV:(b + 1) * KV],
                                               w_o[:, 2 * (n // 2) + hd, :], start=True, stop=True)
                ins.then_inc(s["kv_psum"], 1)
            pe.wait_ge(s["ld_k"], 16)
            for n in range(8):
                bank = kv_bank()
                ins = nc.tensor.matmul(ps[:, bank, :], ctxT[:, (n // 4) * P:(n // 4 + 1) * P], w_k[:, (n % 4) * HALF:(n % 4 + 1) * HALF], start=True, stop=True)
                ins.then_inc(s["kv_psum"], 1)
            pe.wait_ge(s["k_normed"], 1)
            for n in range(PAIRS):
                bank = kv_bank()
                for hd in range(2):
                    for j in range(2):
                        at = (2 * n + hd) * DH
                        ins = nc.tensor.transpose(ps[:, bank, hd * KVT + j * P:hd * KVT + (j + 1) * P], k_raw[:, j, at:at + DH], ident[:, :])
                ins.then_inc(s["kv_psum"], 1)
            pe.wait_ge(s["kv_out"], kv[0])
            pe.wait_ge(s["slots_done"], 1)

            def transpose_rows(tile):
                pe.wait_ge(s["row_ready"], tile + 1)
                pe.wait_ge(s["xT_done"], tile + 1)
                for k in range(KD):
                    ins = nc.tensor.transpose(ps[:, 7, k * P:(k + 1) * P], row_in[:, k * P:(k + 1) * P], ident[:, :])
                ins.then_inc(s["xT_psum"], 1)

            transpose_rows(0)
            for e in range(E):
                w1, w3, w2 = (w_moe[e % 2][:, k * FCH * D:(k + 1) * FCH * D].rearrange("p (k n) -> p k n", k=kk) for k, kk in ((0, KD), (1, KD), (2, FCH)))
                first = pe.value_load(bounds[0:1, e:e + 1], min_val=0, max_val=OUT_TILES - 1)
                last = pe.value_load(bounds[0:1, e + 1:e + 2], min_val=1, max_val=OUT_TILES)
                pe.wait_ge(s[f"ld_w{e % 2}"], 16 * (e // 2 + 1))
                with pe.Fori(first, last) as j:
                    pe.wait_ge(s["xT_done"], j + 2)
                    for q in range(FCH // 2):
                        pe.wait_ge(s["hid_done"], j * (FCH // 2) + q + 1)
                        for w, bank in ((w1, 2 * q), (w3, 2 * q + 1)):
                            for c in range(2):
                                for k in range(KD):
                                    at = (2 * q + c) * P
                                    ins = nc.tensor.matmul(ps[:, bank, c * P:(c + 1) * P], w[:, k, at:at + P], xT[:, k, :],
                                                           start=(k == 0), stop=(k == KD - 1))
                        ins.then_inc(s["gu_psum"], 1)
                    transpose_rows(j + 1)
                    pe.wait_ge(s["y_ready"], j + 1)
                    for c in range(FCH):
                        if c % 2 == 0:
                            pe.wait_ge(s["hid_done"], (j + 1) * (FCH // 2) + c // 2 + 1)
                        ins = nc.tensor.matmul(ps[:, 6, 0:D], hid[:, c, :], w2[:, c, :], start=(c == 0), stop=(c == FCH - 1))
                    ins.then_inc(s["y_psum"], 1)
            for i in range(TILES):
                pe.wait_ge(s["x1_done"], i + 1)
                for k in range(KD):
                    ins = nc.tensor.transpose(ps[:, 2 * k + i // 4, (i % 4) * P:(i % 4 + 1) * P], x[:, i, k * P:(k + 1) * P], ident[:, :])
                    if i == TILES - 1:
                        ins.then_inc(s["x1T_psum"], 1)
            pe.wait_ge(s["x1T_done"], 2)
            pe.wait_ge(s["ld_q"], 16)
            with pe.Fori(0, 2) as half:
                base = half * PAIRS
                for m in range(PAIRS + 2):
                    if m < PAIRS:
                        for hd in range(2):
                            pe.wait_ge(s["q_copied"], 2 * (base + m) + hd + 1)

                            for k in range(KD):
                                at = (2 * m + hd) * DH
                                ins = nc.tensor.matmul(ps[:, hd, :], w_q[:, k, at:at + DH], x1T[:, k, bass.ts(half, HALF)], start=(k == 0), stop=(k == KD - 1))
                            ins.then_inc(s["q_psum"], 1)
                    if m >= 2:
                        n = m - 2
                        pe.wait_ge(s["s_soft"], base + n + 2)
                        pe.wait_ge(s["pT_done"], base + n + 1)
                        for i in range(4):
                            ins = nc.tensor.transpose(ps[:, 4, i * P:(i + 1) * P], soft[:, n % 2, 2 * i:2 * i + 2, :].rearrange("p a b -> p (a b)"), ident[:, :])
                        ins.then_inc(s["pT_psum"], 1)
                        pe.wait_ge(s["pT_done"], base + n + 2)
                        if n == 0:
                            pe.wait_ge(s["attn_taken"], half * 4 + 1)
                        for i in range(4):
                            ins = nc.tensor.matmul(ps[:, 6 + i // 2, (i % 2) * D:(i % 2 + 1) * D], pT[:, n % 2, i * P:(i + 1) * P],
                                                   vw[:, n, half * 2 + i // 2, :], start=(n == 0 and i % 2 == 0), stop=(n == PAIRS - 1),
                                                   skip_group_check=True)
                        ins.then_inc(s["attn_psum"], 1)
                    if m < PAIRS:
                        pe.wait_ge(s["q_copied"], 2 * (base + m) + 4)
                        pe.wait_ge(s["s_shifted"], base + m + 1)
                        for i in range(4):
                            for hd in range(2):
                                nc.tensor.matmul(ps[:, 2 + m % 2, (2 * i + hd) * KV:(2 * i + hd + 1) * KV], q_sb[:, m % 2, hd, i * P:(i + 1) * P],
                                                 kT[:, 2 * m + hd, bass.ds((half * 2 + i // 2) * KV, KV)], start=True, stop=True)
                        pe.wait_ge(s["q_squared"], 2 * (base + m) + 4)
                        pe.wait_ge(s["s_ms"], base + m + 1)
                        for i in range(4):
                            for hd in range(2):
                                ins = nc.tensor.matmul(ps[:, 5, 2 * i + hd:2 * i + hd + 1], q_sq[:, m % 2, hd, i * P:(i + 1) * P], ones[:, 0:1], start=True, stop=True)
                        ins.then_inc(s["s_psum"], 1)
            state = {"diag": 0}

            def spread_rows(n):
                for _ in range(n):
                    state["diag"] += 1
                    pe.wait_ge(s["counted"], state["diag"])
                    if state["diag"] > 1:
                        pe.wait_ge(s["mask_done"], state["diag"] - 1)
                    nc.tensor.matmul(ps[:, 5, 0:P], ones[:, :], diag, start=True, stop=True).then_inc(s["mask_psum"], 1)

            spread_rows(KD + FCH)
            pe.wait_ge(s["tables"], 4)
            for m in range(2):
                pe.wait_ge(s["quant_done"], 2 * m + 2)
                if m:
                    pe.wait_ge(s["wT_done"], 2 * m)
                for k in range(KD):
                    for c in range(FCH):
                        ins = nc.tensor.transpose(ps[:, k, c * P // 2:(c + 1) * P // 2].bitcast(BF16), w_q8[:, c, k * P:(k + 1) * P], ident16[:, :])
                    ins.then_inc(s["wT_psum"], 1)
                spread_rows(FCH)
            pe.wait_ge(s["quant_done"], 5)
            for c in range(FCH):
                pe.wait_ge(s["wT_done"], 4 if c < 2 else 3 + c)
                for k in range(KD):
                    ins = nc.tensor.transpose(ps[:, c % 2, k * P // 2:(k + 1) * P // 2].bitcast(BF16), wd_q8[:, k, c * P:(c + 1) * P], ident16[:, :])
                ins.then_inc(s["wT_psum"], 1)
            spread_rows(KD)
            pe.wait_ge(s["wT_done"], 10)
            pe.wait_ge(s["x_quant"], 1)
            for k in range(KD):
                for i in range(TILES):
                    ins = nc.tensor.transpose(ps[:, 2 * k, i * P // 2:(i + 1) * P // 2].bitcast(BF16), qx[:, i, k * P:(k + 1) * P], ident16[:, :])
                ins.then_inc(s["xT8_psum"], 1)
            pe.wait_ge(s["xT8_done"], 2)

            def up_and_gate(i):
                for m in range(2):
                    for part in range(2):
                        for k in range(KD):
                            ins = nc.tensor.matmul(ps[:, 2 * m + part, 0:FF // 2], qxT[:, k, bass.ts(i, P)], w_fp8T[m][:, k, part * FF // 2:(part + 1) * FF // 2],
                                                   start=(k == 0), stop=(k == KD - 1))
                ins.then_inc(s["ff_psum"], 1)

            with pe.Fori(0, TILES) as i:
                pe.wait_ge(s["ff_read"], i + 1)
                up_and_gate(i)
                pe.wait_ge(s["t_done"], i + 2)
                for c in range(FCH):
                    ins = nc.tensor.transpose(ps[:, 4, c * P // 2:(c + 1) * P // 2].bitcast(BF16), qt[:, c * P:(c + 1) * P], ident16[:, :])
                ins.then_inc(s["t_psum"], 1)
                pe.wait_ge(s["tT_done"], i + 1)
                pe.wait_ge(s["y2_read"], i + 1)
                for c in range(FCH):
                    ins = nc.tensor.matmul(ps[:, 5, 0:D], qtT[:, c, :], w_dT[:, c, :], start=(c == 0), stop=(c == FCH - 1))
                ins.then_inc(s["y2_psum"], 1)


def kernel(**inputs):
    import concourse.bacc as bacc
    from concourse.bass_utils import run_bass_kernel_spmd

    def a(name):
        return np.asarray(inputs["L0_attn_" + name])

    def xa(name):
        return np.asarray(inputs["L0_xattn_" + name])

    def ff(name):
        return np.asarray(inputs["L0_ffn_" + name])

    def chunked(w):
        return w.reshape(-1, P, w.shape[1]).transpose(1, 0, 2)

    def index(v):
        return v.view(np.int32)[::2] if v.dtype.itemsize == 8 else v.view(np.int32)

    w_moe = np.zeros((E, P, MOE_W), np.float32)
    for e in range(E):
        for k, name in enumerate(("w1", "w3")):
            at = k * KD * FPAD
            w_moe[e, :, at:at + KD * FPAD].reshape(P, KD, FPAD)[:, :, :FF] = chunked(a(name)[e].T)
        w2 = np.zeros((FPAD, D), np.float32)
        w2[:FF] = a("w2")[e].T
        w_moe[e, :, 2 * KD * FPAD:] = chunked(w2).reshape(P, -1)
    up, down = index(ff("up_reorder_index")), index(ff("down_reorder_index"))
    down_at = np.zeros(FPAD, np.int32)
    down_at[:FF] = down
    lane = [a("conv_w"), a("conv_b")[:, None], a("dt_proj_b")[:, None], a("D_param")[:, None], a("A_log")]
    cols = [chunked(a("ln_in_w")[:, None])[:, :, 0], a("dt_ln_w")[:, None], chunked(a("ln_ff_w")[:, None])[:, :, 0],
            xa("gq")[:, None], xa("gk")[:, None]]
    data = dict(
        x=np.asarray(inputs["x"]), w_in=chunked(a("in_proj_w").T), cols=np.concatenate(cols, 1),
        bc_ln=np.concatenate([a("b_ln_w"), a("c_ln_w")])[:, None], lane=chunked(np.concatenate(lane, 1)),
        w_x=chunked(a("x_proj_w").T), w_dt=a("dt_proj_w").T, w_out=chunked(a("out_proj_w").T), ln_ff=a("ln_ff_w")[None],
        w_router=chunked(a("router_w").T), w_moe=w_moe, ctxT=np.asarray(inputs["ctx_1024"]).reshape(KVT, CTX).T,
        w_q=chunked(xa("Wq")), w_k=xa("Wk"), w_v=xa("Wv"), w_o=chunked(xa("Wo")),
        w_gate=ff("w_gate"), w_up=ff("w_up"), w_down=chunked(ff("w_down")),
        up_index=up[None], down_index=down[None], down_at=down_at.reshape(FCH, P).T)
    nc = bacc.Bacc("TRN2", target_bir_lowering=False, num_devices=1)
    arrays, inp = {}, {}
    for name, v in data.items():
        v = np.ascontiguousarray(v)
        arrays["in_" + name] = v
        inp[name] = nc.dram_tensor("in_" + name, v.shape, I32 if v.dtype == np.int32 else F32, kind="ExternalInput").ap()
    out = nc.dram_tensor("out", (BATCH, SEQ, D), F32, kind="ExternalOutput").ap()
    build(nc, inp, out)
    return run_bass_kernel_spmd(nc, [arrays], core_ids=[0]).results[0]["out"]
```

```python
from contextlib import ExitStack

import numpy as np

import concourse.bass as bass
from concourse import mybir

F32, BF16 = mybir.dt.float32, mybir.dt.bfloat16
I32, U32 = mybir.dt.int32, mybir.dt.uint32
ALU, ACT, AX = mybir.AluOpType, mybir.ActivationFunctionType, mybir.AxisListType

P = 128
BATCH, SEQ, D = 4, 256, 256
T = BATCH * SEQ
TILES = T // P
KD = D // P
HALF = 512
DI, NS, DR, TAPS = 512, 16, 128, 4
CI = DI // P
XP = DR + 2 * NS
UNITS = CI * NS
LANES = (("conv_w", TAPS), ("conv_b", 1), ("dt_b", 1), ("d_param", 1), ("a_log", NS))
E, FF = 8, 704
FCH = -(-FF // P)
MOE_W = 3 * FCH * D
OUT_TILES = 2 * TILES + E - 1
IN_TILES = OUT_TILES - 1 + TILES
HEADS, DH, KV, CTX = 16, 128, 64, 128
PAIRS = HEADS // 2
KVT = BATCH * KV
FPAD = FCH * P
FP8_MAX = 448.0
ROUND_AT = 2.0 ** 20
LEAST_ADDED = 1.5 * 2.0 ** 14
NOT_SIGN = 0x7FFFFFFF
ARENA_KB = 181
LANE_AT = {}
for _name, _n in LANES:
    LANE_AT[_name] = sum(n for _, n in LANES[:len(LANE_AT)])
LANE_W = sum(n for _, n in LANES)
LOG1P = ((-2.3201779192559524, 0.4319853169731413), (-1.423605531584339, 2.6994923737791177),
         (-0.08170957446752569, 3.254352199747658), (1.0093947016519729, 1.104990747000989))
LOG1P_SCALE = 0.0052534577981952985


def build(nc, inp, out):
    with ExitStack() as ctx:
        def sb(name, shape, dt=F32):
            return ctx.enter_context(nc.sbuf_tensor(name, shape, dt))

        def sem(name):
            return ctx.enter_context(nc.semaphore(name))

        arena = sb("arena", [P, ARENA_KB * 256])

        def view(at_kb, shape, dt=F32, rows=P):
            size = int(np.prod(shape)) * (2 if dt == BF16 else 4)
            assert at_kb * 1024 + size <= ARENA_KB * 1024 and size % 4 == 0
            at = int(at_kb * 256)
            v = arena[0:rows, at:at + size // 4]
            if dt != F32:
                v = v.bitcast(dt)
            dims = ["a", "b", "c"][:len(shape)]
            if len(shape) > 1:
                v = v.rearrange(f"p ({' '.join(dims)}) -> p {' '.join(dims)}", **dict(zip(dims[1:], shape[1:])))
            return v

        x = sb("x", [P, TILES, D])
        cols = sb("cols", [P, 7])
        bc_ln = sb("bc_ln", [2 * NS, 1])
        lane = sb("lane", [P, CI, LANE_W])
        a_neg = sb("a_neg", [P, CI, NS])
        ident = sb("ident", [P, P])
        ones = sb("ones", [P, P])
        before = sb("before", [P, P])
        ln_ff_row = sb("ln_ff_row", [P, D])
        zero = sb("zero", [P, D])
        neg_half = sb("neg_half", [P, P])
        shifts = sb("shifts", [P, len(LOG1P)])
        ms = sb("ms", [P, P])
        rs = sb("rs", [P, P])
        xpad = view(0, [CI, BATCH, SEQ + TAPS - 1])
        u, rv = view(0, [2, T]), view(8, [2, T])
        w_in, hT, conv = view(16.5, [KD, 2 * DI]), view(24.5, [KD, T]), view(32.5, [2, T])
        zs, xc, dt, dtx = (view(40.5 + 16 * k, [CI, T]) for k in range(4))
        xdb, junk = view(163, [TILES, XP]), view(168, [TILES, XP])
        dBx, h = view(0, [2, T]), view(8, [2, T])
        dtnT = view(173, [T])
        bcf, bc_rest = view(177, [T], rows=2 * NS), view(104.5, [T], rows=2 * NS)
        bc_mid, bc3 = view(108.5, [T], BF16, rows=2 * NS), view(128.5, [T], BF16, rows=96)
        hC, dA = view(130.5, [2, T]), view(138.5, [2, T])
        squares = [view(at, [T]) for at in (119.5, 123.5, 130.5, 134.5)]
        xn = view(130.5, [TILES, D])
        w_x, w_dt, w_out = view(146.5, [CI, XP]), view(149, [DI]), view(151, [CI, D])
        row_of = view(155, [2 * NS, P], BF16, rows=96)
        w_moe = [view(163, [MOE_W]), view(16.5, [MOE_W])]
        res, hn = view(0, [TILES, D]), view(8, [TILES, D])
        x_rows = [view(40.5, [TILES, D]), view(48.5, [TILES, D])]
        hfT = view(56.5, [KD, T])
        row_in, xT, hid = view(64.5, [D]), view(65.5, [KD, P]), view(66.5, [FCH, P])
        act_g3, y_row = view(69.5, [3, 2 * P]), view(72.5, [D])
        y_got = [view(163, [TILES, D]), view(171, [TILES, D])]
        w_router = sb("w_router", [P, KD, E])
        logit = sb("logit", [P, TILES, E])
        prob = sb("prob", [P, TILES, E])
        best = sb("best", [P, TILES, 8])
        best_at = sb("best_at", [P, TILES, 8], U32)
        best_f = sb("best_f", [P, TILES, 8])
        picked = [sb(f"picked{k}", [P, TILES, E]) for k in range(2)]
        both = sb("both", [P, TILES, E])
        earlier = sb("earlier", [P, TILES, E])
        iota_e = sb("iota_e", [P, E])
        place = sb("place", [P, TILES, E])
        stat = sb("stat", [P, 4, TILES])
        count = sb("count", [P, 4, E])
        count_i = sb("count_i", [P, E], I32)
        n_tiles = sb("n_tiles", [P, E], I32)
        bounds = sb("bounds", [P, E + 1], I32)
        slot_f = sb("slot_f", [P, 2, TILES])
        slot = sb("slot", [P, 2, TILES], U32)
        bn = sb("bn", [P, TILES, 6])
        mv = sb("mv", [P, TILES, 2])
        ctxT = view(89.5, [KVT])
        vw = view(90.5, [PAIRS, BATCH, D])
        w_v, vT, w_o = view(123, [HEADS * DH]), view(131, [HEADS, KVT]), view(147, [HEADS, D])
        w_k, k_raw, k_junk = view(123, [HEADS * DH]), view(131, [2, HEADS * DH]), view(147, [2, HEADS * DH])
        kT = view(147, [HEADS, KVT])
        w_qT, w_q = view(0, [HEADS, D]), view(16.5, [KD, HEADS * DH])
        qk = [view(40.5, [BATCH, HEADS, KV]), view(123, [BATCH, HEADS, KV])]
        x1T, x_now, q_junk = view(147, [KD, T]), view(155, [2, KD, P]), view(157, [2, HALF])
        shift, soft, pT = view(163, [2, HEADS, KV]), view(171, [2, HEADS, KV]), view(0, [2, PAIRS, P])
        gqk = sb("gqk", [P, 1])
        k_ms = sb("k_ms", [P, 2 * HEADS])
        k_rs = sb("k_rs", [P, 2 * HEADS])
        top = sb("top", [P, 2, HEADS])
        q_ms = sb("q_ms", [P, 2, HEADS])
        q_rs = sb("q_rs", [P, 2, HEADS])
        total_e = sb("total_e", [P, 2, HEADS])
        up_row, down_row, compared = view(96, [D]), view(97, [FF]), view(99.75, [FF])
        down_diag, up_diag = view(90, [FCH, P]), view(93, [KD, P])
        up_mask, down_mask = sb("up_mask", [P, D]), view(96, [FPAD])
        w_raw = [view(72.5, [FCH, D]), view(78.5, [FCH, D]), view(84.5, [KD, FF])]
        w_size = [view(66.5, [FCH * D]), view(66.5, [FCH * D]), view(90, [KD * FF])]
        w_fp8 = [view(110.5, [FCH, D], BF16), view(113.5, [FCH, D], BF16), view(116.5, [KD, FPAD], BF16)]
        w_fp8T = [view(73.5, [KD, FPAD], BF16), view(76.5, [KD, FPAD], BF16), view(79.5, [FCH, D], BF16)]
        diag = view(82.5, [FCH, P])
        scale_rows = [view(56.5, [FPAD]), view(59.5, [FPAD]), view(62.5, [D])]
        x_in, x_size = view(90.5, [TILES, D]), view(98.5, [TILES, D])
        qx, qxT = view(106.5, [TILES, D], BF16), view(110.5, [KD, T], BF16)
        gate_s, up_s = view(0, [2, FF]), view(6, [2, FF])
        prod, t_in, t_size = view(12, [FF]), view(15, [FF]), view(18, [FF])
        t_fp8, t_fp8T = view(21, [FPAD], BF16), view(23, [FCH, P], BF16)
        y_s = view(25, [D])
        up_col = sb("up_col", [P, KD])
        down_col = sb("down_col", [P, FCH])
        down_one = sb("down_one", [P, FCH])

        iota_p = sb("iota_p", [P, FCH])
        gather_at = sb("gather_at", [P, FCH], I32)
        w_max = sb("w_max", [P, 3, FCH])
        w_inv = sb("w_inv", [P, 3, FCH])
        w_scale = sb("w_scale", [P, 3, FCH])
        xmax = sb("xmax", [P, TILES])
        xinv = sb("xinv", [P, TILES])
        xscale = sb("xscale", [P, TILES])
        tmax = sb("tmax", [P, 1])
        tinv = sb("tinv", [P, 1])
        tscale = sb("tscale", [P, 2])
        ident16 = sb("ident16", [P, P], BF16)
        moe_in = nc.dram_tensor("moe_in", (IN_TILES * P, D), F32).ap()
        moe_out = nc.dram_tensor("moe_out", (OUT_TILES * P, D), F32).ap()
        ps = ctx.enter_context(nc.psum_tensor("ps", [P, 8, HALF], F32))

        names = """ld_x ld_small ld_win ld_wx ld_wd ld_wo consts pads selectors
            sumsq1 ms1 rstd1 xn hs_psum hsT in_psum in_out conv_acc conv_out xproj_psum xdb_sb
            ms2 rstd2 xdbn dtn_psum bc_psum dtn_sb bc_sb dt_psum dt_act softplus square_ready factor_taken a_exp a_ready bc_split
            b_ready c_ready da_ready dbx_done scan_done hc_done y_summed y_drained ym_done
            out_psum dve_chain st_out
            ld_lnff iota tables zero_set moe_zeroed res_done sumsq3 ms3 rstd3 hn_done hn_psum hfT_done logit_psum
            logit_sub logit_exp picked_done prefix_psum slots_done scattered ld_rows0 ld_rows1 ld_w0 ld_w1 gathered0 gathered1
            row_ready xT_psum xT_done gu_psum gate_act hid_done y_psum y_ready y_stored gathered x1_sum pool_waited
            bn3 eps3 rstd_x1 x1_done
            ld_v ld_o ld_k ld_qT ld_q kv_psum kv_out k_squared k_ms k_sqrt k_normed
            x1T_psum x1T_done x_now_ready q_psum q_squared q_eps q_rstd s_psum s_taken s_shifted s_exp s_soft pT_psum pT_done
            attn_psum attn_taken
            bn4 eps4 rstd_x2 x2_done
            ld_idx ld_down gathered_w0 gathered_w1 iota_done counted spread_psum spread_done pool_chain quantised wT_psum wT_done
            x_quant xT8_psum xT8_done ff_psum ff_read ff_gate ff_in t_scaled t_in_ready t_size_ready x_scaled x_size_ready
            t_done t_psum tT_done y2_psum y2_read y_scaled
            attn_chain ff_chain bn5 eps5 rstd_out out_done stored""".split()
        s = {n: sem(n) for n in names}

        block = ctx.enter_context(nc.Block())
        HID_BUFS = 3

        @block.sync
        def _(sp):
            def load(dst, src, signal):
                sp.dma_start(dst, src).then_inc(s[signal], 16)
            load(x[:, :, :], inp["x"].rearrange("b s d -> (b s) d").rearrange("(i p) d -> p i d", p=P), "ld_x")
            load(w_in[:, :, :], inp["w_in"], "ld_win")
            load(cols[:, :], inp["cols"], "ld_small")
            load(gather_at[:, :], inp["down_at"], "ld_idx")
            load(up_row.bitcast(I32), inp["up_index"].partition_broadcast(P), "ld_idx")
            load(down_row.bitcast(I32), inp["down_index"].partition_broadcast(P), "ld_idx")
            load(bc_ln[:, :], inp["bc_ln"], "ld_small")
            load(lane[:, :, :], inp["lane"], "ld_small")
            load(w_x[:, :, :], inp["w_x"], "ld_wx")
            load(w_dt[:, :], inp["w_dt"], "ld_wd")
            load(w_out[:, :, :], inp["w_out"], "ld_wo")
            load(w_raw[2], inp["w_down"], "ld_down")
            load(w_router[:, :, :], inp["w_router"], "ld_small")
            load(ln_ff_row[:, :], inp["ln_ff"].partition_broadcast(P), "ld_lnff")
            sp.wait_ge(s["zero_set"], 1)
            load(moe_in.rearrange("(i p) d -> p i d", p=P), zero[:, :].unsqueeze(1).to_broadcast([P, IN_TILES, D]), "moe_zeroed")
            load(moe_out.rearrange("(i p) d -> p i d", p=P), zero[:, :].unsqueeze(1).to_broadcast([P, OUT_TILES, D]), "moe_zeroed")

            def load_weights(e):
                sp.dma_start(w_moe[e % 2], inp["w_moe"][e]).then_inc(s[f"ld_w{e % 2}"], 16)

            def load_rows(e):
                first = sp.value_load(bounds[0:1, e:e + 1], min_val=0, max_val=OUT_TILES - 1)
                sp.dma_start(x_rows[e % 2], moe_in[bass.ds(first * P, TILES * P), :].rearrange("(i p) d -> p i d", p=P))\
                    .then_inc(s[f"ld_rows{e % 2}"], 16)

            sp.wait_ge(s["conv_out"], CI)
            load_weights(1)
            sp.wait_ge(s["bc_split"], 2)
            sp.wait_ge(s["dt_psum"], 2 * CI)
            load_weights(0)
            sp.wait_ge(s["scattered"], 2 * TILES * 16)
            load_rows(0)
            load_rows(1)
            load(w_qT, inp["w_qT"], "ld_qT")
            for e in range(E):
                if 1 <= e < E - 1:
                    sp.wait_ge(s["y_stored"], sp.value_load(bounds[0:1, e:e + 1], min_val=1, max_val=OUT_TILES) * 16 + 16)
                    load_weights(e + 1)
                    load_rows(e + 1)
                first = sp.value_load(bounds[0:1, e:e + 1], min_val=0, max_val=OUT_TILES - 1)
                last = sp.value_load(bounds[0:1, e + 1:e + 2], min_val=1, max_val=OUT_TILES)
                with sp.Fori(first, last) as j:
                    sp.wait_ge(s["y_ready"], j + 2)
                    sp.dma_start(moe_out[bass.ds(j * P, P), :], y_row).then_inc(s["y_stored"], 16)
            sp.wait_ge(s["y_ready"], last + 1)
            load(w_q, inp["w_q"], "ld_q")
            o = out.rearrange("b s d -> (b s) d").rearrange("(i p) d -> p i d", p=P)
            for half in range(2):
                tiles = slice(half * TILES // 2, (half + 1) * TILES // 2)
                sp.wait_ge(s["out_done"], (half + 1) * TILES // 2)
                sp.dma_start(o[:, tiles, :], x[:, tiles, :]).then_inc(s["stored"], 16)
            sp.wait_ge(s["stored"], 32)

        @block.gpsimd
        def _(pool):
            pool.memset(ident[:, :], 0.0).then_inc(s["pads"], 1)
            pool.wait_ge(s["pads"], 1)
            pool.affine_select(out=ident[:, :], in_=ident[:, :], compare_op=ALU.not_equal, fill=1.0, base=0,
                               pattern=[[-1, P]], channel_multiplier=1).then_inc(s["consts"], 1)
            pool.memset(zero[:, :], 0.0).then_inc(s["zero_set"], 1)
            pool.memset(ones[:, :], 1.0).then_inc(s["tables"], 1)
            pool.wait_ge(s["tables"], 1)
            pool.affine_select(out=before[:, :], in_=ones[:, :], compare_op=ALU.is_gt, fill=0.0, base=0,
                               pattern=[[1, P]], channel_multiplier=-1).then_inc(s["tables"], 1)
            pool.iota(iota_e[:, :], pattern=[[1, E]], base=0, channel_multiplier=0,
                      allow_small_or_imprecise_dtypes=True).then_inc(s["tables"], 1)
            pool.wait_ge(s["consts"], 1)
            pool.tensor_copy(ident16[:, :], ident[:, :]).then_inc(s["tables"], 1)
            pool.iota(iota_p[:, :], pattern=[[P, FCH]], base=0, channel_multiplier=1,
                      allow_small_or_imprecise_dtypes=True).then_inc(s["iota_done"], 1)
            for k, (shift_by, _) in enumerate(LOG1P):
                pool.memset(shifts[:, k:k + 1], shift_by)
            pool.memset(neg_half[:, :], -0.5).then_inc(s["consts"], 1)
            pool.memset(xpad[:, :, :, 0:TAPS - 1], 0.0).then_inc(s["consts"], 1)
            pool.wait_ge(s["consts"], 2)
            pool.wait_ge(s["ms1"], 1)
            pool.tensor_tensor(rs[:, 0:TILES], ms[:, 0:TILES], neg_half[:, 0:TILES], ALU.pow).then_inc(s["rstd1"], 1)
            pool.memset(dA[:, :, :].rearrange("p k (b t) -> p k b t", b=BATCH)[:, :, :, 0:1], 0.0).then_inc(s["consts"], 1)
            pool.memset(row_of[:, :, :], 0.0).then_inc(s["selectors"], 1)
            for k in range(3):
                pool.wait_ge(s["selectors"], k + 1)
                pool.affine_select(out=row_of[:, :, :], in_=row_of[:, :, :], compare_op=ALU.not_equal, fill=1.0,
                                   base=-2 * NS * k, pattern=[[-1, 2 * NS], [0, P]], channel_multiplier=1)\
                    .then_inc(s["selectors"], 1)
            pool.wait_ge(s["ms2"], 3)
            pool.tensor_tensor(rs[:, TILES:4 * TILES], ms[:, TILES:4 * TILES], neg_half[:, 0:3 * TILES], ALU.pow).then_inc(s["rstd2"], 1)

            pool.wait_ge(s["ld_idx"], 48)
            pool.wait_ge(s["da_ready"], 3 * NS)
            for m, name in enumerate(("w_gate", "w_up")):
                for c in range(FCH):
                    pool.indirect_dma_start(w_raw[m][:, c, :], None, inp[name], bass.IndirectOffsetOnAxis(gather_at[:, c:c + 1].bitcast(U32), 0))\
                        .then_inc(s[f"gathered_w{m}"], 16)
            pool.wait_ge(s["ms3"], 1)
            pool.tensor_tensor(rs[:, 0:TILES], ms[:, 0:TILES], neg_half[:, 0:TILES], ALU.pow).then_inc(s["rstd3"], 1)
            pool.wait_ge(s["slots_done"], 1)
            pool.wait_ge(s["moe_zeroed"], 32)
            pool.wait_ge(s["hn_done"], TILES)
            for k in range(2):
                for i in range(TILES):
                    pool.indirect_dma_start(moe_in[0:OUT_TILES * P, :], bass.IndirectOffsetOnAxis(slot[:, k, i:i + 1], 0), hn[:, i, :], None)\
                        .then_inc(s["scattered"], 16)

            for e in range(E):
                first = pool.value_load(bounds[0:1, e:e + 1], min_val=0, max_val=OUT_TILES - 1)
                tiles = pool.value_load(n_tiles[0:1, e:e + 1], min_val=1, max_val=TILES)
                pool.wait_ge(s[f"ld_rows{e % 2}"], 16 * (e // 2 + 1))
                with pool.Fori(0, tiles) as j:
                    pool.wait_ge(s["xT_psum"], first + j + 1)
                    pool.sem_inc(s["pool_waited"], 1)
                    pool.tensor_copy(row_in, x_rows[e % 2][:, j, :]).then_inc(s["row_ready"], 1)
            total = pool.value_load(bounds[0:1, E:E + 1], min_val=E, max_val=OUT_TILES)
            pool.wait_ge(s["xT_psum"], total + 1)
            pool.sem_inc(s["pool_waited"], 1)
            pool.tensor_copy(row_in, x_rows[(E - 1) % 2][:, 0, :]).then_inc(s["row_ready"], 1)
            pool.wait_ge(s["y_stored"], total * 16 + 16)
            pool.sem_inc(s["pool_waited"], 1)
            for half in range(2):
                for i in range(half * 4, half * 4 + 4):
                    for k in range(2):
                        pool.indirect_dma_start(y_got[k][:, i, :], None, moe_out[:, :], bass.IndirectOffsetOnAxis(slot[:, k, i:i + 1], 0))\
                            .then_inc(s[f"gathered{half}"], 16)

            def rstd(eps, done):
                pool.wait_ge(s[eps], 1)
                pool.tensor_tensor(rs[:, 0:TILES], ms[:, 0:TILES], neg_half[:, 0:TILES], ALU.pow).then_inc(s[done], 1)

            rstd("eps3", "rstd_x1")

            pool.wait_ge(s["x1T_done"], 2)

            def place_tile(i, j):
                pool.wait_ge(s["q_psum"], 4 * i + 12)
                pool.sem_inc(s["pool_waited"], 1)
                for k in range(KD):
                    ins = pool.tensor_copy(x_now[:, j, k, :], x1T[:, k, bass.ts(i, P)])
                ins.then_inc(s["x_now_ready"], 1)

            def query_rstd(i, j):
                pool.wait_ge(s["q_eps"], i + 1)
                pool.sem_inc(s["pool_waited"], 1)
                pool.tensor_tensor(q_rs[:, j, :], q_ms[:, j, :], neg_half[:, 0:HEADS], ALU.pow).then_inc(s["q_rstd"], 1)

            place_tile(0, 0)
            with pool.Fori(0, TILES // 2 - 1) as turn:
                for j in range(2):
                    place_tile(2 * turn + j + 1, (j + 1) % 2)
                    query_rstd(2 * turn + j, j)
            place_tile(TILES - 1, 1)
            query_rstd(TILES - 2, 0)
            query_rstd(TILES - 1, 1)
            rstd("eps4", "rstd_x2")
            pool.wait_ge(s["x2_done"], TILES)
            pool.memset(t_fp8[:, FF:], 0.0).then_inc(s["iota_done"], 1)
            rstd("eps5", "rstd_out")

        @block.scalar
        def _(act):
            act.wait_ge(s["ld_x"], 16)
            for i in range(TILES):
                nc.scalar.activation(xn[:, i, :], x[:, i, :], ACT.Square,
                                     accum_out=ms[:, i:i + 1]).then_inc(s["sumsq1"], 1)
            act.wait_ge(s["ld_small"], 64)
            nc.scalar.activation(a_neg[:, :, :], lane[:, :, LANE_AT["a_log"]:LANE_AT["a_log"] + NS], ACT.Exp).then_inc(s["a_exp"], 1)
            act.wait_ge(s["hs_psum"], 2)
            nc.scalar.activation(hT[:, 1, :], ps[:, 2:4, :].rearrange("p a b -> p (a b)"), ACT.Identity,
                                 scale=cols[:, 1:2]).then_inc(s["hsT"], 1)
            act.wait_ge(s["consts"], 3)
            for n in range(4 * CI):
                c, half = divmod(n, 2)
                act.wait_ge(s["in_psum"], n + 1)
                src = ps[:, 4 + n % 4, :]
                if c < CI:
                    nc.scalar.activation(xpad[:, c, 2 * half:2 * half + 2, TAPS - 1:], src.rearrange("p (b t) -> p b t", b=2),
                                         ACT.Identity).then_inc(s["in_out"], 1)
                else:
                    nc.scalar.activation(zs[:, c - CI, half * HALF:(half + 1) * HALF], src, ACT.Silu).then_inc(s["in_out"], 1)
            for c in range(CI):
                act.wait_ge(s["conv_acc"], c + 1)
                nc.scalar.activation(xc[:, c, :], conv[:, c % 2, :], ACT.Silu,
                                     bias=lane[:, c, LANE_AT["conv_b"]:LANE_AT["conv_b"] + 1]).then_inc(s["conv_out"], 1)
            act.wait_ge(s["xproj_psum"], TILES)
            nc.scalar.activation(xdb[:, :, :].rearrange("p (a b) c -> p a b c", b=2),
                                 ps[:, 0:4, :].rearrange("p a (b c) -> p a b c", b=2)[:, :, :, 0:XP], ACT.Identity).then_inc(s["xdb_sb"], 1)
            for c in range(CI):
                act.wait_ge(s["dt_psum"], 2 * c + 2)
                if c >= 2:
                    act.wait_ge(s["softplus"], c - 1)
                v = ps[:, 4 + 2 * (c % 2):6 + 2 * (c % 2), :].rearrange("p a b -> p (a b)")
                bias = lane[:, c, LANE_AT["dt_b"]:LANE_AT["dt_b"] + 1]
                nc.scalar.activation(rv[:, c % 2, :], v, ACT.Relu, bias=bias).then_inc(s["dt_act"], 1)
                nc.scalar.activation(u[:, c % 2, :], v, ACT.Abs, bias=bias).then_inc(s["dt_act"], 1)
                act.wait_ge(s["dt_act"], 3 * c + 2)
                nc.scalar.activation(u[:, c % 2, :], u[:, c % 2, :], ACT.Exp, scale=-1.0).then_inc(s["dt_act"], 1)
                act.wait_ge(s["dt_act"], 3 * c + 3)
                act.wait_ge(s["consts"], 2)
                for k in range(len(LOG1P)):
                    if c:
                        act.wait_ge(s["factor_taken"], (c - 1) * len(LOG1P) + k + 1)
                    nc.scalar.activation(squares[k], u[:, c % 2, :], ACT.Square, bias=shifts[:, k:k + 1]).then_inc(s["square_ready"], 1)
            act.wait_ge(s["a_ready"], 1)
            act.wait_ge(s["consts"], 4)
            act.wait_ge(s["softplus"], CI)
            dt_b = dt[:, :, :].rearrange("p c (b t) -> p c b t", b=BATCH)
            dA_b = dA[:, :, :].rearrange("p k (b t) -> p k b t", b=BATCH)
            with act.Fori(0, CI) as c:
                for n in range(NS):
                    unit = c * NS + n
                    act.wait_ge(s["scan_done"], unit + 1)
                    nc.scalar.activation(dA_b[:, n % 2, :, 1:], dt_b[:, c, :, 1:], ACT.Exp,
                                         scale=a_neg[:, c, n:n + 1]).then_inc(s["da_ready"], 1)

            act.wait_ge(s["out_psum"], TILES)
            act.dma_start(ctxT, inp["ctxT"]).then_inc(s["ld_v"], 16)
            act.dma_start(w_v, inp["w_v"]).then_inc(s["ld_v"], 16)
            act.dma_start(w_o, inp["w_o"]).then_inc(s["ld_o"], 16)
            act.wait_ge(s["res_done"], 4)
            for i in range(TILES):
                nc.scalar.activation(hn[:, i, :], res[:, i, :], ACT.Square, accum_out=ms[:, i:i + 1]).then_inc(s["sumsq3"], 1)
            act.wait_ge(s["hn_psum"], KD)
            nc.scalar.activation(hfT[:, 1, :], ps[:, 6:8, :].rearrange("p a b -> p (a b)"), ACT.Identity).then_inc(s["hfT_done"], 1)
            act.wait_ge(s["logit_sub"], 1)
            nc.scalar.activation(prob[:, :, :], logit[:, :, :], ACT.Exp).then_inc(s["logit_exp"], 1)
            step = 0
            for n in range(PAIRS):
                act.wait_ge(s["kv_psum"], step + 1)
                nc.scalar.activation(vT[:, 2 * n:2 * n + 2, :], ps[:, 2 + step % 6, :].rearrange("p (a b) -> p a b", a=2), ACT.Identity).then_inc(s["kv_out"], 1)
                step += 1
            for n in range(2 * PAIRS):
                act.wait_ge(s["kv_psum"], step + 1)
                nc.scalar.activation(vw[:, n // 2, 2 * (n % 2):2 * (n % 2) + 2, :], ps[:, 2 + step % 6, :].rearrange("p (a b) -> p a b", a=2),
                                     ACT.Identity).then_inc(s["kv_out"], 1)
                step += 1
                if n == 0:
                    act.dma_start(w_k, inp["w_k"]).then_inc(s["ld_k"], 16)

            act.wait_ge(s["slots_done"], 1)
            total = act.value_load(bounds[0:1, E:E + 1], min_val=E, max_val=OUT_TILES)
            with act.Fori(0, total) as j:
                for q in range(FCH // 2):
                    act.wait_ge(s["gu_psum"], j * (FCH // 2) + q + 1)
                    act.wait_ge(s["hid_done"], j * (FCH // 2) + q + 1)
                    nc.scalar.activation(act_g3[:, q, :], ps[:, 2 * q, 0:2 * P], ACT.Silu).then_inc(s["gate_act"], 1)

            for n in range(8):
                act.wait_ge(s["kv_psum"], step + 1)
                bank = 2 + step % 6
                at = (n % 4) * HALF
                nc.scalar.activation(k_raw[:, n // 4, at:at + HALF], ps[:, bank, :], ACT.Identity).then_inc(s["k_squared"], 1)
                for hd in range(4):
                    one = slice(at + hd * DH, at + (hd + 1) * DH)
                    ins = nc.scalar.activation(k_junk[:, n // 4, one], ps[:, bank, hd * DH:(hd + 1) * DH], ACT.Square,
                                               scale=float(DH) ** -0.5, accum_out=k_ms[:, 4 * n + hd:4 * n + hd + 1])
                ins.then_inc(s["kv_out"], 1)
                step += 1
            act.wait_ge(s["k_ms"], 1)
            nc.scalar.activation(k_rs[:, :], k_ms[:, :], ACT.Sqrt).then_inc(s["k_sqrt"], 1)
            for n in range(PAIRS):
                act.wait_ge(s["kv_psum"], step + 1)
                nc.scalar.activation(kT[:, 2 * n:2 * n + 2, :], ps[:, 2 + step % 6, :].rearrange("p (a b) -> p a b", a=2), ACT.Identity,
                                     scale=gqk[:, 0:1]).then_inc(s["kv_out"], 1)
                step += 1
            for n in range(KD * PAIRS):
                act.wait_ge(s["kv_psum"], step + 1)
                pair = n // KD
                nc.scalar.activation(qk[n % KD][:, :, 2 * pair:2 * pair + 2, :].rearrange("p b h t -> p h b t"),
                                     ps[:, 2 + step % 6, :].rearrange("p (h b t) -> p h b t", h=2, b=BATCH), ACT.Identity).then_inc(s["kv_out"], 1)
                step += 1

            act.wait_ge(s["x1T_psum"], 2)
            nc.scalar.activation(x1T[:, 1, :], ps[:, 2:4, :].rearrange("p a b -> p (a b)"), ACT.Identity).then_inc(s["x1T_done"], 1)
            def mean_squares(i, j):
                for g in range(4):
                    act.wait_ge(s["q_psum"], 4 * i + g + 17)
                    act.wait_ge(s["q_squared"], 4 * i + g + 1)
                    if g == 0:
                        act.wait_ge(s["q_rstd"], i + 1)
                    for hd in range(4):
                        ins = nc.scalar.activation(q_junk[:, g % 2, hd * DH:(hd + 1) * DH], ps[:, g % 2, hd * DH:(hd + 1) * DH], ACT.Square,
                                                   scale=float(DH) ** -0.5, accum_out=q_ms[:, j, 4 * g + hd:4 * g + hd + 1])
                    ins.then_inc(s["q_squared"], 1)

            def exponential(i, j):
                act.wait_ge(s["s_shifted"], i + 1)
                nc.scalar.activation(shift[:, j, :, :], shift[:, j, :, :], ACT.Exp).then_inc(s["s_exp"], 1)

            def take_transposed_probs(i, j):
                act.wait_ge(s["attn_psum"], i + 1)
                for half in range(2):
                    act.wait_ge(s["pT_psum"], 2 * i + half + 5)
                    nc.scalar.activation(pT[:, j, 4 * half:4 * half + 4, :], ps[:, 4 + half, :].rearrange("p (a b) -> p a b", b=P),
                                         ACT.Identity).then_inc(s["pT_done"], 1)

            mean_squares(0, 0)
            with act.Fori(0, TILES // 2 - 1) as turn:
                for j in range(2):
                    exponential(2 * turn + j, j)
                    mean_squares(2 * turn + j + 1, (j + 1) % 2)
                    take_transposed_probs(2 * turn + j, j)
            exponential(TILES - 2, 0)
            mean_squares(TILES - 1, 1)
            take_transposed_probs(TILES - 2, 0)
            exponential(TILES - 1, 1)
            take_transposed_probs(TILES - 1, 1)
            for half in range(2):
                tiles = slice(4 * half, 4 * half + 4)
                act.wait_ge(s["x_scaled"], 4 * half + 4)
                nc.scalar.activation(x_size[:, tiles, :], x_in[:, tiles, :], ACT.Abs, scale=ROUND_AT).then_inc(s["x_size_ready"], 1)
            act.wait_ge(s["xT8_psum"], 2)
            nc.scalar.activation(qxT[:, 1, :], ps[:, 2, :].bitcast(BF16), ACT.Identity).then_inc(s["xT8_done"], 1)
            def gate_of(i, j):
                act.wait_ge(s["ff_in"], i + 1)
                nc.scalar.activation(gate_s[:, j, :], gate_s[:, j, :], ACT.Silu, scale=xscale[:, bass.ds(i, 1)]).then_inc(s["ff_gate"], 1)

            def scale_row(i):
                act.wait_ge(s["t_scaled"], i + 1)
                nc.scalar.activation(t_in, prod, ACT.Identity, scale=tinv[:, 0:1]).then_inc(s["t_in_ready"], 1)
                act.wait_ge(s["t_in_ready"], i + 1)
                nc.scalar.activation(t_size, t_in, ACT.Abs, scale=ROUND_AT).then_inc(s["t_size_ready"], 1)

            def take_hidden(i):
                act.wait_ge(s["t_psum"], i + 2)
                act.wait_ge(s["y2_psum"], i + 1)
                nc.scalar.activation(t_fp8T, ps[:, 4, 0:FPAD // 2].bitcast(BF16).rearrange("p (a b) -> p a b", b=P), ACT.Identity).then_inc(s["tT_done"], 1)

            gate_of(0, 0)
            scale_row(0)
            gate_of(1, 1)
            take_hidden(0)
            with act.Fori(0, TILES // 2 - 1) as turn:
                for j in range(1, 3):
                    scale_row(2 * turn + j)
                    gate_of(2 * turn + j + 1, (j + 1) % 2)
                    take_hidden(2 * turn + j)
            scale_row(TILES - 1)
            take_hidden(TILES - 1)

        @block.vector
        def _(dve):
            chain = [0]

            def link(ins):
                chain[0] += 1
                ins.then_inc(s["dve_chain"], 1)
                dve.wait_ge(s["dve_chain"], chain[0])



            for name, credit in (("scan_done", 2), ("y_summed", 2), ("hc_done", 2), ("y_drained", 1)):
                dve.sem_inc(s[name], credit)
            dve.wait_ge(s["sumsq1"], TILES)
            nc.vector.tensor_scalar(ms[:, 0:TILES], ms[:, 0:TILES], 1.0 / D, 1e-6, ALU.mult, ALU.add).then_inc(s["ms1"], 1)
            dve.wait_ge(s["rstd1"], 1)
            for i in range(TILES):
                nc.vector.tensor_scalar(xn[:, i, :], x[:, i, :], rs[:, i:i + 1], None, ALU.mult).then_inc(s["xn"], 1)
            dve.wait_ge(s["a_exp"], 1)
            nc.vector.tensor_scalar(a_neg[:, :, :], a_neg[:, :, :], -1.0, None, ALU.mult).then_inc(s["a_ready"], 1)
            dve.wait_ge(s["hs_psum"], 1)
            dve.wait_ge(s["ld_small"], 64)
            nc.vector.tensor_scalar(hT[:, 0, :], ps[:, 0:2, :].rearrange("p a b -> p (a b)"), cols[:, 0:1], None, ALU.mult).then_inc(s["hsT"], 1)
            dve.wait_ge(s["ld_idx"], 48)
            dve.wait_ge(s["iota_done"], 1)
            for row_i, width, col, chunks in ((up_row, D, up_col, KD), (down_row, FF, down_col, FCH)):
                link(nc.vector.tensor_copy(row_i, row_i.bitcast(I32)))
                for c in range(chunks):
                    link(nc.vector.tensor_scalar(compared[:, 0:width], row_i, iota_p[:, c:c + 1], None, ALU.is_equal))
                    link(nc.vector.tensor_reduce(col[:, c:c + 1], compared[:, 0:width], axis=AX.X, op=ALU.add))

            def diagonals(dst, col, chunks):
                return nc.vector.tensor_tensor(dst, ident[:, :].unsqueeze(1).to_broadcast([P, chunks, P]),
                                               col.unsqueeze(2).to_broadcast([P, chunks, P]), ALU.mult)

            dve.wait_ge(s["consts"], 1)
            diagonals(up_diag, up_col[:, :], KD).then_inc(s["counted"], 1)
            diagonals(down_diag, down_col[:, :], FCH).then_inc(s["counted"], 1)
            for c in range(CI):
                dve.wait_ge(s["in_out"], 2 * c + 2)
                if c >= 2:
                    dve.wait_ge(s["conv_out"], c - 1)
                acc = conv[:, c % 2, :].rearrange("p (b t) -> p b t", b=BATCH)
                tap = lambda k: lane[:, c, LANE_AT["conv_w"] + k:LANE_AT["conv_w"] + k + 1]
                link(nc.vector.tensor_scalar(acc, xpad[:, c, :, 0:SEQ], tap(0), None, ALU.mult))
                for k in range(1, TAPS):
                    ins = nc.vector.scalar_tensor_tensor(acc, xpad[:, c, :, k:k + SEQ], tap(k), acc, ALU.mult, ALU.add)
                    if k < TAPS - 1:
                        link(ins)
                    else:
                        ins.then_inc(s["conv_acc"], 1)
            dve.wait_ge(s["spread_psum"], 2)
            nc.vector.tensor_scalar(up_mask[:, :], ps[:, 2, 0:D], 1.0, None, ALU.min).then_inc(s["spread_done"], 1)
            nc.vector.tensor_scalar(down_mask, ps[:, 0:2, :].rearrange("p a b -> p (a b)")[:, 0:FPAD], 1.0, None, ALU.min).then_inc(s["spread_done"], 1)
            dve.wait_ge(s["spread_done"], 2)

            def quantise(m):
                mask, chunks, width = ((up_mask[:, :], FCH, D), (up_mask[:, :], FCH, D), (down_mask[:, 0:FF], KD, FF))[m]
                w, size = w_raw[m], w_size[m][:, 0:chunks * width].rearrange("p (a b) -> p a b", b=width)
                largest, inverse, scale = (v[:, m, 0:chunks] for v in (w_max, w_inv, w_scale))
                dve.wait_ge(*((s["gathered_w0"], FCH * 16), (s["gathered_w1"], FCH * 16), (s["ld_down"], 16))[m])
                link(nc.vector.tensor_tensor(w, w, mask.unsqueeze(1).to_broadcast([P, chunks, width]), ALU.mult))
                link(nc.vector.tensor_reduce(largest, w, axis=AX.X, op=ALU.max, apply_absolute_value=True))
                link(nc.vector.tensor_scalar(scale, largest, 1.0 / FP8_MAX, None, ALU.mult))
                link(nc.vector.reciprocal(inverse, scale))
                for c in range(chunks):
                    ins = nc.vector.tensor_scalar(w[:, c, :], w[:, c, :], inverse[:, c:c + 1], None, ALU.mult)
                link(ins)
                link(nc.vector.tensor_scalar(size.bitcast(I32), w.bitcast(I32), NOT_SIGN, None, ALU.bitwise_and))
                link(nc.vector.tensor_scalar(size, size, ROUND_AT, LEAST_ADDED, ALU.mult, ALU.max))
                link(nc.vector.tensor_tensor(w, w, size, ALU.add))
                link(nc.vector.tensor_tensor(w_fp8[m][:, :, 0:width], size, w, ALU.subtract))
                if m == 2:
                    link(nc.vector.memset(w_fp8[m][:, :, FF:], 0.0))
                dve.sem_inc(s["quantised"], 1)

            quantise(2)
            dve.wait_ge(s["xdb_sb"], 1)
            sq = junk
            link(nc.vector.tensor_tensor(sq, xdb[:, :, :], xdb[:, :, :], ALU.mult))
            groups = ((0, DR), (DR, NS), (DR + NS, NS))
            for g, (at, width) in enumerate(groups):
                dst = ms[:, (g + 1) * TILES:(g + 2) * TILES]
                link(nc.vector.tensor_reduce(dst, sq[:, :, at:at + width], axis=AX.X, op=ALU.add))
                nc.vector.tensor_scalar(dst, dst, 1.0 / width, 1e-6, ALU.mult, ALU.add).then_inc(s["ms2"], 1)
            dve.wait_ge(s["rstd2"], 1)
            for g, (at, width) in enumerate(groups):
                part = xdb[:, :, at:at + width]
                rstd = rs[:, (g + 1) * TILES:(g + 2) * TILES].unsqueeze(2).to_broadcast([P, TILES, width])
                nc.vector.tensor_tensor(part, part, rstd, ALU.mult).then_inc(s["xdbn"], 1)
            dve.wait_ge(s["dtn_psum"], 1)
            nc.vector.tensor_scalar(dtnT, ps[:, 0:2, :].rearrange("p a b -> p (a b)"), cols[:, 2:3], None, ALU.mult).then_inc(s["dtn_sb"], 1)
            dve.wait_ge(s["bc_psum"], 1)
            R = 2 * NS
            link(nc.vector.tensor_scalar(bcf, ps[0:R, 2:4, :].rearrange("p a b -> p (a b)"), bc_ln[:, 0:1], None, ALU.mult))
            link(nc.vector.tensor_copy(bc3[0:R, :], bcf))
            link(nc.vector.tensor_tensor(bc_rest, bcf, bc3[0:R, :], ALU.subtract))
            link(nc.vector.tensor_copy(bc_mid, bc_rest))
            nc.vector.tensor_copy(bc3[R:2 * R, :], bc_mid).then_inc(s["bc_split"], 1)
            nc.vector.tensor_tensor(bc3[2 * R:3 * R, :], bc_rest, bc_mid, ALU.subtract).then_inc(s["bc_split"], 1)
            for c in range(CI):
                dve.wait_ge(s["dt_act"], 3 * c + 3)
                acc = dt[:, c, :]
                for k, (_, add) in enumerate(LOG1P):
                    dve.wait_ge(s["square_ready"], c * len(LOG1P) + k + 1)
                    nc.vector.scalar_tensor_tensor(acc, squares[k], add, acc if k else u[:, c % 2, :], ALU.add, ALU.mult).then_inc(s["factor_taken"], 1)
                    dve.wait_ge(s["factor_taken"], c * len(LOG1P) + k + 1)
                nc.vector.scalar_tensor_tensor(acc, acc, LOG1P_SCALE, rv[:, c % 2, :], ALU.mult, ALU.add).then_inc(s["softplus"], 1)
                dve.wait_ge(s["softplus"], c + 1)
                dve.wait_ge(s["conv_out"], c + 1)
                link(nc.vector.tensor_tensor(dtx[:, c, :], acc, xc[:, c, :], ALU.mult))
            pB = ps[:, 0:2, :].rearrange("p a b -> p (a b)")
            pC = ps[:, 2:4, :].rearrange("p a b -> p (a b)")
            pY = ps[:, 4:6, :].rearrange("p a b -> p (a b)")

            def input_of(c, n):
                unit = c * NS + n
                dve.wait_ge(s["b_ready"], unit + 1)
                dve.wait_ge(s["scan_done"], unit + 1)
                nc.vector.tensor_tensor(dBx[:, n % 2, :], dtx[:, c, :], pB, ALU.mult).then_inc(s["dbx_done"], 1)

            def scan_of(c, n):
                unit = c * NS + n
                dve.wait_ge(s["da_ready"], unit + 1)
                dve.wait_ge(s["dbx_done"], unit + 1)
                dve.wait_ge(s["hc_done"], unit + 1)
                nc.vector.tensor_tensor_scan(h[:, n % 2, :], dA[:, n % 2, :], dBx[:, n % 2, :], 0.0, ALU.mult, ALU.add).then_inc(s["scan_done"], 1)

            def output_of(c, n):
                unit = c * NS + n
                dve.wait_ge(s["c_ready"], unit + 1)
                dve.wait_ge(s["scan_done"], unit + 3)
                dve.wait_ge(s["y_summed"], unit + 1)
                nc.vector.tensor_tensor(hC[:, n % 2, :], h[:, n % 2, :], pC, ALU.mult).then_inc(s["hc_done"], 1)

            def add_skip(c):
                dve.wait_ge(s["y_summed"], (c + 1) * NS + 2)
                dve.wait_ge(s["dbx_done"], (c + 1) * NS)
                nc.vector.scalar_tensor_tensor(dtx[:, c, :], xc[:, c, :], lane[:, c, LANE_AT["d_param"]:LANE_AT["d_param"] + 1],
                                               pY, ALU.mult, ALU.add).then_inc(s["y_drained"], 1)

            def times_gate(c):
                dve.wait_ge(s["y_drained"], c + 2)
                nc.vector.tensor_tensor(dtx[:, c, :], dtx[:, c, :], zs[:, c, :], ALU.mult).then_inc(s["ym_done"], 1)

            def chunk(c, before):
                input_of(c, 0)
                for n in range(NS):
                    scan_of(c, n)
                    if n < NS - 1:
                        input_of(c, n + 1)
                    if n == 0 and before is not None:
                        add_skip(before)
                    output_of(c, n)
                    if n == 1 and before is not None:
                        times_gate(before)

            chunk(0, None)
            with dve.Fori(0, CI - 1) as c:
                chunk(c + 1, c)
            add_skip(CI - 1)
            times_gate(CI - 1)
            quantise(0)
            for q in range(4):
                dve.wait_ge(s["out_psum"], 2 * q + 2)
                nc.vector.tensor_tensor(res[:, 2 * q:2 * q + 2, :], x[:, 2 * q:2 * q + 2, :],
                                        ps[:, q, :].rearrange("p (a b) -> p a b", b=D), ALU.add).then_inc(s["res_done"], 1)
            dve.wait_ge(s["sumsq3"], TILES)
            nc.vector.tensor_scalar(ms[:, 0:TILES], ms[:, 0:TILES], 1.0 / D, 1e-6, ALU.mult, ALU.add).then_inc(s["ms3"], 1)
            dve.wait_ge(s["rstd3"], 1)
            dve.wait_ge(s["ld_lnff"], 16)
            for i in range(TILES):
                nc.vector.scalar_tensor_tensor(hn[:, i, :], res[:, i, :], rs[:, i:i + 1], ln_ff_row[:, :], ALU.mult, ALU.mult).then_inc(s["hn_done"], 1)
            dve.wait_ge(s["hn_psum"], 1)
            nc.vector.tensor_copy(hfT[:, 0, :], ps[:, 4:6, :].rearrange("p a b -> p (a b)")).then_inc(s["hfT_done"], 1)
            stat_of = lambda k, n=E: stat[:, k, :].unsqueeze(2).to_broadcast([P, TILES, n])
            dve.wait_ge(s["logit_psum"], 1)
            link(nc.vector.tensor_copy(logit[:, :, :], ps[:, 0, 0:TILES * E].rearrange("p (i e) -> p i e", e=E)))
            link(nc.vector.tensor_reduce(stat[:, 0, :], logit[:, :, :], axis=AX.X, op=ALU.max))
            nc.vector.tensor_tensor(logit[:, :, :], logit[:, :, :], stat_of(0), ALU.subtract).then_inc(s["logit_sub"], 1)
            dve.wait_ge(s["logit_exp"], 1)
            link(nc.vector.tensor_reduce(stat[:, 1, :], prob[:, :, :], axis=AX.X, op=ALU.add))
            link(nc.vector.reciprocal(stat[:, 2, :], stat[:, 1, :]))
            link(nc.vector.tensor_tensor(prob[:, :, :], prob[:, :, :], stat_of(2), ALU.mult))
            for i in range(TILES):
                ins = nc.vector.max(best[:, i, :], prob[:, i, :])
            link(ins)
            for i in range(TILES):
                ins = nc.vector.max_index(best_at[:, i, :], best[:, i, :], prob[:, i, :])
            link(ins)
            link(nc.vector.tensor_copy(best_f[:, :, :], best_at[:, :, :]))
            dve.wait_ge(s["tables"], 3)
            for k in range(2):
                nc.vector.tensor_tensor(picked[k][:, :, :], iota_e[:, :].unsqueeze(1).to_broadcast([P, TILES, E]),
                                        best_f[:, :, k:k + 1].to_broadcast([P, TILES, E]), ALU.is_equal).then_inc(s["picked_done"], 1)
            dve.wait_ge(s["picked_done"], 2)
            link(nc.vector.tensor_tensor(both[:, :, :], picked[0][:, :, :], picked[1][:, :, :], ALU.add))
            link(nc.vector.memset(earlier[:, 0, :], 0.0))
            for i in range(1, TILES):
                ins = nc.vector.tensor_tensor(earlier[:, i, :], earlier[:, i - 1, :], both[:, i - 1, :], ALU.add)
                if i < TILES - 1:
                    link(ins)
            ins.then_inc(s["picked_done"], 1)
            dve.wait_ge(s["prefix_psum"], 1)
            link(nc.vector.tensor_scalar(count_i[:, :], ps[:, 1, 0:E], float(P - 1), None, ALU.add))
            link(nc.vector.tensor_scalar(count_i[:, :], count_i[:, :], 7, None, ALU.logical_shift_right))
            link(nc.vector.tensor_scalar(count[:, 0, :], count_i[:, :], 1.0, None, ALU.max))
            link(nc.vector.tensor_tensor_scan(count[:, 1, :], ones[:, 0:E], count[:, 0, :], 0.0, ALU.mult, ALU.add))
            link(nc.vector.tensor_copy(n_tiles[:, :], count[:, 0, :]))
            link(nc.vector.memset(bounds[:, 0:1], 0))
            link(nc.vector.tensor_copy(bounds[:, 1:E + 1], count[:, 1, :]))
            link(nc.vector.tensor_tensor(count[:, 2, :], count[:, 1, :], count[:, 0, :], ALU.subtract))
            link(nc.vector.tensor_scalar(count[:, 3, :], count[:, 2, :], float(P), None, ALU.mult))
            link(nc.vector.tensor_tensor(place[:, :, :], ps[:, 1, E:E + TILES * E].rearrange("p (i e) -> p i e", e=E),
                                         count[:, 3, :].unsqueeze(1).to_broadcast([P, TILES, E]), ALU.add))
            for k in range(2):
                link(nc.vector.tensor_tensor(picked[k][:, :, :], picked[k][:, :, :], place[:, :, :], ALU.mult))
                link(nc.vector.tensor_reduce(slot_f[:, k, :], picked[k][:, :, :], axis=AX.X, op=ALU.add))
            nc.vector.tensor_copy(slot[:, :, :], slot_f[:, :, :]).then_inc(s["slots_done"], 1)
            link(nc.vector.tensor_tensor(gqk[:, :], cols[:, 5:6], cols[:, 6:7], ALU.mult))
            link(nc.vector.tensor_scalar(gqk[:, :], gqk[:, :], float(DH) ** -0.5, None, ALU.mult))
            quantise(1)
            dve.wait_ge(s["quantised"], 3)
            link(nc.vector.tensor_scalar(down_one[:, :], down_col[:, :], 1.0, None, ALU.min))
            link(nc.vector.tensor_tensor(w_scale[:, 1, :], w_scale[:, 1, :], down_one[:, :], ALU.mult))
            flat_banks = ps[:, 0:2, :].rearrange("p a b -> p (a b)")
            for m in range(3):
                for half in range(2):
                    dve.wait_ge(s["wT_psum"], 2 * m + half + 1)
                    src = ps[:, half, 0:FPAD // 2].bitcast(BF16)
                    if m < 2:
                        ins = nc.vector.tensor_scalar(w_fp8T[m][:, half, :], src, up_col[:, half:half + 1], None, ALU.mult)
                    else:
                        three = slice(3 * half, 3 * half + 3)
                        ins = nc.vector.tensor_tensor(w_fp8T[m][:, three, :], src.rearrange("p (a b) -> p a b", b=D),
                                                      down_col[:, three].unsqueeze(2).to_broadcast([P, 3, D]), ALU.mult)
                    ins.then_inc(s["wT_done"], 1)
            for m, chunks in enumerate((FCH, FCH, KD)):
                diagonals(diag[:, 0:chunks, :], w_scale[:, m, 0:chunks], chunks).then_inc(s["counted"], 1)
                dve.wait_ge(s["spread_psum"], m + 3)
                nc.vector.tensor_copy(scale_rows[m], flat_banks[:, 0:chunks * P]).then_inc(s["spread_done"], 1)
                dve.wait_ge(s["spread_done"], m + 3)
            dve.wait_ge(s["slots_done"], 1)
            dve.sem_inc(s["hid_done"], HID_BUFS)
            dve.sem_inc(s["xT_psum"], 1)
            dve.sem_inc(s["y_psum"], 1)
            dve.sem_inc(s["y_ready"], 1)
            dve.sem_inc(s["y_stored"], 16)
            dve.sem_inc(s["xT_done"], 1)
            total = dve.value_load(bounds[0:1, E:E + 1], min_val=E, max_val=OUT_TILES)

            def take_transposed(tile):
                dve.wait_ge(s["xT_psum"], tile + 2)
                nc.vector.tensor_copy(xT, ps[:, 7, 0:D].rearrange("p (k n) -> p k n", k=KD)).then_inc(s["xT_done"], 1)

            take_transposed(0)
            with dve.Fori(0, total) as j:
                for q in range(FCH // 2):
                    dve.wait_ge(s["gate_act"], j * (FCH // 2) + q + 1)
                    dve.wait_ge(s["y_psum"], j + 1)
                    nc.vector.tensor_tensor(hid[:, 2 * q:2 * q + 2, :], act_g3[:, q, :].rearrange("p (a b) -> p a b", b=P),
                                            ps[:, 2 * q + 1, 0:2 * P].rearrange("p (a b) -> p a b", b=P), ALU.mult).then_inc(s["hid_done"], 1)
                take_transposed(j + 1)
                dve.wait_ge(s["y_psum"], j + 2)
                dve.wait_ge(s["y_stored"], j * 16 + 16)
                nc.vector.tensor_copy(y_row, ps[:, 6, 0:D]).then_inc(s["y_ready"], 1)
            dve.wait_ge(s["kv_out"], 3 * PAIRS + 8)
            nc.vector.tensor_scalar(k_ms[:, :], k_ms[:, :], 1e-5, None, ALU.add).then_inc(s["k_ms"], 1)
            dve.wait_ge(s["k_sqrt"], 1)
            link(nc.vector.reciprocal(k_rs[:, :], k_rs[:, :]))
            for j in range(2):
                k_heads = k_raw[:, j, :].rearrange("p (h d) -> p h d", d=DH)
                nc.vector.tensor_tensor(k_heads, k_heads, k_rs[:, j * HEADS:(j + 1) * HEADS].unsqueeze(2).to_broadcast([P, HEADS, DH]),
                                        ALU.mult).then_inc(s["k_normed"], 1)
            for half in range(2):
                dve.wait_ge(s[f"gathered{half}"], TILES * 16)
                tiles = range(half * 4, half * 4 + 4)
                for k in range(2):
                    for n, i in enumerate(tiles):
                        if k:
                            dve.wait_ge(s["x1_sum"], half * TILES + n + 1)
                        nc.vector.scalar_tensor_tensor(x[:, i, :], y_got[k][:, i, :], best[:, i, k:k + 1], x[:, i, :], ALU.mult, ALU.add).then_inc(s["x1_sum"], 1)
                for n, i in enumerate(tiles):
                    dve.wait_ge(s["x1_sum"], half * TILES + n + 5)
                    nc.vector.bn_stats(bn[:, i, :], x[:, i, :]).then_inc(s["bn3"], 1)

            def layernorm(stats, eps, rstd, done):
                dve.wait_ge(s[stats], TILES)
                for i in range(TILES):
                    ins = nc.vector.bn_aggr(mv[:, i, :], bn[:, i, :])
                link(ins)
                nc.vector.tensor_scalar(ms[:, 0:TILES], mv[:, :, 1:2].rearrange("p a b -> p (a b)"), 1e-5, None, ALU.add).then_inc(s[eps], 1)
                dve.wait_ge(s[rstd], 1)
                for i in range(TILES):
                    nc.vector.tensor_scalar(x[:, i, :], x[:, i, :], mv[:, i, 0:1], rs[:, i:i + 1], ALU.subtract, ALU.mult).then_inc(s[done], 1)

            layernorm("bn3", "eps3", "rstd_x1", "x1_done")

            for name, credit in (("q_psum", 16), ("q_squared", 2), ("q_rstd", 2), ("s_taken", 1), ("s_soft", 2),
                                 ("pT_psum", 4), ("pT_done", 2), ("attn_psum", 2), ("attn_taken", 2)):
                dve.sem_inc(s[name], credit)
            dve.wait_ge(s["x1T_psum"], 1)
            nc.vector.tensor_copy(x1T[:, 0, :], ps[:, 0:2, :].rearrange("p a b -> p (a b)")).then_inc(s["x1T_done"], 1)

            over = lambda t, j: t[:, j, :].unsqueeze(2).to_broadcast([P, HEADS, KV])
            scores = ps[:, 2:4, :].rearrange("p a (h t) -> p (a h) t", t=KV)

            def softmax(i, j):
                def link_tile(ins, n):
                    ins.then_inc(s["attn_chain"], 1)
                    dve.wait_ge(s["attn_chain"], 3 * i + n)
                dve.wait_ge(s["s_psum"], i + 1)
                link_tile(nc.vector.tensor_reduce(top[:, j, :], scores, axis=AX.X, op=ALU.max), 1)
                dve.wait_ge(s["s_soft"], i + 1)
                nc.vector.tensor_tensor(shift[:, j, :, :], scores, over(top, j), ALU.subtract).then_inc(s["s_taken"], 1)
                dve.wait_ge(s["q_squared"], 4 * i + 6)
                nc.vector.tensor_scalar(q_ms[:, j, :], q_ms[:, j, :], 1e-5, None, ALU.add).then_inc(s["q_eps"], 1)
                dve.wait_ge(s["s_taken"], i + 2)
                dve.wait_ge(s["q_rstd"], i + 3)
                nc.vector.tensor_tensor(shift[:, j, :, :], shift[:, j, :, :], over(q_rs, j), ALU.mult).then_inc(s["s_shifted"], 1)
                dve.wait_ge(s["s_exp"], i + 1)
                link_tile(nc.vector.tensor_reduce(total_e[:, j, :], shift[:, j, :, :], axis=AX.X, op=ALU.add), 2)
                link_tile(nc.vector.reciprocal(total_e[:, j, :], total_e[:, j, :]), 3)
                dve.wait_ge(s["pT_psum"], 2 * i + 2)
                nc.vector.tensor_tensor(soft[:, j, :, :], shift[:, j, :, :], over(total_e, j), ALU.mult).then_inc(s["s_soft"], 1)

            def add_attention(i, j):
                dve.wait_ge(s["attn_psum"], i + 3)
                nc.vector.tensor_tensor(x[:, bass.ds(i, 1), :], x[:, bass.ds(i, 1), :], ps[:, 6 + j, 0:D].unsqueeze(1), ALU.add).then_inc(s["attn_taken"], 1)
                dve.wait_ge(s["attn_taken"], i + 3)
                nc.vector.bn_stats(bn[:, bass.ds(i, 1), :].rearrange("p a b -> p (a b)"), x[:, bass.ds(i, 1), :].rearrange("p a b -> p (a b)")).then_inc(s["bn4"], 1)

            softmax(0, 0)
            with dve.Fori(0, TILES // 2 - 1) as turn:
                for j in range(2):
                    softmax(2 * turn + j + 1, (j + 1) % 2)
                    add_attention(2 * turn + j, j)
            softmax(TILES - 1, 1)
            add_attention(TILES - 2, 0)
            add_attention(TILES - 1, 1)

            layernorm("bn4", "eps4", "rstd_x2", "x2_done")
            dve.wait_ge(s["x2_done"], TILES)
            link(nc.vector.tensor_tensor(x_in, x[:, :, :], up_mask[:, :].unsqueeze(1).to_broadcast([P, TILES, D]), ALU.mult))
            link(nc.vector.tensor_reduce(xmax[:, :], x_in, axis=AX.X, op=ALU.max, apply_absolute_value=True))
            link(nc.vector.tensor_scalar(xscale[:, :], xmax[:, :], 1.0 / FP8_MAX, None, ALU.mult))
            link(nc.vector.reciprocal(xinv[:, :], xscale[:, :]))
            for i in range(TILES):
                nc.vector.tensor_scalar(x_in[:, i, :], x_in[:, i, :], xinv[:, i:i + 1], None, ALU.mult).then_inc(s["x_scaled"], 1)
            for half in range(2):
                tiles = slice(4 * half, 4 * half + 4)
                dve.wait_ge(s["x_size_ready"], half + 1)
                link(nc.vector.scalar_tensor_tensor(x_in[:, tiles, :], x_size[:, tiles, :], LEAST_ADDED, x_in[:, tiles, :], ALU.max, ALU.add))
                nc.vector.scalar_tensor_tensor(qx[:, tiles, :], x_size[:, tiles, :], LEAST_ADDED, x_in[:, tiles, :], ALU.max, ALU.subtract).then_inc(s["x_quant"], 1)
            for name in ("ff_read", "t_psum", "tT_done", "y2_psum", "y2_read"):
                dve.sem_inc(s[name], 1)
            dve.wait_ge(s["xT8_psum"], 1)
            nc.vector.tensor_copy(qxT[:, 0, :], ps[:, 0, :].bitcast(BF16)).then_inc(s["xT8_done"], 1)
            in_two = lambda v: v[:, 0:FF].rearrange("p (a b) -> p a b", a=2)

            def link_ff(ins, i, n):
                ins.then_inc(s["ff_chain"], 1)
                dve.wait_ge(s["ff_chain"], 4 * i + n)

            def take_gate_and_up(i, j):
                dve.wait_ge(s["ff_psum"], i + 1)
                nc.vector.tensor_tensor(in_two(gate_s[:, j, :]), ps[:, 0:2, 0:FF // 2], in_two(scale_rows[0]), ALU.mult).then_inc(s["ff_in"], 1)
                nc.vector.scalar_tensor_tensor(in_two(up_s[:, j, :]), ps[:, 2:4, 0:FF // 2], xscale[:, bass.ds(i, 1)], in_two(scale_rows[1]),
                                               ALU.mult, ALU.mult).then_inc(s["ff_read"], 1)

            def hidden(i, j):
                dve.wait_ge(s["ff_gate"], i + 1)
                dve.wait_ge(s["ff_read"], i + 2)
                link_ff(nc.vector.tensor_tensor(prod, gate_s[:, j, :], up_s[:, j, :], ALU.mult), i, 1)
                link_ff(nc.vector.tensor_reduce(tmax[:, :], prod, axis=AX.X, op=ALU.max, apply_absolute_value=True), i, 2)
                link_ff(nc.vector.tensor_scalar(tscale[:, j:j + 1], tmax[:, :], 1.0 / FP8_MAX, None, ALU.mult), i, 3)
                nc.vector.reciprocal(tinv[:, :], tscale[:, j:j + 1]).then_inc(s["t_scaled"], 1)

            def round_hidden(i):
                dve.wait_ge(s["t_size_ready"], i + 1)
                link_ff(nc.vector.scalar_tensor_tensor(t_in, t_size, LEAST_ADDED, t_in, ALU.max, ALU.add), i, 4)
                dve.wait_ge(s["t_psum"], i + 1)
                nc.vector.scalar_tensor_tensor(t_fp8[:, 0:FF], t_size, LEAST_ADDED, t_in, ALU.max, ALU.subtract).then_inc(s["t_done"], 1)

            def take_result(i, j):
                dve.wait_ge(s["y2_psum"], i + 2)
                dve.wait_ge(s["y2_read"], i + 1)
                nc.vector.scalar_tensor_tensor(y_s, ps[:, 5, 0:D], tscale[:, j:j + 1], scale_rows[2], ALU.mult, ALU.mult).then_inc(s["y_scaled"], 1)
                dve.wait_ge(s["y_scaled"], i + 1)
                nc.vector.tensor_tensor(x[:, bass.ds(i, 1), :], x[:, bass.ds(i, 1), :], y_s.unsqueeze(1), ALU.add).then_inc(s["y2_read"], 1)
                dve.wait_ge(s["y2_read"], i + 2)
                nc.vector.bn_stats(bn[:, bass.ds(i, 1), :].rearrange("p a b -> p (a b)"), x[:, bass.ds(i, 1), :].rearrange("p a b -> p (a b)")).then_inc(s["bn5"], 1)

            take_gate_and_up(0, 0)
            hidden(0, 0)
            take_gate_and_up(1, 1)
            round_hidden(0)
            with dve.Fori(0, TILES // 2 - 1) as turn:
                for j in range(1, 3):
                    hidden(2 * turn + j, j % 2)
                    take_gate_and_up(2 * turn + j + 1, (j + 1) % 2)
                    take_result(2 * turn + j - 1, (j - 1) % 2)
                    round_hidden(2 * turn + j)
            hidden(TILES - 1, 1)
            take_result(TILES - 2, 0)
            round_hidden(TILES - 1)
            take_result(TILES - 1, 1)
            layernorm("bn5", "eps5", "rstd_out", "out_done")

        @block.tensor
        def _(pe):
            pe.wait_ge(s["consts"], 1)
            for k in range(KD):
                for i in range(TILES):
                    if k == 0:
                        pe.wait_ge(s["xn"], i + 1)
                    ins = nc.tensor.transpose(ps[:, 2 * k + i // 4, (i % 4) * P:(i % 4 + 1) * P],
                                              xn[:, i, k * P:(k + 1) * P], ident[:, :])
                ins.then_inc(s["hs_psum"], 1)
            pe.wait_ge(s["ld_win"], 16)
            pe.wait_ge(s["hsT"], 2)
            for n in range(4 * CI):
                c, half = divmod(n, 2)
                if n >= 4:
                    pe.wait_ge(s["in_out"], n - 3)
                for k in range(KD):
                    ins = nc.tensor.matmul(ps[:, 4 + n % 4, :], w_in[:, k, c * P:(c + 1) * P], hT[:, k, half * HALF:(half + 1) * HALF],
                                           start=(k == 0), stop=(k == KD - 1))
                ins.then_inc(s["in_psum"], 1)
            pe.wait_ge(s["counted"], 2)
            pe.wait_ge(s["tables"], 1)

            def spread_diagonals(diagonals, chunks, bank):
                for at in range(0, chunks, 4):
                    n = min(4, chunks - at)
                    ins = nc.tensor.matmul(ps[:, bank + at // 4, 0:n * P], ones[:, :], diagonals[:, at:at + n, :].rearrange("p a b -> p (a b)"), start=True, stop=True)
                ins.then_inc(s["spread_psum"], 1)

            spread_diagonals(up_diag, KD, 2)
            spread_diagonals(down_diag, FCH, 0)
            pe.wait_ge(s["spread_done"], 2)
            pe.wait_ge(s["ld_wx"], 16)
            pe.wait_ge(s["conv_out"], CI)
            for i in range(TILES):
                for c in range(CI):
                    ins = nc.tensor.matmul(ps[:, i // 2, (i % 2) * D:(i % 2) * D + XP], xc[:, c, i * P:(i + 1) * P], w_x[:, c, :],
                                           start=(c == 0), stop=(c == CI - 1))
                ins.then_inc(s["xproj_psum"], 1)
            pe.wait_ge(s["xdbn"], 1)
            for i in range(TILES):
                ins = nc.tensor.transpose(ps[:, i // 4, (i % 4) * P:(i % 4 + 1) * P], xdb[:, i, 0:DR], ident[:, :])
            ins.then_inc(s["dtn_psum"], 1)
            pe.wait_ge(s["xdbn"], 3)
            for i in range(TILES):
                ins = nc.tensor.transpose(ps[0:2 * NS, 2 + i // 4, (i % 4) * P:(i % 4 + 1) * P], xdb[:, i, DR:XP], ident[:, :])
            ins.then_inc(s["bc_psum"], 1)
            pe.wait_ge(s["ld_wd"], 16)
            pe.wait_ge(s["dtn_sb"], 1)
            pe.wait_ge(s["in_out"], 4 * CI)
            for c in range(CI):
                if c >= 2:
                    pe.wait_ge(s["dt_act"], 3 * (c - 2) + 2)
                for half in range(2):
                    nc.tensor.matmul(ps[:, 4 + 2 * (c % 2) + half, :], w_dt[:, c * P:(c + 1) * P], dtnT[:, half * HALF:(half + 1) * HALF],
                                     start=True, stop=True).then_inc(s["dt_psum"], 1)
            pe.wait_ge(s["selectors"], 4)
            pe.wait_ge(s["bc_split"], 2)
            pe.wait_ge(s["dt_act"], 3 * CI)

            def spread(bank, row, ready):
                for half in range(2):
                    ins = nc.tensor.matmul(ps[:, bank + half, :], row_of[:, row, :], bc3[:, half * HALF:(half + 1) * HALF],
                                           start=True, stop=True)
                ins.then_inc(s[ready], 1)

            def sum_states(n):
                for half in range(2):
                    ins = nc.tensor.matmul(ps[:, 4 + half, :], ident[:, :], hC[:, n % 2, half * HALF:(half + 1) * HALF],
                                           start=(n == 0), stop=(n == NS - 1))
                ins.then_inc(s["y_summed"], 1)

            spread(0, 0, "b_ready")
            with pe.Fori(0, CI) as c:
                for n in range(NS):
                    unit = c * NS + n
                    pe.wait_ge(s["dbx_done"], unit + 1)
                    spread(0, (n + 1) % NS, "b_ready")
                    pe.wait_ge(s["hc_done"], unit + 2)
                    spread(2, NS + n, "c_ready")
                    if n == 1:
                        pe.wait_ge(s["y_drained"], c + 1)
                    if n:
                        sum_states(n - 1)
                pe.wait_ge(s["hc_done"], (c + 1) * NS + 2)
                sum_states(NS - 1)
            pe.wait_ge(s["ld_wo"], 16)
            pe.wait_ge(s["ym_done"], CI)
            for i in range(TILES):
                for c in range(CI):
                    ins = nc.tensor.matmul(ps[:, i // 2, (i % 2) * D:(i % 2 + 1) * D], dtx[:, c, i * P:(i + 1) * P], w_out[:, c, :],
                                           start=(c == 0), stop=(c == CI - 1))
                ins.then_inc(s["out_psum"], 1)
            for k in range(KD):
                for i in range(TILES):
                    if k == 0:
                        pe.wait_ge(s["hn_done"], i + 1)
                    ins = nc.tensor.transpose(ps[:, 4 + 2 * k + i // 4, (i % 4) * P:(i % 4 + 1) * P], hn[:, i, k * P:(k + 1) * P], ident[:, :])
                ins.then_inc(s["hn_psum"], 1)
            pe.wait_ge(s["hfT_done"], KD)
            pe.wait_ge(s["res_done"], 1)
            pe.wait_ge(s["ld_small"], 64)
            for i in range(TILES):
                for k in range(KD):
                    ins = nc.tensor.matmul(ps[:, 0, i * E:(i + 1) * E], hfT[:, k, i * P:(i + 1) * P], w_router[:, k, :],
                                           start=(k == 0), stop=(k == KD - 1))
            ins.then_inc(s["logit_psum"], 1)
            pe.wait_ge(s["tables"], 3)
            pe.wait_ge(s["picked_done"], 3)
            nc.tensor.matmul(ps[:, 1, 0:E], ones[:, :], earlier[:, TILES - 1, :], start=True, stop=False)
            nc.tensor.matmul(ps[:, 1, 0:E], ones[:, :], both[:, TILES - 1, :], start=False, stop=True)
            flat = lambda t: t[:, :, :].rearrange("p i e -> p (i e)")
            nc.tensor.matmul(ps[:, 1, E:E + TILES * E], ones[:, :], flat(earlier), start=True, stop=False)
            nc.tensor.matmul(ps[:, 1, E:E + TILES * E], before[:, :], flat(both), start=False, stop=True).then_inc(s["prefix_psum"], 1)
            kv = [0]

            def kv_bank():
                if kv[0] >= 6:
                    pe.wait_ge(s["kv_out"], kv[0] - 5)
                kv[0] += 1
                return 2 + (kv[0] - 1) % 6

            pe.wait_ge(s["hfT_done"], KD)
            pe.wait_ge(s["ld_v"], 32)
            for n in range(PAIRS):
                bank = kv_bank()
                for hd in range(2):
                    ins = nc.tensor.matmul(ps[:, bank, hd * KVT:(hd + 1) * KVT], w_v[:, (2 * n + hd) * DH:(2 * n + hd + 1) * DH], ctxT, start=True, stop=True)
                ins.then_inc(s["kv_psum"], 1)

            def transpose_fp8(m):
                pe.wait_ge(s["quantised"], (2, 3, 1)[m])
                pe.wait_ge(s["tables"], 4)
                pe.wait_ge(s["slots_done"], 1)
                if m:
                    pe.wait_ge(s["wT_done"], 2 * m)
                for half in range(2):
                    for n in range(FCH):
                        src = w_fp8[m][:, n, half * P:(half + 1) * P] if m < 2 else w_fp8[m][:, n % KD, (3 * half + n // KD) * P:(3 * half + n // KD + 1) * P]
                        ins = nc.tensor.transpose(ps[:, half, n * P // 2:(n + 1) * P // 2].bitcast(BF16), src, ident16[:, :])
                    ins.then_inc(s["wT_psum"], 1)

            pe.wait_ge(s["ld_o"], 16)
            for n in range(2 * PAIRS):
                bank = kv_bank()
                if n % 2 == 0:
                    pe.wait_ge(s["kv_out"], n // 2 + 1)
                for b in range(2 * (n % 2), 2 * (n % 2) + 2):
                    for hd in range(2):
                        ins = nc.tensor.matmul(ps[hd * KV:(hd + 1) * KV, bank, (b % 2) * D:(b % 2 + 1) * D], vT[:, 2 * (n // 2) + hd, b * KV:(b + 1) * KV],
                                               w_o[:, 2 * (n // 2) + hd, :], start=True, stop=True)
                ins.then_inc(s["kv_psum"], 1)
                if n in (3, 9, 11):
                    transpose_fp8((0, 1, 2)[(3, 9, 11).index(n)])
                elif n in (13, 14, 15):
                    m = n - 13
                    pe.wait_ge(s["counted"], 3 + m)
                    pe.wait_ge(s["wT_done"], 6)
                    if m:
                        pe.wait_ge(s["spread_done"], 2 + m)
                    spread_diagonals(diag, (FCH, FCH, KD)[m], 0)
            pe.wait_ge(s["kv_out"], kv[0])
            pe.wait_ge(s["slots_done"], 1)

            def transpose_rows(tile):
                pe.wait_ge(s["row_ready"], tile + 1)
                pe.wait_ge(s["xT_done"], tile + 1)
                for k in range(KD):
                    ins = nc.tensor.transpose(ps[:, 7, k * P:(k + 1) * P], row_in[:, k * P:(k + 1) * P], ident[:, :])
                ins.then_inc(s["xT_psum"], 1)

            transpose_rows(0)
            for e in range(E):
                w1, w3, w2 = (w_moe[e % 2][:, k * FCH * D:(k + 1) * FCH * D].rearrange("p (k n) -> p k n", k=kk) for k, kk in ((0, KD), (1, KD), (2, FCH)))
                first = pe.value_load(bounds[0:1, e:e + 1], min_val=0, max_val=OUT_TILES - 1)
                last = pe.value_load(bounds[0:1, e + 1:e + 2], min_val=1, max_val=OUT_TILES)
                pe.wait_ge(s[f"ld_w{e % 2}"], 16 * (e // 2 + 1))
                with pe.Fori(first, last) as j:
                    pe.wait_ge(s["xT_done"], j + 2)
                    for q in range(FCH // 2):
                        pe.wait_ge(s["hid_done"], j * (FCH // 2) + q + 1)
                        for w, bank in ((w1, 2 * q), (w3, 2 * q + 1)):
                            for c in range(2):
                                for k in range(KD):
                                    at = (2 * q + c) * P
                                    ins = nc.tensor.matmul(ps[:, bank, c * P:(c + 1) * P], w[:, k, at:at + P], xT[:, k, :],
                                                           start=(k == 0), stop=(k == KD - 1))
                        ins.then_inc(s["gu_psum"], 1)
                    transpose_rows(j + 1)
                    pe.wait_ge(s["y_ready"], j + 1)
                    for c in range(FCH):
                        if c % 2 == 0:
                            pe.wait_ge(s["hid_done"], (j + 1) * (FCH // 2) + c // 2 + 1)
                        ins = nc.tensor.matmul(ps[:, 6, 0:D], hid[:, c, :], w2[:, c, :], start=(c == 0), stop=(c == FCH - 1))
                    ins.then_inc(s["y_psum"], 1)
            pe.wait_ge(s["y_ready"], last + 1)
            pe.wait_ge(s["xT_done"], last + 2)
            pe.wait_ge(s["ld_k"], 16)
            for n in range(8):
                bank = kv_bank()
                ins = nc.tensor.matmul(ps[:, bank, :], ctxT[:, (n // 4) * P:(n // 4 + 1) * P], w_k[:, (n % 4) * HALF:(n % 4 + 1) * HALF], start=True, stop=True)
                ins.then_inc(s["kv_psum"], 1)
            pe.wait_ge(s["k_normed"], 2)
            for n in range(PAIRS):
                bank = kv_bank()
                for hd in range(2):
                    for j in range(2):
                        at = (2 * n + hd) * DH
                        ins = nc.tensor.transpose(ps[:, bank, hd * KVT + j * P:hd * KVT + (j + 1) * P], k_raw[:, j, at:at + DH], ident[:, :])
                ins.then_inc(s["kv_psum"], 1)
            pe.wait_ge(s["ld_qT"], 16)
            for n in range(KD * PAIRS):
                bank = kv_bank()
                pair, k = divmod(n, KD)
                pe.wait_ge(s["kv_out"], 3 * PAIRS + 9 + pair)
                for hd in range(2):
                    ins = nc.tensor.matmul(ps[:, bank, hd * KVT:(hd + 1) * KVT], w_qT[:, 2 * pair + hd, k * P:(k + 1) * P], kT[:, 2 * pair + hd, :],
                                           start=True, stop=True)
                ins.then_inc(s["kv_psum"], 1)
            pe.wait_ge(s["kv_out"], kv[0])
            for i in range(TILES):
                pe.wait_ge(s["x1_done"], i + 1)
                for k in range(KD):
                    ins = nc.tensor.transpose(ps[:, 2 * k + i // 4, (i % 4) * P:(i % 4 + 1) * P], x[:, i, k * P:(k + 1) * P], ident[:, :])
                    if i == TILES - 1:
                        ins.then_inc(s["x1T_psum"], 1)
            pe.wait_ge(s["x1T_done"], 2)
            pe.wait_ge(s["ld_q"], 16)

            def scores_of(i, j, b):
                pe.wait_ge(s["x_now_ready"], i + 1)
                pe.wait_ge(s["s_taken"], i + 1)
                for half in range(2):
                    for k in range(KD):
                        ins = nc.tensor.matmul(ps[:, 2 + half, :], x_now[:, j, k, :],
                                               qk[k].rearrange("p b h t -> p b (h t)")[:, b, half * HALF:(half + 1) * HALF],
                                               start=(k == 0), stop=(k == KD - 1))
                ins.then_inc(s["s_psum"], 1)

            def queries_of(i, j):
                for g in range(4):
                    pe.wait_ge(s["q_squared"], 4 * i + g + 1)
                    for k in range(KD):
                        ins = nc.tensor.matmul(ps[:, g % 2, :], x_now[:, j, k, :], w_q[:, k, g * HALF:(g + 1) * HALF],
                                               start=(k == 0), stop=(k == KD - 1))
                    ins.then_inc(s["q_psum"], 1)

            def values_of(i, j, b):
                pe.wait_ge(s["s_soft"], i + 3)
                for half in range(2):
                    pe.wait_ge(s["pT_done"], 2 * i + half + 1)
                    for n in range(4):
                        at = 8 * half + 2 * n
                        ins = nc.tensor.transpose(ps[:, 4 + half, n * P:(n + 1) * P], soft[:, j, at:at + 2, :].rearrange("p a b -> p (a b)"), ident[:, :])
                    ins.then_inc(s["pT_psum"], 1)
                pe.wait_ge(s["attn_taken"], i + 1)
                for n in range(PAIRS):
                    if n % 4 == 0:
                        pe.wait_ge(s["pT_done"], 2 * i + n // 4 + 3)
                    ins = nc.tensor.matmul(ps[:, 6 + j, 0:D], pT[:, j, n, :], vw[:, n, b, :], start=(n == 0), stop=(n == PAIRS - 1))
                ins.then_inc(s["attn_psum"], 1)

            scores_of(0, 0, 0)
            queries_of(0, 0)
            with pe.Fori(0, TILES // 2 - 1) as turn:
                for j in range(2):
                    scores_of(2 * turn + j + 1, (j + 1) % 2, turn + (j + 1) // 2)
                    queries_of(2 * turn + j + 1, (j + 1) % 2)
                    values_of(2 * turn + j, j, turn)
            scores_of(TILES - 1, 1, BATCH - 1)
            queries_of(TILES - 1, 1)
            values_of(TILES - 2, 0, BATCH - 1)
            values_of(TILES - 1, 1, BATCH - 1)
            pe.wait_ge(s["x_quant"], 2)
            for k in range(KD):
                for i in range(TILES):
                    ins = nc.tensor.transpose(ps[:, 2 * k, i * P // 2:(i + 1) * P // 2].bitcast(BF16), qx[:, i, k * P:(k + 1) * P], ident16[:, :])
                ins.then_inc(s["xT8_psum"], 1)
            pe.wait_ge(s["xT8_done"], 2)

            def gate_and_up(i):
                pe.wait_ge(s["ff_read"], i + 1)
                for m in range(2):
                    for part in range(2):
                        for k in range(KD):
                            ins = nc.tensor.matmul(ps[:, 2 * m + part, 0:FF // 2], qxT[:, k, bass.ts(i, P)], w_fp8T[m][:, k, part * FF // 2:(part + 1) * FF // 2],
                                                   start=(k == 0), stop=(k == KD - 1))
                ins.then_inc(s["ff_psum"], 1)

            def down(i):
                pe.wait_ge(s["t_done"], i + 1)
                pe.wait_ge(s["tT_done"], i + 1)
                for c in range(FCH):
                    ins = nc.tensor.transpose(ps[:, 4, c * P // 2:(c + 1) * P // 2].bitcast(BF16), t_fp8[:, c * P:(c + 1) * P], ident16[:, :])
                ins.then_inc(s["t_psum"], 1)
                pe.wait_ge(s["tT_done"], i + 2)
                pe.wait_ge(s["y2_read"], i + 1)
                for c in range(FCH):
                    ins = nc.tensor.matmul(ps[:, 5, 0:D], t_fp8T[:, c, :], w_fp8T[2][:, c, :], start=(c == 0), stop=(c == FCH - 1))
                ins.then_inc(s["y2_psum"], 1)

            pe.wait_ge(s["iota_done"], 2)
            gate_and_up(0)
            gate_and_up(1)
            with pe.Fori(0, TILES - 2) as i:
                gate_and_up(i + 2)
                down(i)
            down(TILES - 2)
            down(TILES - 1)


def kernel(**inputs):
    import concourse.bacc as bacc
    from concourse.bass_utils import run_bass_kernel_spmd

    def a(name):
        return np.asarray(inputs["L0_attn_" + name])

    def xa(name):
        return np.asarray(inputs["L0_xattn_" + name])

    def ff(name):
        return np.asarray(inputs["L0_ffn_" + name])

    def chunked(w):
        return w.reshape(-1, P, w.shape[1]).transpose(1, 0, 2)

    def index(v):
        return v.view(np.int32)[::2] if v.dtype.itemsize == 8 else v.view(np.int32)

    w_moe = np.zeros((E, P, MOE_W), np.float32)
    for e in range(E):
        for k, name in enumerate(("w1", "w3")):
            at = k * KD * FPAD
            w_moe[e, :, at:at + KD * FPAD].reshape(P, KD, FPAD)[:, :, :FF] = chunked(a(name)[e].T)
        w2 = np.zeros((FPAD, D), np.float32)
        w2[:FF] = a("w2")[e].T
        w_moe[e, :, 2 * KD * FPAD:] = chunked(w2).reshape(P, -1)
    up, down = index(ff("up_reorder_index")), index(ff("down_reorder_index"))
    down_at = np.zeros(FPAD, np.int32)
    down_at[:FF] = down
    lane = [a("conv_w"), a("conv_b")[:, None], a("dt_proj_b")[:, None], a("D_param")[:, None], a("A_log")]
    cols = [chunked(a("ln_in_w")[:, None])[:, :, 0], a("dt_ln_w")[:, None], chunked(a("ln_ff_w")[:, None])[:, :, 0],
            xa("gq")[:, None], xa("gk")[:, None]]
    data = dict(
        x=np.asarray(inputs["x"]), w_in=chunked(a("in_proj_w").T), cols=np.concatenate(cols, 1),
        bc_ln=np.concatenate([a("b_ln_w"), a("c_ln_w")])[:, None], lane=chunked(np.concatenate(lane, 1)),
        w_x=chunked(a("x_proj_w").T), w_dt=a("dt_proj_w").T, w_out=chunked(a("out_proj_w").T), ln_ff=a("ln_ff_w")[None],
        w_router=chunked(a("router_w").T), w_moe=w_moe, ctxT=np.asarray(inputs["ctx_1024"]).reshape(KVT, CTX).T,
        w_q=chunked(xa("Wq")), w_qT=xa("Wq").T.reshape(HEADS, DH, D).transpose(1, 0, 2), w_k=xa("Wk"), w_v=xa("Wv"), w_o=chunked(xa("Wo")),
        w_gate=ff("w_gate"), w_up=ff("w_up"), w_down=chunked(ff("w_down")),
        up_index=up[None], down_index=down[None], down_at=down_at.reshape(FCH, P).T)
    nc = bacc.Bacc("TRN2", target_bir_lowering=False, num_devices=1)
    arrays, inp = {}, {}
    for name, v in data.items():
        v = np.ascontiguousarray(v)
        arrays["in_" + name] = v
        inp[name] = nc.dram_tensor("in_" + name, v.shape, I32 if v.dtype == np.int32 else F32, kind="ExternalInput").ap()
    out = nc.dram_tensor("out", (BATCH, SEQ, D), F32, kind="ExternalOutput").ap()
    build(nc, inp, out)
    return run_bass_kernel_spmd(nc, [arrays], core_ids=[0]).results[0]["out"]
```

```python
from contextlib import ExitStack

import numpy as np

import concourse.bass as bass
from concourse import mybir

F32, BF16 = mybir.dt.float32, mybir.dt.bfloat16
I32, U32 = mybir.dt.int32, mybir.dt.uint32
ALU, ACT, AX = mybir.AluOpType, mybir.ActivationFunctionType, mybir.AxisListType

P = 128
BATCH, SEQ, D = 4, 256, 256
T = BATCH * SEQ
TILES = T // P
KD = D // P
HALF = 512
DI, NS, DR, TAPS = 512, 16, 128, 4
CI = DI // P
XP = DR + 2 * NS
LANES = (("conv_w", TAPS), ("conv_b", 1), ("dt_b", 1), ("d_param", 1), ("a_log", NS))
E, FF = 8, 704
FCH = -(-FF // P)
MOE_W = 3 * FCH * D
OUT_TILES = 2 * TILES + E - 1
IN_TILES = OUT_TILES + 2
HEADS, DH, KV, CTX = 16, 128, 64, 128
PAIRS = HEADS // 2
KVT = BATCH * KV
FPAD = FCH * P
FP8_MAX = 448.0
ROUND_AT = 2.0 ** 20
LEAST_ADDED = 1.5 * 2.0 ** 14
NOT_SIGN = 0x7FFFFFFF
ARENA_KB = 181
LANE_AT = {}
for _name, _n in LANES:
    LANE_AT[_name] = sum(n for _, n in LANES[:len(LANE_AT)])
LANE_W = sum(n for _, n in LANES)
LOG1P = ((-2.3201779192559524, 0.4319853169731413), (-1.423605531584339, 2.6994923737791177),
         (-0.08170957446752569, 3.254352199747658), (1.0093947016519729, 1.104990747000989))
LOG1P_SCALE = 0.0052534577981952985


def build(nc, inp, out):
    with ExitStack() as ctx:
        def sb(name, shape, dt=F32):
            return ctx.enter_context(nc.sbuf_tensor(name, shape, dt))

        def sem(name):
            return ctx.enter_context(nc.semaphore(name))

        arena = sb("arena", [P, ARENA_KB * 256])

        def view(at_kb, shape, dt=F32, rows=P):
            size = int(np.prod(shape)) * (2 if dt == BF16 else 4)
            assert at_kb * 1024 + size <= ARENA_KB * 1024 and size % 4 == 0
            at = int(at_kb * 256)
            v = arena[0:rows, at:at + size // 4]
            if dt != F32:
                v = v.bitcast(dt)
            dims = ["a", "b", "c"][:len(shape)]
            if len(shape) > 1:
                v = v.rearrange(f"p ({' '.join(dims)}) -> p {' '.join(dims)}", **dict(zip(dims[1:], shape[1:])))
            return v

        x = sb("x", [P, TILES, D])
        cols = sb("cols", [P, 7])
        bc_ln = sb("bc_ln", [2 * NS, 1])
        lane = sb("lane", [P, CI, LANE_W])
        a_neg = sb("a_neg", [P, CI, NS])
        ident = sb("ident", [P, P])
        ones = sb("ones", [P, P])
        before = sb("before", [P, P])
        ln_ff_row = sb("ln_ff_row", [P, D])
        zero = sb("zero", [P, D])
        neg_half = sb("neg_half", [P, P])
        shifts = sb("shifts", [P, len(LOG1P)])
        ms = sb("ms", [P, P])
        rs = sb("rs", [P, P])
        xpad = view(0, [CI, BATCH, SEQ + TAPS - 1])
        u, rv = view(0, [2, T]), view(8, [2, T])
        w_in, hT, conv = view(16.5, [KD, 2 * DI]), view(24.5, [KD, T]), view(32.5, [2, T])
        zs, xc, dt, dtx = (view(40.5 + 16 * k, [CI, T]) for k in range(4))
        xdb, junk = view(163, [TILES, XP]), view(168, [TILES, XP])
        dBx, h = view(0, [2, T]), view(8, [2, T])
        c_copy = view(104.5, [2, T])
        dtnT = view(173, [T])
        bcf, bc_rest = view(177, [T], rows=2 * NS), view(104.5, [T], rows=2 * NS)
        bc_mid, bc3 = view(108.5, [T], BF16, rows=2 * NS), view(128.5, [T], BF16, rows=96)
        hC, dA = view(130.5, [2, T]), view(138.5, [2, T])
        squares = [view(at, [T]) for at in (119.5, 123.5, 130.5, 134.5)]
        xn = view(130.5, [TILES, D])
        w_x, w_dt, w_out = view(146.5, [CI, XP]), view(149, [DI]), view(151, [CI, D])
        row_of = view(155, [2 * NS, P], BF16, rows=96)
        w_moe = [view(163, [MOE_W]), view(16.5, [MOE_W])]
        res, hn = view(0, [TILES, D]), view(8, [TILES, D])

        hfT = view(56.5, [KD, T])
        row_in, xT, hid = view(64.5, [D]), view(65.5, [KD, P]), view(66.5, [FCH, P])
        act_g3, y_row = view(69.5, [3, 2 * P]), view(72.5, [D])
        y_got = [view(163, [TILES, D]), view(171, [TILES, D])]
        w_router = sb("w_router", [P, KD, E])
        logit = sb("logit", [P, TILES, E])
        prob = sb("prob", [P, TILES, E])
        best = sb("best", [P, TILES, 8])
        best_at = sb("best_at", [P, TILES, 8], U32)
        best_f = sb("best_f", [P, TILES, 8])
        picked = [sb(f"picked{k}", [P, TILES, E]) for k in range(2)]
        both = sb("both", [P, TILES, E])
        earlier = sb("earlier", [P, TILES, E])
        iota_e = sb("iota_e", [P, E])
        place = sb("place", [P, TILES, E])
        stat = sb("stat", [P, 4, TILES])
        count = sb("count", [P, 4, E])
        count_i = sb("count_i", [P, E], I32)

        bounds = sb("bounds", [P, E + 1], I32)
        slot_f = sb("slot_f", [P, 2, TILES])
        slot = sb("slot", [P, 2, TILES], U32)
        bn = sb("bn", [P, TILES, 6])
        mv = sb("mv", [P, TILES, 2])
        ctxT = view(127.5, [KVT])
        vw = view(90.5, [PAIRS, BATCH, D])
        w_v, vT, w_o = view(119.5, [HEADS * DH]), view(131, [HEADS, KVT]), view(147, [HEADS, D])
        w_k, k_raw, k_sq = view(40.5, [HEADS * DH]), view(131, [2, HEADS * DH]), view(147, [2, HEADS * DH])
        kT = view(147, [HEADS, KVT])
        w_qT, w_q = view(0, [HEADS, D]), view(16.5, [KD, HEADS * DH])
        qk = [view(40.5, [BATCH, HEADS, KV]), view(123, [BATCH, HEADS, KV])]
        x1T, x_now, q_junk = view(147, [KD, T]), view(155, [2, KD, P]), view(157, [2, HALF])
        shift, soft, pT = view(163, [2, HEADS, KV]), view(171, [2, HEADS, KV]), view(0, [2, PAIRS, P])
        gqk = sb("gqk", [P, 1])
        k_ms = sb("k_ms", [P, 2 * HEADS])
        k_rs = sb("k_rs", [P, 2 * HEADS])
        top = sb("top", [P, 2, HEADS])
        q_ms = sb("q_ms", [P, 2, HEADS])
        q_rs = sb("q_rs", [P, 2, HEADS])
        total_e = sb("total_e", [P, 2, HEADS])
        up_row, down_row = view(96, [D]), view(97, [FF])
        up_equal, down_equal = view(104.5, [KD, D]), view(106.5, [FCH, FF])
        down_diag, up_diag = view(90, [FCH, P]), view(93, [KD, P])
        up_mask, down_mask = sb("up_mask", [P, D]), view(96, [FPAD])
        w_raw = [view(72.5, [FCH, D]), view(78.5, [FCH, D]), view(84.5, [KD, FF])]
        w_size = [view(66.5, [FCH * D]), view(66.5, [FCH * D]), view(90, [KD * FF])]
        w_fp8 = [view(34.5, [FCH, D], BF16), view(37.5, [FCH, D], BF16), view(116.5, [KD, FPAD], BF16)]
        w_fp8T = [view(73.5, [KD, FPAD], BF16), view(76.5, [KD, FPAD], BF16), view(84.5, [FCH, D], BF16)]
        diag = [view(87.5, [FCH, P]), view(66.5, [FCH, P]), view(69.5, [KD, P])]
        scale_rows = [view(56.5, [FPAD]), view(59.5, [FPAD]), view(62.5, [D])]
        x_in, x_size = view(66.5, [2, D]), view(68.5, [2, D])
        qx, qxT = view(32.5, [TILES, D], BF16), view(36.5, [KD, T], BF16)
        gate_s, up_s = view(0, [2, FF]), view(6, [2, FF])
        prod, t_in, t_size = view(12, [FF]), view(15, [FF]), view(18, [FF])
        t_fp8, t_fp8T = view(21, [FPAD], BF16), view(23, [FCH, P], BF16)
        y_s = view(25, [D])
        up_col = sb("up_col", [P, KD])
        down_col = sb("down_col", [P, FCH])
        down_one = sb("down_one", [P, FCH])
        tile_bn = sb("tile_bn", [P, 2, 6])
        tile_var = sb("tile_var", [P, 2])
        tile_rs = sb("tile_rs", [P, 2])
        tile_scale = sb("tile_scale", [P, 2])
        tile_inv = sb("tile_inv", [P, 2])

        iota_p = sb("iota_p", [P, FCH])
        gather_at = sb("gather_at", [P, FCH], I32)
        w_max = sb("w_max", [P, 3, FCH])
        w_inv = sb("w_inv", [P, 3, FCH])
        w_scale = sb("w_scale", [P, 3, FCH])
        xmax = sb("xmax", [P, TILES])
        xinv = sb("xinv", [P, TILES])
        xscale = sb("xscale", [P, TILES])
        tmax = sb("tmax", [P, 1])
        tinv = sb("tinv", [P, 1])
        tscale = sb("tscale", [P, 2])
        ident16 = sb("ident16", [P, P], BF16)
        moe_in = nc.dram_tensor("moe_in", (IN_TILES * P, D), F32).ap()
        moe_out = nc.dram_tensor("moe_out", (OUT_TILES * P, D), F32).ap()
        ps = ctx.enter_context(nc.psum_tensor("ps", [P, 8, HALF], F32))

        names = """ld_x ld_small ld_win ld_wx ld_wd ld_wo consts pads selectors sumsq1 ms1 rstd1
            xn hs_psum hsT in_psum in_out conv_acc conv_out xproj_psum xdb_sb ms2 rstd2 xdbn
            dtn_psum bc_psum dtn_sb dt_psum dt_act softplus square_ready factor_taken a_exp a_ready bc_split bc_float
            rows_float compared indexed dtx_done c_copied b_ready c_ready da_ready dbx_done scan_done hc_done y_summed y_drained ym_done
            out_psum dve_chain ld_lnff tables zero_set moe_zeroed res_done sumsq3 ms3 rstd3 hn_done hn_psum
            hfT_done logit_psum logit_sub logit_exp picked_done prefix_psum slots_done scattered ld_rows ld_w0 ld_w1 gathered0
            gathered1 xT_psum xT_done gu_psum gate_act hid_done y_psum y_ready y_stored x1_sum pool_waited dve_waited
            bn3 eps3 rstd_x1 x1_done ld_v ld_o ld_k ld_qT ld_q kv_psum kv_out k_squared
            k_ms k_sqrt k_normed x1T_psum x1T_done x_now_ready q_psum q_squared q_eps q_rstd s_psum s_taken
            s_shifted s_exp s_soft pT_psum pT_done attn_psum attn_taken eps4 rstd_x2 ld_idx ld_down gathered_w0
            gathered_w1 iota_done counted spread_psum spread_done pool_chain quantised wT_psum wT_done x_quant xT8_psum xT8_done
            ff_psum ff_read ff_gate ff_in t_scaled t_in_ready t_size_ready x2_stats x2_chain prod_done t_done t_psum
            tT_done y2_psum y2_read y_scaled attn_chain ff_chain bn5 eps5 rstd_out out_done stored""".split()
        s = {n: sem(n) for n in names}

        block = ctx.enter_context(nc.Block())
        HID_BUFS = 3
        EARLY = 4

        @block.sync
        def _(sp):
            def load(dst, src, signal):
                sp.dma_start(dst, src).then_inc(s[signal], 16)
            load(x[:, :, :], inp["x"].rearrange("b s d -> (b s) d").rearrange("(i p) d -> p i d", p=P), "ld_x")
            load(w_in[:, :, :], inp["w_in"], "ld_win")
            load(cols[:, :], inp["cols"], "ld_small")
            load(gather_at[:, :], inp["down_at"], "ld_idx")
            load(up_row.bitcast(I32), inp["up_index"].partition_broadcast(P), "ld_idx")
            load(down_row.bitcast(I32), inp["down_index"].partition_broadcast(P), "ld_idx")
            load(bc_ln[:, :], inp["bc_ln"], "ld_small")
            load(lane[:, :, :], inp["lane"], "ld_small")
            load(w_x[:, :, :], inp["w_x"], "ld_wx")
            load(w_dt[:, :], inp["w_dt"], "ld_wd")
            load(w_out[:, :, :], inp["w_out"], "ld_wo")
            load(w_raw[2], inp["w_down"], "ld_down")
            load(w_router[:, :, :], inp["w_router"], "ld_small")
            load(ln_ff_row[:, :], inp["ln_ff"].partition_broadcast(P), "ld_lnff")
            sp.wait_ge(s["zero_set"], 1)
            load(moe_in.rearrange("(i p) d -> p i d", p=P), zero[:, :].unsqueeze(1).to_broadcast([P, IN_TILES, D]), "moe_zeroed")
            load(moe_out.rearrange("(i p) d -> p i d", p=P), zero[:, :].unsqueeze(1).to_broadcast([P, OUT_TILES, D]), "moe_zeroed")

            def load_weights(e):
                sp.dma_start(w_moe[e % 2], inp["w_moe"][e]).then_inc(s[f"ld_w{e % 2}"], 16)

            def load_row_tile(tile):
                sp.dma_start(row_in, moe_in[bass.ds(tile * P, P), :]).then_inc(s["ld_rows"], 16)

            sp.wait_ge(s["conv_out"], CI)
            load_weights(1)
            sp.wait_ge(s["bc_split"], 2)
            sp.wait_ge(s["dt_psum"], 2 * CI)
            load_weights(0)
            sp.wait_ge(s["softplus"], CI)
            load(ctxT, inp["ctxT"], "ld_v")
            load(w_v, inp["w_v"], "ld_v")
            sp.wait_ge(s["scattered"], 2 * TILES * 16)
            sp.dma_start(row_in, moe_in[0:P, :]).then_inc(s["ld_rows"], 16)
            sp.wait_ge(s["xT_psum"], 2)
            sp.dma_start(row_in, moe_in[P:2 * P, :]).then_inc(s["ld_rows"], 16)
            load(w_qT, inp["w_qT"], "ld_qT")
            for e in range(E):
                if 1 <= e < E - 1:
                    load_weights(e + 1)
                first = sp.value_load(bounds[0:1, e:e + 1], min_val=0, max_val=OUT_TILES - 1)
                last = sp.value_load(bounds[0:1, e + 1:e + 2], min_val=1, max_val=OUT_TILES)
                with sp.Fori(first, last) as j:
                    sp.wait_ge(s["xT_psum"], j + 3)
                    load_row_tile(j + 2)
                    sp.wait_ge(s["y_ready"], j + 2)
                    sp.dma_start(moe_out[bass.ds(j * P, P), :], y_row).then_inc(s["y_stored"], 16)
            sp.wait_ge(s["y_ready"], last + 1)
            load(w_q, inp["w_q"], "ld_q")
            o = out.rearrange("b s d -> (b s) d").rearrange("(i p) d -> p i d", p=P)
            for half in range(2):
                tiles = slice(half * TILES // 2, (half + 1) * TILES // 2)
                sp.wait_ge(s["out_done"], (half + 1) * TILES // 2)
                sp.dma_start(o[:, tiles, :], x[:, tiles, :]).then_inc(s["stored"], 16)
            sp.wait_ge(s["stored"], 32)

        @block.gpsimd
        def _(pool):
            pool.memset(ident[:, :], 0.0).then_inc(s["pads"], 1)
            pool.wait_ge(s["pads"], 1)
            pool.affine_select(out=ident[:, :], in_=ident[:, :], compare_op=ALU.not_equal, fill=1.0, base=0,
                               pattern=[[-1, P]], channel_multiplier=1).then_inc(s["consts"], 1)
            pool.memset(zero[:, :], 0.0).then_inc(s["zero_set"], 1)
            pool.memset(ones[:, :], 1.0).then_inc(s["tables"], 1)
            pool.wait_ge(s["tables"], 1)
            pool.affine_select(out=before[:, :], in_=ones[:, :], compare_op=ALU.is_gt, fill=0.0, base=0,
                               pattern=[[1, P]], channel_multiplier=-1).then_inc(s["tables"], 1)
            pool.iota(iota_e[:, :], pattern=[[1, E]], base=0, channel_multiplier=0,
                      allow_small_or_imprecise_dtypes=True).then_inc(s["tables"], 1)
            pool.wait_ge(s["consts"], 1)
            pool.tensor_copy(ident16[:, :], ident[:, :]).then_inc(s["tables"], 1)
            pool.iota(iota_p[:, :], pattern=[[P, FCH]], base=0, channel_multiplier=1,
                      allow_small_or_imprecise_dtypes=True).then_inc(s["iota_done"], 1)
            for k, (shift_by, _) in enumerate(LOG1P):
                pool.memset(shifts[:, k:k + 1], shift_by)
            pool.memset(neg_half[:, :], -0.5).then_inc(s["consts"], 1)
            pool.memset(xpad[:, :, :, 0:TAPS - 1], 0.0).then_inc(s["consts"], 1)
            pool.wait_ge(s["iota_done"], 1)
            pool.wait_ge(s["consts"], 2)
            pool.wait_ge(s["ms1"], 1)
            pool.tensor_tensor(rs[:, 0:TILES], ms[:, 0:TILES], neg_half[:, 0:TILES], ALU.pow).then_inc(s["rstd1"], 1)
            pool.wait_ge(s["ld_idx"], 48)
            for row in (up_row, down_row):
                pool.tensor_copy(row, row.bitcast(I32)).then_inc(s["rows_float"], 1)
            pool.wait_ge(s["rows_float"], 2)
            for row, equal, chunks in ((up_row, up_equal, KD), (down_row, down_equal, FCH)):
                for c in range(chunks):
                    pool.tensor_scalar(equal[:, c, :], row, iota_p[:, c:c + 1], None, ALU.is_equal).then_inc(s["compared"], 1)
            pool.memset(dA[:, :, :].rearrange("p k (b t) -> p k b t", b=BATCH)[:, :, :, 0:1], 0.0).then_inc(s["consts"], 1)
            pool.memset(row_of[:, :, :], 0.0).then_inc(s["selectors"], 1)
            for k in range(3):
                pool.wait_ge(s["selectors"], k + 1)
                pool.affine_select(out=row_of[:, :, :], in_=row_of[:, :, :], compare_op=ALU.not_equal, fill=1.0,
                                   base=-2 * NS * k, pattern=[[-1, 2 * NS], [0, P]], channel_multiplier=1)\
                    .then_inc(s["selectors"], 1)
            pool.wait_ge(s["ms2"], 3)
            pool.tensor_tensor(rs[:, TILES:4 * TILES], ms[:, TILES:4 * TILES], neg_half[:, 0:3 * TILES], ALU.pow).then_inc(s["rstd2"], 1)
            chained = [0]

            def link(ins):
                chained[0] += 1
                ins.then_inc(s["pool_chain"], 1)
                pool.wait_ge(s["pool_chain"], chained[0])

            R = 2 * NS
            pool.wait_ge(s["bc_float"], 1)
            link(pool.tensor_copy(bc3[0:R, :], bcf))
            link(pool.tensor_tensor(bc_rest, bcf, bc3[0:R, :], ALU.subtract))
            link(pool.tensor_copy(bc_mid, bc_rest))
            pool.tensor_copy(bc3[R:2 * R, :], bc_mid).then_inc(s["bc_split"], 1)
            pool.tensor_tensor(bc3[2 * R:3 * R, :], bc_rest, bc_mid, ALU.subtract).then_inc(s["bc_split"], 1)
            pool.wait_ge(s["bc_split"], 2)
            for c in range(CI):
                pool.wait_ge(s["softplus"], c + 1)
                pool.wait_ge(s["conv_out"], c + 1)
                pool.tensor_tensor(dtx[:, c, :], dt[:, c, :], xc[:, c, :], ALU.mult).then_inc(s["dtx_done"], 1)
            with pool.Fori(0, CI // 2) as pair:
                for n in range(NS):
                    step = pair * NS + n
                    pool.wait_ge(s["c_copied"], step + 1)
                    for k in range(2):
                        unit = step * 2 + k
                        pool.wait_ge(s["scan_done"], unit + 3)
                        pool.wait_ge(s["y_summed"], unit + 1)
                        pool.tensor_tensor(hC[:, k, :], h[:, k, :], c_copy[:, n % 2, :], ALU.mult).then_inc(s["hc_done"], 1)
            pool.wait_ge(s["ld_idx"], 48)
            pool.wait_ge(s["da_ready"], CI * NS)
            for m, name in enumerate(("w_gate", "w_up")):
                for c in range(FCH):
                    pool.indirect_dma_start(w_raw[m][:, c, :], None, inp[name], bass.IndirectOffsetOnAxis(gather_at[:, c:c + 1].bitcast(U32), 0))\
                        .then_inc(s[f"gathered_w{m}"], 16)
                if m == 0:
                    pool.wait_ge(s["ms3"], 1)
                    pool.tensor_tensor(rs[:, 0:TILES], ms[:, 0:TILES], neg_half[:, 0:TILES], ALU.pow).then_inc(s["rstd3"], 1)
            pool.wait_ge(s["slots_done"], 1)
            pool.wait_ge(s["moe_zeroed"], 32)
            pool.wait_ge(s["hn_done"], TILES)
            for k in range(2):
                for i in range(TILES):
                    pool.indirect_dma_start(moe_in[0:OUT_TILES * P, :], bass.IndirectOffsetOnAxis(slot[:, k, i:i + 1], 0), hn[:, i, :], None)\
                        .then_inc(s["scattered"], 16)

            total = pool.value_load(bounds[0:1, E:E + 1], min_val=E, max_val=OUT_TILES)
            pool.wait_ge(s["y_stored"], total * 16 + 16)
            pool.sem_inc(s["pool_waited"], 1)
            for half in range(2):
                for i in range(half * 4, half * 4 + 4):
                    for k in range(2):
                        pool.indirect_dma_start(y_got[k][:, i, :], None, moe_out[:, :], bass.IndirectOffsetOnAxis(slot[:, k, i:i + 1], 0))\
                            .then_inc(s[f"gathered{half}"], 16)

            def rstd(eps, done, turn, tiles):
                pool.wait_ge(s[eps], turn)
                pool.tensor_tensor(rs[:, tiles], ms[:, tiles], neg_half[:, tiles], ALU.pow).then_inc(s[done], 1)

            rstd("eps3", "rstd_x1", 1, slice(0, TILES))

            pool.wait_ge(s["x1T_done"], 2)

            def place_tile(i, j):
                pool.wait_ge(s["q_psum"], 4 * i + 12)
                pool.sem_inc(s["pool_waited"], 1)
                for k in range(KD):
                    ins = pool.tensor_copy(x_now[:, j, k, :], x1T[:, k, bass.ts(i, P)])
                ins.then_inc(s["x_now_ready"], 1)

            def query_rstd(i, j):
                pool.wait_ge(s["q_eps"], i + 1)
                pool.sem_inc(s["pool_waited"], 1)
                pool.tensor_tensor(q_rs[:, j, :], q_ms[:, j, :], neg_half[:, 0:HEADS], ALU.pow).then_inc(s["q_rstd"], 1)

            def tile_rstd(i, j):
                pool.wait_ge(s["eps4"], i + 1)
                pool.sem_inc(s["pool_waited"], 1)
                pool.tensor_tensor(tile_rs[:, j:j + 1], tile_var[:, j:j + 1], neg_half[:, 0:1], ALU.pow).then_inc(s["rstd_x2"], 1)

            place_tile(0, 0)
            place_tile(1, 1)
            query_rstd(0, 0)
            with pool.Fori(0, TILES // 2 - 1) as turn:
                for j in range(1, 3):
                    place_tile(2 * turn + j + 1, (j + 1) % 2)
                    query_rstd(2 * turn + j, j % 2)
                    tile_rstd(2 * turn + j - 1, (j + 1) % 2)
            query_rstd(TILES - 1, 1)
            tile_rstd(TILES - 2, 0)
            tile_rstd(TILES - 1, 1)
            pool.wait_ge(s["x_quant"], TILES)
            pool.memset(t_fp8[:, FF:], 0.0).then_inc(s["iota_done"], 1)
            with pool.Fori(0, TILES // 2) as turn:
                for j in range(2):
                    i = 2 * turn + j
                    pool.wait_ge(s["ff_gate"], i + 1)
                    pool.wait_ge(s["ff_read"], i + 2)
                    pool.wait_ge(s["t_in_ready"], i + 1)
                    pool.tensor_tensor(prod, gate_s[:, j, :], up_s[:, j, :], ALU.mult).then_inc(s["prod_done"], 1)
            rstd("eps5", "rstd_out", 1, slice(0, TILES - 1))
            rstd("eps5", "rstd_out", 2, slice(TILES - 1, TILES))

        @block.scalar
        def _(act):
            act.wait_ge(s["ld_x"], 16)
            for i in range(TILES):
                nc.scalar.activation(xn[:, i, :], x[:, i, :], ACT.Square,
                                     accum_out=ms[:, i:i + 1]).then_inc(s["sumsq1"], 1)
            act.wait_ge(s["ld_small"], 64)
            nc.scalar.activation(a_neg[:, :, :], lane[:, :, LANE_AT["a_log"]:LANE_AT["a_log"] + NS], ACT.Exp).then_inc(s["a_exp"], 1)
            act.wait_ge(s["hs_psum"], 2)
            nc.scalar.activation(hT[:, 1, :], ps[:, 2:4, :].rearrange("p a b -> p (a b)"), ACT.Identity,
                                 scale=cols[:, 1:2]).then_inc(s["hsT"], 1)
            act.wait_ge(s["consts"], 3)

            def convolved(c):
                act.wait_ge(s["conv_acc"], c + 1)
                nc.scalar.activation(xc[:, c, :], conv[:, c % 2, :], ACT.Silu,
                                     bias=lane[:, c, LANE_AT["conv_b"]:LANE_AT["conv_b"] + 1]).then_inc(s["conv_out"], 1)

            for n in range(4 * CI):
                c, half = divmod(n, 2)
                act.wait_ge(s["in_psum"], n + 1)
                src = ps[:, 4 + n % 4, :]
                if c < CI:
                    nc.scalar.activation(xpad[:, c, 2 * half:2 * half + 2, TAPS - 1:], src.rearrange("p (b t) -> p b t", b=2),
                                         ACT.Identity).then_inc(s["in_out"], 1)
                else:
                    nc.scalar.activation(zs[:, c - CI, half * HALF:(half + 1) * HALF], src, ACT.Silu).then_inc(s["in_out"], 1)
                if n < KD + FCH:
                    act.wait_ge(s["compared"], n + 1)
                    equal, col, k = (up_equal, up_col, n) if n < KD else (down_equal, down_col, n - KD)
                    nc.scalar.activation(equal[:, k, :], equal[:, k, :], ACT.Identity, accum_out=col[:, k:k + 1]).then_inc(s["indexed"], 1)
                if n in (6, 9, 12):
                    convolved((n - 6) // 3)
            convolved(CI - 1)
            act.wait_ge(s["xproj_psum"], TILES)
            nc.scalar.activation(xdb[:, :, :].rearrange("p (a b) c -> p a b c", b=2),
                                 ps[:, 0:4, :].rearrange("p a (b c) -> p a b c", b=2)[:, :, :, 0:XP], ACT.Identity).then_inc(s["xdb_sb"], 1)
            for c in range(CI):
                act.wait_ge(s["dt_psum"], 2 * c + 2)
                if c >= 2:
                    act.wait_ge(s["softplus"], c - 1)
                v = ps[:, 4 + 2 * (c % 2):6 + 2 * (c % 2), :].rearrange("p a b -> p (a b)")
                bias = lane[:, c, LANE_AT["dt_b"]:LANE_AT["dt_b"] + 1]
                nc.scalar.activation(rv[:, c % 2, :], v, ACT.Relu, bias=bias).then_inc(s["dt_act"], 1)
                nc.scalar.activation(u[:, c % 2, :], v, ACT.Abs, bias=bias).then_inc(s["dt_act"], 1)
                act.wait_ge(s["dt_act"], 3 * c + 2)
                nc.scalar.activation(u[:, c % 2, :], u[:, c % 2, :], ACT.Exp, scale=-1.0).then_inc(s["dt_act"], 1)
                act.wait_ge(s["dt_act"], 3 * c + 3)
                act.wait_ge(s["consts"], 2)
                for k in range(len(LOG1P)):
                    if c:
                        act.wait_ge(s["factor_taken"], (c - 1) * len(LOG1P) + k + 1)
                    nc.scalar.activation(squares[k], u[:, c % 2, :], ACT.Square, bias=shifts[:, k:k + 1]).then_inc(s["square_ready"], 1)
            act.wait_ge(s["a_ready"], 1)
            act.wait_ge(s["consts"], 4)
            dt_b = dt[:, :, :].rearrange("p c (b t) -> p c b t", b=BATCH)
            dA_b = dA[:, :, :].rearrange("p k (b t) -> p k b t", b=BATCH)
            with act.Fori(0, CI // 2) as pair:
                act.wait_ge(s["softplus"], pair * 2 + 2)
                for n in range(NS):
                    step = pair * NS + n
                    for k in range(2):
                        c, unit = pair * 2 + k, step * 2 + k
                        act.wait_ge(s["scan_done"], unit + 1)
                        nc.scalar.activation(dA_b[:, k, :, 1:], dt_b[:, c, :, 1:], ACT.Exp,
                                             scale=a_neg[:, c, n:n + 1]).then_inc(s["da_ready"], 1)
                        if k == 0:
                            act.wait_ge(s["c_ready"], step + 1)
                            act.wait_ge(s["hc_done"], step * 2)
                            nc.scalar.activation(c_copy[:, n % 2, :], ps[:, 2:4, :].rearrange("p a b -> p (a b)"), ACT.Identity)\
                                .then_inc(s["c_copied"], 1)

            act.wait_ge(s["out_psum"], TILES)
            act.dma_start(w_o, inp["w_o"]).then_inc(s["ld_o"], 16)
            act.dma_start(w_k, inp["w_k"]).then_inc(s["ld_k"], 16)
            act.wait_ge(s["res_done"], TILES)
            for i in range(TILES):
                nc.scalar.activation(hn[:, i, :], res[:, i, :], ACT.Square, accum_out=ms[:, i:i + 1]).then_inc(s["sumsq3"], 1)
            step = 0
            for n in range(PAIRS):
                act.wait_ge(s["kv_psum"], step + 1)
                nc.scalar.activation(vT[:, 2 * n:2 * n + 2, :], ps[:, 2 + step % 6, :].rearrange("p (a b) -> p a b", a=2), ACT.Identity).then_inc(s["kv_out"], 1)
                step += 1
            act.wait_ge(s["hn_psum"], KD)
            nc.scalar.activation(hfT[:, 1, :], ps[:, 6:8, :].rearrange("p a b -> p (a b)"), ACT.Identity).then_inc(s["hfT_done"], 1)
            act.wait_ge(s["logit_sub"], 1)
            nc.scalar.activation(prob[:, :, :], logit[:, :, :], ACT.Exp).then_inc(s["logit_exp"], 1)
            for n in range(2 * PAIRS):
                act.wait_ge(s["kv_psum"], step + 1)
                nc.scalar.activation(vw[:, n // 2, 2 * (n % 2):2 * (n % 2) + 2, :], ps[:, 2 + step % 6, :].rearrange("p (a b) -> p a b", a=2),
                                     ACT.Identity).then_inc(s["kv_out"], 1)
                step += 1

            act.wait_ge(s["slots_done"], 1)
            total = act.value_load(bounds[0:1, E:E + 1], min_val=E, max_val=OUT_TILES)
            with act.Fori(0, total) as j:
                for q in range(FCH // 2):
                    act.wait_ge(s["gu_psum"], j * (FCH // 2) + q + 1)
                    act.wait_ge(s["hid_done"], j * (FCH // 2) + q + 1)
                    nc.scalar.activation(act_g3[:, q, :], ps[:, 2 * q, 0:2 * P], ACT.Silu).then_inc(s["gate_act"], 1)

            for n in range(8):
                act.wait_ge(s["kv_psum"], step + 1)
                bank = 2 + step % 6
                at = (n % 4) * HALF
                nc.scalar.activation(k_sq[:, n // 4, at:at + HALF], ps[:, bank, :], ACT.Square, scale=float(DH) ** -0.5).then_inc(s["k_squared"], 1)
                nc.scalar.activation(k_raw[:, n // 4, at:at + HALF], ps[:, bank, :], ACT.Identity).then_inc(s["kv_out"], 1)
                step += 1
            act.wait_ge(s["k_ms"], 1)
            nc.scalar.activation(k_rs[:, :], k_ms[:, :], ACT.Sqrt).then_inc(s["k_sqrt"], 1)
            for n in range(PAIRS):
                if n % 3 == 0:
                    m = n // 3
                    act.wait_ge(s["spread_psum"], 3 + m)
                    width = (FCH, FCH, KD)[m] * P
                    nc.scalar.activation(scale_rows[m], ps[:, 0:2, :].rearrange("p a b -> p (a b)")[:, 0:width], ACT.Identity).then_inc(s["spread_done"], 1)
                act.wait_ge(s["kv_psum"], step + 1)
                nc.scalar.activation(kT[:, 2 * n:2 * n + 2, :], ps[:, 2 + step % 6, :].rearrange("p (a b) -> p a b", a=2), ACT.Identity,
                                     scale=gqk[:, 0:1]).then_inc(s["kv_out"], 1)
                step += 1
            for n in range(KD * PAIRS):
                act.wait_ge(s["kv_psum"], step + 1)
                pair = n // KD
                nc.scalar.activation(qk[n % KD][:, :, 2 * pair:2 * pair + 2, :].rearrange("p b h t -> p h b t"),
                                     ps[:, 2 + step % 6, :].rearrange("p (h b t) -> p h b t", h=2, b=BATCH), ACT.Identity).then_inc(s["kv_out"], 1)
                step += 1

            act.wait_ge(s["x1T_psum"], 2)
            nc.scalar.activation(x1T[:, 1, :], ps[:, 2:4, :].rearrange("p a b -> p (a b)"), ACT.Identity).then_inc(s["x1T_done"], 1)
            def mean_squares(i, j, groups):
                for g in groups:
                    act.wait_ge(s["q_psum"], 4 * i + g + 17)
                    act.wait_ge(s["q_squared"], 4 * i + g + 1)
                    if g == 0:
                        act.wait_ge(s["q_rstd"], i + 1)
                    for hd in range(4):
                        ins = nc.scalar.activation(q_junk[:, g % 2, hd * DH:(hd + 1) * DH], ps[:, g % 2, hd * DH:(hd + 1) * DH], ACT.Square,
                                                   scale=float(DH) ** -0.5, accum_out=q_ms[:, j, 4 * g + hd:4 * g + hd + 1])
                    ins.then_inc(s["q_squared"], 1)

            def exponential(i, j):
                act.wait_ge(s["s_shifted"], i + 1)
                nc.scalar.activation(shift[:, j, :, :], shift[:, j, :, :], ACT.Exp).then_inc(s["s_exp"], 1)

            def take_transposed_probs(i, j):
                act.wait_ge(s["attn_psum"], i + 1)
                for half in range(2):
                    act.wait_ge(s["pT_psum"], 2 * i + half + 5)
                    nc.scalar.activation(pT[:, j, 4 * half:4 * half + 4, :], ps[:, 4 + half, :].rearrange("p (a b) -> p a b", b=P),
                                         ACT.Identity).then_inc(s["pT_done"], 1)

            mean_squares(0, 0, range(4))
            with act.Fori(0, TILES // 2 - 1) as turn:
                for j in range(2):
                    exponential(2 * turn + j, j)
                    mean_squares(2 * turn + j + 1, (j + 1) % 2, (0,))
                    mean_squares(2 * turn + j + 1, (j + 1) % 2, (1, 2))
                    take_transposed_probs(2 * turn + j, j)
                    mean_squares(2 * turn + j + 1, (j + 1) % 2, (3,))
            exponential(TILES - 2, 0)
            mean_squares(TILES - 1, 1, (0,))
            mean_squares(TILES - 1, 1, (1, 2))
            take_transposed_probs(TILES - 2, 0)
            mean_squares(TILES - 1, 1, (3,))
            exponential(TILES - 1, 1)

            def take_tokens(half):
                act.wait_ge(s["xT8_psum"], half + 1)
                nc.scalar.activation(qxT[:, :, half * HALF:(half + 1) * HALF], ps[:, 2 + 4 * half, :].bitcast(BF16).rearrange("p (a b) -> p a b", a=KD), ACT.Identity).then_inc(s["xT8_done"], 1)

            take_tokens(0)
            take_transposed_probs(TILES - 1, 1)

            def gate_of(i, j):
                act.wait_ge(s["ff_in"], i + 1)
                nc.scalar.activation(gate_s[:, j, :], gate_s[:, j, :], ACT.Silu, scale=xscale[:, bass.ds(i, 1)]).then_inc(s["ff_gate"], 1)

            def scale_row(i):
                act.wait_ge(s["t_scaled"], i + 1)
                nc.scalar.activation(t_in, prod, ACT.Identity, scale=tinv[:, 0:1]).then_inc(s["t_in_ready"], 1)
                act.wait_ge(s["t_in_ready"], i + 2)
                nc.scalar.activation(t_size, t_in, ACT.Abs, scale=ROUND_AT).then_inc(s["t_size_ready"], 1)

            def take_hidden(i):
                act.wait_ge(s["t_psum"], i + 2)
                act.wait_ge(s["y2_psum"], i + 1)
                nc.scalar.activation(t_fp8T, ps[:, 4, 0:FPAD // 2].bitcast(BF16).rearrange("p (a b) -> p a b", b=P), ACT.Identity).then_inc(s["tT_done"], 1)

            gate_of(0, 0)
            take_tokens(1)
            scale_row(0)
            gate_of(1, 1)
            take_hidden(0)
            with act.Fori(0, TILES // 2 - 1) as turn:
                for j in range(1, 3):
                    scale_row(2 * turn + j)
                    gate_of(2 * turn + j + 1, (j + 1) % 2)
                    take_hidden(2 * turn + j)
            scale_row(TILES - 1)
            take_hidden(TILES - 1)

        @block.vector
        def _(dve):
            chain = [0]

            def link(ins):
                chain[0] += 1
                ins.then_inc(s["dve_chain"], 1)
                dve.wait_ge(s["dve_chain"], chain[0])



            for name, credit in (("scan_done", 2), ("y_summed", 2), ("hc_done", 2), ("y_drained", 2)):
                dve.sem_inc(s[name], credit)
            dve.wait_ge(s["sumsq1"], TILES)
            nc.vector.tensor_scalar(ms[:, 0:TILES], ms[:, 0:TILES], 1.0 / D, 1e-6, ALU.mult, ALU.add).then_inc(s["ms1"], 1)
            dve.wait_ge(s["rstd1"], 1)
            for i in range(TILES):
                nc.vector.tensor_scalar(xn[:, i, :], x[:, i, :], rs[:, i:i + 1], None, ALU.mult).then_inc(s["xn"], 1)
            dve.wait_ge(s["a_exp"], 1)
            nc.vector.tensor_scalar(a_neg[:, :, :], a_neg[:, :, :], -1.0, None, ALU.mult).then_inc(s["a_ready"], 1)
            dve.wait_ge(s["hs_psum"], 1)
            dve.wait_ge(s["ld_small"], 64)
            nc.vector.tensor_scalar(hT[:, 0, :], ps[:, 0:2, :].rearrange("p a b -> p (a b)"), cols[:, 0:1], None, ALU.mult).then_inc(s["hsT"], 1)
            def diagonals(dst, col, chunks):
                return nc.vector.tensor_tensor(dst, ident[:, :].unsqueeze(1).to_broadcast([P, chunks, P]),
                                               col.unsqueeze(2).to_broadcast([P, chunks, P]), ALU.mult)

            for c in range(CI):
                if c == CI - 1:
                    dve.wait_ge(s["indexed"], KD + FCH)
                    diagonals(up_diag, up_col[:, :], KD).then_inc(s["counted"], 1)
                    diagonals(down_diag, down_col[:, :], FCH).then_inc(s["counted"], 1)
                dve.wait_ge(s["in_out"], 2 * c + 2)
                if c >= 2:
                    dve.wait_ge(s["conv_out"], c - 1)
                acc = conv[:, c % 2, :].rearrange("p (b t) -> p b t", b=BATCH)
                tap = lambda k: lane[:, c, LANE_AT["conv_w"] + k:LANE_AT["conv_w"] + k + 1]
                link(nc.vector.tensor_scalar(acc, xpad[:, c, :, 0:SEQ], tap(0), None, ALU.mult))
                for k in range(1, TAPS):
                    ins = nc.vector.scalar_tensor_tensor(acc, xpad[:, c, :, k:k + SEQ], tap(k), acc, ALU.mult, ALU.add)
                    if k < TAPS - 1:
                        link(ins)
                    else:
                        ins.then_inc(s["conv_acc"], 1)
            dve.wait_ge(s["spread_psum"], 2)
            nc.vector.tensor_scalar(up_mask[:, :], ps[:, 2, 0:D], 1.0, None, ALU.min).then_inc(s["spread_done"], 1)
            nc.vector.tensor_scalar(down_mask, ps[:, 0:2, :].rearrange("p a b -> p (a b)")[:, 0:FPAD], 1.0, None, ALU.min).then_inc(s["spread_done"], 1)
            dve.wait_ge(s["spread_done"], 2)

            def quantise(m, parts=(0, 1, 2)):
                mask, chunks, width = ((up_mask[:, :], FCH, D), (up_mask[:, :], FCH, D), (down_mask[:, 0:FF], KD, FF))[m]
                w, size = w_raw[m], w_size[m][:, 0:chunks * width].rearrange("p (a b) -> p a b", b=width)
                largest, inverse, scale = (v[:, m, 0:chunks] for v in (w_max, w_inv, w_scale))
                if 0 in parts:
                    dve.wait_ge(*((s["gathered_w0"], FCH * 16), (s["gathered_w1"], FCH * 16), (s["ld_down"], 16))[m])
                    link(nc.vector.tensor_tensor(w, w, mask.unsqueeze(1).to_broadcast([P, chunks, width]), ALU.mult))
                    link(nc.vector.tensor_reduce(largest, w, axis=AX.X, op=ALU.max, apply_absolute_value=True))
                    link(nc.vector.tensor_scalar(scale, largest, 1.0 / FP8_MAX, None, ALU.mult))
                    link(nc.vector.reciprocal(inverse, scale))
                if 1 in parts:
                    for c in range(chunks):
                        ins = nc.vector.tensor_scalar(w[:, c, :], w[:, c, :], inverse[:, c:c + 1], None, ALU.mult)
                    link(ins)
                    link(nc.vector.tensor_scalar(size.bitcast(I32), w.bitcast(I32), NOT_SIGN, None, ALU.bitwise_and))
                    link(nc.vector.tensor_scalar(size, size, ROUND_AT, LEAST_ADDED, ALU.mult, ALU.max))
                if 2 in parts:
                    link(nc.vector.tensor_tensor(w, w, size, ALU.add))
                    link(nc.vector.tensor_tensor(w_fp8[m][:, :, 0:width], size, w, ALU.subtract))
                    if m == 2:
                        link(nc.vector.memset(w_fp8[m][:, :, FF:], 0.0))
                    dve.sem_inc(s["quantised"], 1)

            quantise(2)
            dve.wait_ge(s["xdb_sb"], 1)
            sq = junk
            link(nc.vector.tensor_tensor(sq, xdb[:, :, :], xdb[:, :, :], ALU.mult))
            groups = ((0, DR), (DR, NS), (DR + NS, NS))
            for g, (at, width) in enumerate(groups):
                dst = ms[:, (g + 1) * TILES:(g + 2) * TILES]
                link(nc.vector.tensor_reduce(dst, sq[:, :, at:at + width], axis=AX.X, op=ALU.add))
                nc.vector.tensor_scalar(dst, dst, 1.0 / width, 1e-6, ALU.mult, ALU.add).then_inc(s["ms2"], 1)
            dve.wait_ge(s["rstd2"], 1)
            for g, (at, width) in enumerate(groups):
                part = xdb[:, :, at:at + width]
                rstd = rs[:, (g + 1) * TILES:(g + 2) * TILES].unsqueeze(2).to_broadcast([P, TILES, width])
                nc.vector.tensor_tensor(part, part, rstd, ALU.mult).then_inc(s["xdbn"], 1)
            dve.wait_ge(s["dtn_psum"], 1)
            nc.vector.tensor_scalar(dtnT, ps[:, 0:2, :].rearrange("p a b -> p (a b)"), cols[:, 2:3], None, ALU.mult).then_inc(s["dtn_sb"], 1)
            dve.wait_ge(s["bc_psum"], 1)
            R = 2 * NS
            nc.vector.tensor_scalar(bcf, ps[0:R, 2:4, :].rearrange("p a b -> p (a b)"), bc_ln[:, 0:1], None, ALU.mult).then_inc(s["bc_float"], 1)
            for c in range(CI):
                dve.wait_ge(s["dt_act"], 3 * c + 3)
                acc = dt[:, c, :]
                for k, (_, add) in enumerate(LOG1P):
                    dve.wait_ge(s["square_ready"], c * len(LOG1P) + k + 1)
                    nc.vector.scalar_tensor_tensor(acc, squares[k], add, acc if k else u[:, c % 2, :], ALU.add, ALU.mult).then_inc(s["factor_taken"], 1)
                    dve.wait_ge(s["factor_taken"], c * len(LOG1P) + k + 1)
                nc.vector.scalar_tensor_tensor(acc, acc, LOG1P_SCALE, rv[:, c % 2, :], ALU.mult, ALU.add).then_inc(s["softplus"], 1)

            pB = ps[:, 0:2, :].rearrange("p a b -> p (a b)")
            def inputs_of(pair, n):
                step = pair * NS + n
                dve.wait_ge(s["b_ready"], step + 1)
                for k in range(2):
                    dve.wait_ge(s["scan_done"], step * 2 + k + 1)
                    nc.vector.tensor_tensor(dBx[:, k, :], dtx[:, pair * 2 + k, :], pB, ALU.mult).then_inc(s["dbx_done"], 1)

            def scans_of(pair, n):
                for k in range(2):
                    unit = (pair * NS + n) * 2 + k
                    dve.wait_ge(s["da_ready"], unit + 1)
                    dve.wait_ge(s["dbx_done"], unit + 1)
                    dve.wait_ge(s["hc_done"], unit + 1)
                    nc.vector.tensor_tensor_scan(h[:, k, :], dA[:, k, :], dBx[:, k, :], 0.0, ALU.mult, ALU.add).then_inc(s["scan_done"], 1)

            def add_skips(pair):
                dve.wait_ge(s["dbx_done"], (pair + 1) * NS * 2)
                for k in range(2):
                    c = pair * 2 + k
                    dve.wait_ge(s["y_summed"], (pair + 1) * NS * 2 + k + 1)
                    nc.vector.scalar_tensor_tensor(dtx[:, c, :], xc[:, c, :], lane[:, c, LANE_AT["d_param"]:LANE_AT["d_param"] + 1],
                                                   ps[:, 4 + 2 * k:6 + 2 * k, :].rearrange("p a b -> p (a b)"), ALU.mult, ALU.add)\
                        .then_inc(s["y_drained"], 1)

            def times_gates(pair):
                for k in range(2):
                    c = pair * 2 + k
                    dve.wait_ge(s["y_drained"], c + 3)
                    nc.vector.tensor_tensor(dtx[:, c, :], dtx[:, c, :], zs[:, c, :], ALU.mult).then_inc(s["ym_done"], 1)

            def scan_pair(pair, before):
                for n in range(NS):
                    inputs_of(pair, n)
                    scans_of(pair, n)
                    if n == 0 and before is not None:
                        add_skips(before)
                    if n == 2 and before is not None:
                        times_gates(before)

            dve.wait_ge(s["dtx_done"], 2)
            scan_pair(0, None)
            dve.wait_ge(s["dtx_done"], CI)
            with dve.Fori(0, CI // 2 - 1) as pair:
                scan_pair(pair + 1, pair)
            add_skips(CI // 2 - 1)
            times_gates(CI // 2 - 1)
            for i in range(TILES):
                dve.wait_ge(s["out_psum"], i + 1)
                nc.vector.tensor_tensor(res[:, i, :], x[:, i, :], ps[:, i, 0:D], ALU.add).then_inc(s["res_done"], 1)
            quantise(0, (0,))
            dve.wait_ge(s["sumsq3"], TILES)
            nc.vector.tensor_scalar(ms[:, 0:TILES], ms[:, 0:TILES], 1.0 / D, 1e-6, ALU.mult, ALU.add).then_inc(s["ms3"], 1)
            dve.wait_ge(s["rstd3"], 1)
            dve.wait_ge(s["ld_lnff"], 16)
            for i in range(TILES):
                nc.vector.scalar_tensor_tensor(hn[:, i, :], res[:, i, :], rs[:, i:i + 1], ln_ff_row[:, :], ALU.mult, ALU.mult).then_inc(s["hn_done"], 1)
            dve.wait_ge(s["hn_psum"], 1)
            nc.vector.tensor_copy(hfT[:, 0, :], ps[:, 4:6, :].rearrange("p a b -> p (a b)")).then_inc(s["hfT_done"], 1)
            quantise(0, (1,))
            stat_of = lambda k, n=E: stat[:, k, :].unsqueeze(2).to_broadcast([P, TILES, n])
            dve.wait_ge(s["logit_psum"], 1)
            link(nc.vector.tensor_copy(logit[:, :, :], ps[:, 0, 0:TILES * E].rearrange("p (i e) -> p i e", e=E)))
            link(nc.vector.tensor_reduce(stat[:, 0, :], logit[:, :, :], axis=AX.X, op=ALU.max))
            nc.vector.tensor_tensor(logit[:, :, :], logit[:, :, :], stat_of(0), ALU.subtract).then_inc(s["logit_sub"], 1)
            dve.wait_ge(s["logit_exp"], 1)
            link(nc.vector.tensor_reduce(stat[:, 1, :], prob[:, :, :], axis=AX.X, op=ALU.add))
            link(nc.vector.reciprocal(stat[:, 2, :], stat[:, 1, :]))
            link(nc.vector.tensor_tensor(prob[:, :, :], prob[:, :, :], stat_of(2), ALU.mult))
            for i in range(TILES):
                ins = nc.vector.max(best[:, i, :], prob[:, i, :])
            link(ins)
            for i in range(TILES):
                ins = nc.vector.max_index(best_at[:, i, :], best[:, i, :], prob[:, i, :])
            link(ins)
            link(nc.vector.tensor_copy(best_f[:, :, :], best_at[:, :, :]))
            dve.wait_ge(s["tables"], 3)
            for k in range(2):
                nc.vector.tensor_tensor(picked[k][:, :, :], iota_e[:, :].unsqueeze(1).to_broadcast([P, TILES, E]),
                                        best_f[:, :, k:k + 1].to_broadcast([P, TILES, E]), ALU.is_equal).then_inc(s["picked_done"], 1)
            dve.wait_ge(s["picked_done"], 2)
            link(nc.vector.tensor_tensor(both[:, :, :], picked[0][:, :, :], picked[1][:, :, :], ALU.add))
            link(nc.vector.memset(earlier[:, 0, :], 0.0))
            for i in range(1, TILES):
                ins = nc.vector.tensor_tensor(earlier[:, i, :], earlier[:, i - 1, :], both[:, i - 1, :], ALU.add)
                if i < TILES - 1:
                    link(ins)
            ins.then_inc(s["picked_done"], 1)
            dve.wait_ge(s["prefix_psum"], 1)
            link(nc.vector.tensor_scalar(count_i[:, :], ps[:, 1, 0:E], float(P - 1), None, ALU.add))
            link(nc.vector.tensor_scalar(count_i[:, :], count_i[:, :], 7, None, ALU.logical_shift_right))
            link(nc.vector.tensor_scalar(count[:, 0, :], count_i[:, :], 1.0, None, ALU.max))
            link(nc.vector.tensor_tensor_scan(count[:, 1, :], ones[:, 0:E], count[:, 0, :], 0.0, ALU.mult, ALU.add))

            link(nc.vector.memset(bounds[:, 0:1], 0))
            link(nc.vector.tensor_copy(bounds[:, 1:E + 1], count[:, 1, :]))
            link(nc.vector.tensor_tensor(count[:, 2, :], count[:, 1, :], count[:, 0, :], ALU.subtract))
            link(nc.vector.tensor_scalar(count[:, 3, :], count[:, 2, :], float(P), None, ALU.mult))
            link(nc.vector.tensor_tensor(place[:, :, :], ps[:, 1, E:E + TILES * E].rearrange("p (i e) -> p i e", e=E),
                                         count[:, 3, :].unsqueeze(1).to_broadcast([P, TILES, E]), ALU.add))
            for k in range(2):
                link(nc.vector.tensor_tensor(picked[k][:, :, :], picked[k][:, :, :], place[:, :, :], ALU.mult))
                link(nc.vector.tensor_reduce(slot_f[:, k, :], picked[k][:, :, :], axis=AX.X, op=ALU.add))
            nc.vector.tensor_copy(slot[:, :, :], slot_f[:, :, :]).then_inc(s["slots_done"], 1)
            link(nc.vector.tensor_tensor(gqk[:, :], cols[:, 5:6], cols[:, 6:7], ALU.mult))
            link(nc.vector.tensor_scalar(gqk[:, :], gqk[:, :], float(DH) ** -0.5, None, ALU.mult))
            link(nc.vector.tensor_scalar(down_one[:, :], down_col[:, :], 1.0, None, ALU.min))
            for turn, m in enumerate((0, 2, 1)):
                if m == 0:
                    quantise(0, (2,))
                if m == 2:
                    quantise(1, (0,))
                if m == 1:
                    quantise(1, (1, 2))
                    link(nc.vector.tensor_tensor(w_scale[:, 1, :], w_scale[:, 1, :], down_one[:, :], ALU.mult))
                for half in range(2):
                    dve.wait_ge(s["wT_psum"], 2 * turn + half + 1)
                    src = ps[:, half, 0:FPAD // 2].bitcast(BF16)
                    if m < 2:
                        ins = nc.vector.tensor_scalar(w_fp8T[m][:, half, :], src, up_col[:, half:half + 1], None, ALU.mult)
                    else:
                        three = slice(3 * half, 3 * half + 3)
                        ins = nc.vector.tensor_tensor(w_fp8T[m][:, three, :], src.rearrange("p (a b) -> p a b", b=D),
                                                      down_col[:, three].unsqueeze(2).to_broadcast([P, 3, D]), ALU.mult)
                    ins.then_inc(s["wT_done"], 1)
            dve.wait_ge(s["slots_done"], 1)
            dve.sem_inc(s["hid_done"], HID_BUFS)
            dve.sem_inc(s["xT_psum"], 1)
            dve.sem_inc(s["y_psum"], 1)
            dve.sem_inc(s["y_ready"], 1)
            dve.sem_inc(s["y_stored"], 16)
            dve.sem_inc(s["xT_done"], 1)
            total = dve.value_load(bounds[0:1, E:E + 1], min_val=E, max_val=OUT_TILES)

            def take_transposed(tile):
                dve.wait_ge(s["xT_psum"], tile + 2)
                nc.vector.tensor_copy(xT, ps[:, 7, 0:D].rearrange("p (k n) -> p k n", k=KD)).then_inc(s["xT_done"], 1)

            take_transposed(0)
            with dve.Fori(0, total) as j:
                for q in range(FCH // 2):
                    dve.wait_ge(s["gate_act"], j * (FCH // 2) + q + 1)
                    dve.wait_ge(s["y_psum"], j + 1)
                    nc.vector.tensor_tensor(hid[:, 2 * q:2 * q + 2, :], act_g3[:, q, :].rearrange("p (a b) -> p a b", b=P),
                                            ps[:, 2 * q + 1, 0:2 * P].rearrange("p (a b) -> p a b", b=P), ALU.mult).then_inc(s["hid_done"], 1)
                take_transposed(j + 1)
                dve.wait_ge(s["y_psum"], j + 2)
                dve.wait_ge(s["y_stored"], j * 16 + 16)
                nc.vector.tensor_copy(y_row, ps[:, 6, 0:D]).then_inc(s["y_ready"], 1)
            for m, chunks in enumerate((FCH, FCH, KD)):
                diagonals(diag[m], w_scale[:, m, 0:chunks], chunks).then_inc(s["counted"], 1)
            for n in range(8):
                dve.wait_ge(s["k_squared"], n + 1)
                ins = nc.vector.tensor_reduce(k_ms[:, 4 * n:4 * n + 4], k_sq[:, n // 4, (n % 4) * HALF:(n % 4 + 1) * HALF].rearrange("p (h d) -> p h d", d=DH),
                                              axis=AX.X, op=ALU.add)
            link(ins)
            nc.vector.tensor_scalar(k_ms[:, :], k_ms[:, :], 1e-5, None, ALU.add).then_inc(s["k_ms"], 1)
            dve.wait_ge(s["k_sqrt"], 1)
            dve.wait_ge(s["kv_out"], 3 * PAIRS + 8)
            link(nc.vector.reciprocal(k_rs[:, :], k_rs[:, :]))
            for quarter in range(4):
                heads = slice(quarter * HEADS // 4, (quarter + 1) * HEADS // 4)
                k_heads = k_raw.rearrange("p j (h d) -> p j h d", d=DH)[:, :, heads, :]
                k_rstd = k_rs[:, :].rearrange("p (j h) -> p j h", j=2)[:, :, heads].unsqueeze(3).to_broadcast([P, 2, HEADS // 4, DH])
                nc.vector.tensor_tensor(k_heads, k_heads, k_rstd, ALU.mult).then_inc(s["k_normed"], 1)
            for half in range(2):
                dve.wait_ge(s[f"gathered{half}"], TILES * 16)
                tiles = range(half * 4, half * 4 + 4)
                for k in range(2):
                    for n, i in enumerate(tiles):
                        if k:
                            dve.wait_ge(s["x1_sum"], half * TILES + n + 1)
                        nc.vector.scalar_tensor_tensor(x[:, i, :], y_got[k][:, i, :], best[:, i, k:k + 1], x[:, i, :], ALU.mult, ALU.add).then_inc(s["x1_sum"], 1)
                for n, i in enumerate(tiles):
                    dve.wait_ge(s["x1_sum"], half * TILES + n + 5)
                    nc.vector.bn_stats(bn[:, i, :], x[:, i, :]).then_inc(s["bn3"], 1)

            def variances(stats, eps, tiles):
                dve.wait_ge(s[stats], tiles.stop)
                for i in range(tiles.start, tiles.stop):
                    ins = nc.vector.bn_aggr(mv[:, i, :], bn[:, i, :])
                link(ins)
                nc.vector.tensor_scalar(ms[:, tiles], mv[:, tiles, 1:2].rearrange("p a b -> p (a b)"), 1e-5, None, ALU.add).then_inc(s[eps], 1)

            def normalise(done, tiles):
                for i in range(tiles.start, tiles.stop):
                    nc.vector.tensor_scalar(x[:, i, :], x[:, i, :], mv[:, i, 0:1], rs[:, i:i + 1], ALU.subtract, ALU.mult).then_inc(s[done], 1)

            variances("bn3", "eps3", slice(0, TILES))
            dve.wait_ge(s["rstd_x1"], 1)
            normalise("x1_done", slice(0, TILES))

            for name, credit in (("q_psum", 16), ("q_squared", 2), ("q_rstd", 2), ("s_taken", 1), ("s_soft", 2),
                                 ("pT_psum", 4), ("pT_done", 2), ("attn_psum", 2), ("attn_taken", 2)):
                dve.sem_inc(s[name], credit)
            dve.wait_ge(s["x1T_psum"], 1)
            nc.vector.tensor_copy(x1T[:, 0, :], ps[:, 0:2, :].rearrange("p a b -> p (a b)")).then_inc(s["x1T_done"], 1)

            over = lambda t, j: t[:, j, :].unsqueeze(2).to_broadcast([P, HEADS, KV])
            scores = ps[:, 2:4, :].rearrange("p a (h t) -> p (a h) t", t=KV)

            def link_tile(ins, i, n):
                ins.then_inc(s["attn_chain"], 1)
                dve.wait_ge(s["attn_chain"], 3 * i + n)

            def take_scores(i, j):
                dve.wait_ge(s["s_psum"], i + 1)
                link_tile(nc.vector.tensor_reduce(top[:, j, :], scores, axis=AX.X, op=ALU.max), i, 1)
                dve.wait_ge(s["s_soft"], i + 1)
                nc.vector.tensor_tensor(shift[:, j, :, :], scores, over(top, j), ALU.subtract).then_inc(s["s_taken"], 1)

            def add_epsilon(i, j):
                dve.wait_ge(s["q_squared"], 4 * i + 6)
                nc.vector.tensor_scalar(q_ms[:, j, :], q_ms[:, j, :], 1e-5, None, ALU.add).then_inc(s["q_eps"], 1)

            def softmax(i, j):
                dve.wait_ge(s["s_taken"], i + 2)
                dve.wait_ge(s["q_rstd"], i + 3)
                nc.vector.tensor_tensor(shift[:, j, :, :], shift[:, j, :, :], over(q_rs, j), ALU.mult).then_inc(s["s_shifted"], 1)
                dve.wait_ge(s["s_exp"], i + 1)
                link_tile(nc.vector.tensor_reduce(total_e[:, j, :], shift[:, j, :, :], axis=AX.X, op=ALU.add), i, 2)
                link_tile(nc.vector.reciprocal(total_e[:, j, :], total_e[:, j, :]), i, 3)
                dve.wait_ge(s["pT_psum"], 2 * i + 2)
                nc.vector.tensor_tensor(soft[:, j, :, :], shift[:, j, :, :], over(total_e, j), ALU.mult).then_inc(s["s_soft"], 1)

            def add_attention(i, j):
                dve.wait_ge(s["attn_psum"], i + 3)
                nc.vector.tensor_tensor(x[:, bass.ds(i, 1), :], x[:, bass.ds(i, 1), :], ps[:, 6 + j, 0:D].unsqueeze(1), ALU.add).then_inc(s["attn_taken"], 1)
                dve.wait_ge(s["attn_taken"], i + 3)
                link_x2(nc.vector.bn_stats(bn[:, bass.ds(i, 1), :].rearrange("p a b -> p (a b)"), x_row(i)), i, 1)
                link_x2(nc.vector.tensor_scalar(tile_bn[:, j, :], bn[:, bass.ds(i, 1), :].rearrange("p a b -> p (a b)"), 1.0, None, ALU.mult), i, 2)
                dve.sem_inc(s["dve_waited"], 1)
                link_x2(nc.vector.bn_aggr(mv[:, j, :], tile_bn[:, j, :]), i, 3)
                nc.vector.tensor_scalar(tile_var[:, j:j + 1], mv[:, j, 1:2], 1e-5, None, ALU.add).then_inc(s["eps4"], 1)

            x_row = lambda i: x[:, bass.ds(i, 1), :].rearrange("p a b -> p (a b)")

            def link_x2(ins, i, n):
                ins.then_inc(s["x2_stats"], 1)
                dve.wait_ge(s["x2_stats"], 3 * i + n)

            def link_q(ins, i, n):
                ins.then_inc(s["x2_chain"], 1)
                dve.wait_ge(s["x2_chain"], 9 * i + n)

            def quantise_tile(i, j):
                dve.wait_ge(s["rstd_x2"], i + 1)
                link_q(nc.vector.tensor_scalar(x_row(i), x_row(i), mv[:, j, 0:1], tile_rs[:, j:j + 1], ALU.subtract, ALU.mult), i, 1)
                link_q(nc.vector.tensor_tensor(x_in[:, j, :], x_row(i), up_mask[:, :], ALU.mult), i, 2)
                link_q(nc.vector.tensor_reduce(tile_inv[:, j:j + 1], x_in[:, j, :], axis=AX.X, op=ALU.max, apply_absolute_value=True), i, 3)
                link_q(nc.vector.tensor_scalar(tile_scale[:, j:j + 1], tile_inv[:, j:j + 1], 1.0 / FP8_MAX, None, ALU.mult), i, 4)
                nc.vector.tensor_scalar(xscale[:, bass.ds(i, 1)], tile_scale[:, j:j + 1], 1.0, None, ALU.mult)
                link_q(nc.vector.reciprocal(tile_inv[:, j:j + 1], tile_scale[:, j:j + 1]), i, 5)
                link_q(nc.vector.tensor_scalar(x_in[:, j, :], x_in[:, j, :], tile_inv[:, j:j + 1], None, ALU.mult), i, 6)
                link_q(nc.vector.tensor_scalar(x_size[:, j, :].bitcast(I32), x_in[:, j, :].bitcast(I32), NOT_SIGN, None, ALU.bitwise_and), i, 7)
                link_q(nc.vector.tensor_scalar(x_size[:, j, :], x_size[:, j, :], ROUND_AT, LEAST_ADDED, ALU.mult, ALU.max), i, 8)
                link_q(nc.vector.tensor_tensor(x_in[:, j, :], x_in[:, j, :], x_size[:, j, :], ALU.add), i, 9)
                nc.vector.tensor_tensor(qx[:, bass.ds(i, 1), :].rearrange("p a b -> p (a b)"), x_size[:, j, :], x_in[:, j, :], ALU.subtract).then_inc(s["x_quant"], 1)

            dve.wait_ge(s["spread_done"], 5)
            def attention_step(turn, j, last=False):
                softmax(2 * turn + j + 1, (j + 1) % 2)
                if not last:
                    take_scores(2 * turn + j + 2, j % 2)
                add_attention(2 * turn + j, j % 2)
                if not last:
                    add_epsilon(2 * turn + j + 2, j % 2)
                quantise_tile(2 * turn + j - 1, (j + 1) % 2)

            take_scores(0, 0)
            add_epsilon(0, 0)
            softmax(0, 0)
            take_scores(1, 1)
            add_epsilon(1, 1)
            softmax(1, 1)
            take_scores(2, 0)
            add_attention(0, 0)
            add_epsilon(2, 0)
            with dve.Fori(0, TILES // 2 - 2) as turn:
                for j in range(1, 3):
                    attention_step(turn, j)
            attention_step(TILES // 2 - 2, 1)
            attention_step(TILES // 2 - 2, 2, last=True)
            for name in ("ff_read", "t_in_ready", "t_psum", "tT_done", "y2_psum", "y2_read"):
                dve.sem_inc(s[name], 1)
            in_two = lambda v: v[:, 0:FF].rearrange("p (a b) -> p a b", a=2)

            def link_ff(ins, i, n):
                ins.then_inc(s["ff_chain"], 1)
                dve.wait_ge(s["ff_chain"], 3 * i + n)

            def take_gate_and_up(i, j):
                dve.wait_ge(s["ff_psum"], i + 1)
                nc.vector.tensor_tensor(in_two(gate_s[:, j, :]), ps[:, 0:2, 0:FF // 2], in_two(scale_rows[0]), ALU.mult).then_inc(s["ff_in"], 1)
                nc.vector.scalar_tensor_tensor(in_two(up_s[:, j, :]), ps[:, 2:4, 0:FF // 2], xscale[:, bass.ds(i, 1)], in_two(scale_rows[1]),
                                               ALU.mult, ALU.mult).then_inc(s["ff_read"], 1)

            def hidden(i, j):
                dve.wait_ge(s["prod_done"], i + 1)
                link_ff(nc.vector.tensor_reduce(tmax[:, :], prod, axis=AX.X, op=ALU.max, apply_absolute_value=True), i, 1)
                link_ff(nc.vector.tensor_scalar(tscale[:, j:j + 1], tmax[:, :], 1.0 / FP8_MAX, None, ALU.mult), i, 2)
                nc.vector.reciprocal(tinv[:, :], tscale[:, j:j + 1]).then_inc(s["t_scaled"], 1)

            def round_hidden(i):
                dve.wait_ge(s["t_size_ready"], i + 1)
                nc.vector.scalar_tensor_tensor(t_in, t_size, LEAST_ADDED, t_in, ALU.max, ALU.add).then_inc(s["ff_chain"], 1)

            def keep_rounded(i):
                dve.wait_ge(s["ff_chain"], 3 * i + 3)
                dve.wait_ge(s["t_psum"], i + 1)
                nc.vector.scalar_tensor_tensor(t_fp8[:, 0:FF], t_size, LEAST_ADDED, t_in, ALU.max, ALU.subtract).then_inc(s["t_done"], 1)

            def scale_result(i, j):
                dve.wait_ge(s["y2_psum"], i + 2)
                dve.wait_ge(s["y2_read"], i + 1)
                nc.vector.scalar_tensor_tensor(y_s, ps[:, 5, 0:D], tscale[:, j:j + 1], scale_rows[2], ALU.mult, ALU.mult).then_inc(s["y_scaled"], 1)

            def add_result(i):
                dve.wait_ge(s["y_scaled"], i + 1)
                nc.vector.tensor_tensor(x[:, bass.ds(i, 1), :], x[:, bass.ds(i, 1), :], y_s.unsqueeze(1), ALU.add).then_inc(s["y2_read"], 1)

            def sum_result(i):
                dve.wait_ge(s["y2_read"], i + 2)
                nc.vector.bn_stats(bn[:, bass.ds(i, 1), :].rearrange("p a b -> p (a b)"), x[:, bass.ds(i, 1), :].rearrange("p a b -> p (a b)")).then_inc(s["bn5"], 1)

            quantise_tile(TILES - 2, 0)
            add_attention(TILES - 1, 1)
            take_gate_and_up(0, 0)
            quantise_tile(TILES - 1, 1)
            take_gate_and_up(1, 1)
            hidden(0, 0)
            round_hidden(0)
            keep_rounded(0)
            with dve.Fori(0, TILES // 2 - 1) as turn:
                for j in range(1, 3):
                    i = 2 * turn + j
                    hidden(i, j % 2)
                    take_gate_and_up(i + 1, (j + 1) % 2)
                    scale_result(i - 1, (j - 1) % 2)
                    round_hidden(i)
                    add_result(i - 1)
                    keep_rounded(i)
                    sum_result(i - 1)
            hidden(TILES - 1, 1)
            scale_result(TILES - 2, 0)
            round_hidden(TILES - 1)
            add_result(TILES - 2)
            keep_rounded(TILES - 1)
            sum_result(TILES - 2)
            variances("bn5", "eps5", slice(0, TILES - 1))
            dve.wait_ge(s["rstd_out"], 1)
            normalise("out_done", slice(0, TILES // 2))
            scale_result(TILES - 1, 1)
            add_result(TILES - 1)
            sum_result(TILES - 1)
            variances("bn5", "eps5", slice(TILES - 1, TILES))
            normalise("out_done", slice(TILES // 2, TILES - 1))
            dve.wait_ge(s["rstd_out"], 2)
            normalise("out_done", slice(TILES - 1, TILES))

        @block.tensor
        def _(pe):
            pe.wait_ge(s["consts"], 1)
            for k in range(KD):
                for i in range(TILES):
                    if k == 0:
                        pe.wait_ge(s["xn"], i + 1)
                    ins = nc.tensor.transpose(ps[:, 2 * k + i // 4, (i % 4) * P:(i % 4 + 1) * P],
                                              xn[:, i, k * P:(k + 1) * P], ident[:, :])
                ins.then_inc(s["hs_psum"], 1)
            pe.wait_ge(s["ld_win"], 16)
            pe.wait_ge(s["hsT"], 2)
            for n in range(4 * CI):
                c, half = divmod(n, 2)
                if n >= 4:
                    pe.wait_ge(s["in_out"], n - 3)
                for k in range(KD):
                    ins = nc.tensor.matmul(ps[:, 4 + n % 4, :], w_in[:, k, c * P:(c + 1) * P], hT[:, k, half * HALF:(half + 1) * HALF],
                                           start=(k == 0), stop=(k == KD - 1))
                ins.then_inc(s["in_psum"], 1)
            pe.wait_ge(s["counted"], 2)
            pe.wait_ge(s["tables"], 1)

            def spread_diagonals(diagonals, chunks, bank):
                for at in range(0, chunks, 4):
                    n = min(4, chunks - at)
                    ins = nc.tensor.matmul(ps[:, bank + at // 4, 0:n * P], ones[:, :], diagonals[:, at:at + n, :].rearrange("p a b -> p (a b)"), start=True, stop=True)
                ins.then_inc(s["spread_psum"], 1)

            spread_diagonals(up_diag, KD, 2)
            spread_diagonals(down_diag, FCH, 0)
            pe.wait_ge(s["spread_done"], 2)
            pe.wait_ge(s["ld_wx"], 16)
            pe.wait_ge(s["conv_out"], CI)
            for i in range(TILES):
                for c in range(CI):
                    ins = nc.tensor.matmul(ps[:, i // 2, (i % 2) * D:(i % 2) * D + XP], xc[:, c, i * P:(i + 1) * P], w_x[:, c, :],
                                           start=(c == 0), stop=(c == CI - 1))
                ins.then_inc(s["xproj_psum"], 1)
            pe.wait_ge(s["xdbn"], 1)
            for i in range(TILES):
                ins = nc.tensor.transpose(ps[:, i // 4, (i % 4) * P:(i % 4 + 1) * P], xdb[:, i, 0:DR], ident[:, :])
            ins.then_inc(s["dtn_psum"], 1)
            pe.wait_ge(s["xdbn"], 3)
            for i in range(TILES):
                ins = nc.tensor.transpose(ps[0:2 * NS, 2 + i // 4, (i % 4) * P:(i % 4 + 1) * P], xdb[:, i, DR:XP], ident[:, :])
            ins.then_inc(s["bc_psum"], 1)
            pe.wait_ge(s["ld_wd"], 16)
            pe.wait_ge(s["dtn_sb"], 1)
            pe.wait_ge(s["in_out"], 4 * CI)
            for c in range(CI):
                if c >= 2:
                    pe.wait_ge(s["dt_act"], 3 * (c - 2) + 2)
                for half in range(2):
                    nc.tensor.matmul(ps[:, 4 + 2 * (c % 2) + half, :], w_dt[:, c * P:(c + 1) * P], dtnT[:, half * HALF:(half + 1) * HALF],
                                     start=True, stop=True).then_inc(s["dt_psum"], 1)
            pe.wait_ge(s["selectors"], 4)
            pe.wait_ge(s["bc_split"], 2)
            pe.wait_ge(s["dt_act"], 3 * CI)

            def spread(bank, row, ready):
                for half in range(2):
                    ins = nc.tensor.matmul(ps[:, bank + half, :], row_of[:, row, :], bc3[:, half * HALF:(half + 1) * HALF],
                                           start=True, stop=True)
                ins.then_inc(s[ready], 1)

            spread(0, 0, "b_ready")
            spread(2, NS, "c_ready")
            with pe.Fori(0, CI // 2) as pair:
                def sum_states(n, k):
                    if n == 0:
                        pe.wait_ge(s["y_drained"], pair * 2 + k + 1)
                    pe.wait_ge(s["hc_done"], (pair * NS + n) * 2 + k + 3)
                    for half in range(2):
                        ins = nc.tensor.matmul(ps[:, 4 + 2 * k + half, :], ident[:, :], hC[:, k, half * HALF:(half + 1) * HALF],
                                               start=(n == 0), stop=(n == NS - 1))
                    ins.then_inc(s["y_summed"], 1)

                for n in range(NS):
                    step = pair * NS + n
                    if n:
                        sum_states(n - 1, 0)
                    pe.wait_ge(s["dbx_done"], step * 2 + 2)
                    spread(0, (n + 1) % NS, "b_ready")
                    if n:
                        sum_states(n - 1, 1)
                    pe.wait_ge(s["c_copied"], step + 1)
                    spread(2, NS + (n + 1) % NS, "c_ready")
                sum_states(NS - 1, 0)
                sum_states(NS - 1, 1)
            pe.wait_ge(s["ld_wo"], 16)
            pe.wait_ge(s["ym_done"], 2)
            for cs in ((0, 1), (2, 3)):
                if cs[0]:
                    pe.wait_ge(s["ym_done"], CI)
                for i in range(TILES):
                    if cs[0] == 0 and i == 4:
                        pe.wait_ge(s["y_drained"], CI + 2)
                    for c in cs:
                        ins = nc.tensor.matmul(ps[:, i, 0:D], dtx[:, c, i * P:(i + 1) * P], w_out[:, c, :],
                                               start=(c == 0), stop=(c == CI - 1))
                    if cs[0]:
                        ins.then_inc(s["out_psum"], 1)
            kv = [0]

            def kv_bank():
                if kv[0] >= 6:
                    pe.wait_ge(s["kv_out"], kv[0] - 5)
                kv[0] += 1
                return 2 + (kv[0] - 1) % 6

            pe.wait_ge(s["res_done"], TILES)
            pe.wait_ge(s["ld_v"], 32)
            for n in range(PAIRS):
                bank = kv_bank()
                for hd in range(2):
                    ins = nc.tensor.matmul(ps[:, bank, hd * KVT:(hd + 1) * KVT], w_v[:, (2 * n + hd) * DH:(2 * n + hd + 1) * DH], ctxT, start=True, stop=True)
                ins.then_inc(s["kv_psum"], 1)
            pe.wait_ge(s["kv_out"], PAIRS)
            for k in range(KD):
                for i in range(TILES):
                    if k == 0:
                        pe.wait_ge(s["hn_done"], i + 1)
                    ins = nc.tensor.transpose(ps[:, 4 + 2 * k + i // 4, (i % 4) * P:(i % 4 + 1) * P], hn[:, i, k * P:(k + 1) * P], ident[:, :])
                ins.then_inc(s["hn_psum"], 1)
            pe.wait_ge(s["hfT_done"], KD)
            pe.wait_ge(s["res_done"], TILES)
            pe.wait_ge(s["ld_small"], 64)
            for i in range(TILES):
                for k in range(KD):
                    ins = nc.tensor.matmul(ps[:, 0, i * E:(i + 1) * E], hfT[:, k, i * P:(i + 1) * P], w_router[:, k, :],
                                           start=(k == 0), stop=(k == KD - 1))
            ins.then_inc(s["logit_psum"], 1)
            def values_times_output(n):
                bank = kv_bank()
                for b in range(2 * (n % 2), 2 * (n % 2) + 2):
                    for hd in range(2):
                        ins = nc.tensor.matmul(ps[hd * KV:(hd + 1) * KV, bank, (b % 2) * D:(b % 2 + 1) * D], vT[:, 2 * (n // 2) + hd, b * KV:(b + 1) * KV],
                                               w_o[:, 2 * (n // 2) + hd, :], start=True, stop=True)
                ins.then_inc(s["kv_psum"], 1)
            pe.wait_ge(s["ld_o"], 16)
            for n in range(EARLY):
                values_times_output(n)
            pe.wait_ge(s["tables"], 3)
            pe.wait_ge(s["picked_done"], 3)
            nc.tensor.matmul(ps[:, 1, 0:E], ones[:, :], earlier[:, TILES - 1, :], start=True, stop=False)
            nc.tensor.matmul(ps[:, 1, 0:E], ones[:, :], both[:, TILES - 1, :], start=False, stop=True)
            flat = lambda t: t[:, :, :].rearrange("p i e -> p (i e)")
            nc.tensor.matmul(ps[:, 1, E:E + TILES * E], ones[:, :], flat(earlier), start=True, stop=False)
            nc.tensor.matmul(ps[:, 1, E:E + TILES * E], before[:, :], flat(both), start=False, stop=True).then_inc(s["prefix_psum"], 1)
            def transpose_fp8(m):
                pe.wait_ge(s["quantised"], (2, 3, 1)[m])
                pe.wait_ge(s["tables"], 4)
                pe.wait_ge(s["slots_done"], 1)
                if m:
                    pe.wait_ge(s["wT_done"], {2: 2, 1: 4}[m])
                for half in range(2):
                    for n in range(FCH):
                        src = w_fp8[m][:, n, half * P:(half + 1) * P] if m < 2 else w_fp8[m][:, n % KD, (3 * half + n // KD) * P:(3 * half + n // KD + 1) * P]
                        ins = nc.tensor.transpose(ps[:, half, n * P // 2:(n + 1) * P // 2].bitcast(BF16), src, ident16[:, :])
                    ins.then_inc(s["wT_psum"], 1)

            for n in range(EARLY, 2 * PAIRS):
                values_times_output(n)
                if n in (8, 11, 15):
                    transpose_fp8({8: 0, 11: 2, 15: 1}[n])
            pe.wait_ge(s["kv_out"], kv[0])
            pe.wait_ge(s["slots_done"], 1)

            def transpose_rows(tile):
                pe.wait_ge(s["ld_rows"], 16 * tile + 16)
                pe.wait_ge(s["xT_done"], tile + 1)
                for k in range(KD):
                    ins = nc.tensor.transpose(ps[:, 7, k * P:(k + 1) * P], row_in[:, k * P:(k + 1) * P], ident[:, :])
                ins.then_inc(s["xT_psum"], 1)

            transpose_rows(0)
            for e in range(E):
                w1, w3, w2 = (w_moe[e % 2][:, k * FCH * D:(k + 1) * FCH * D].rearrange("p (k n) -> p k n", k=kk) for k, kk in ((0, KD), (1, KD), (2, FCH)))
                first = pe.value_load(bounds[0:1, e:e + 1], min_val=0, max_val=OUT_TILES - 1)
                last = pe.value_load(bounds[0:1, e + 1:e + 2], min_val=1, max_val=OUT_TILES)
                pe.wait_ge(s[f"ld_w{e % 2}"], 16 * (e // 2 + 1))
                with pe.Fori(first, last) as j:
                    pe.wait_ge(s["xT_done"], j + 2)
                    for q in range(FCH // 2):
                        pe.wait_ge(s["hid_done"], j * (FCH // 2) + q + 1)
                        for w, bank in ((w1, 2 * q), (w3, 2 * q + 1)):
                            for c in range(2):
                                for k in range(KD):
                                    at = (2 * q + c) * P
                                    ins = nc.tensor.matmul(ps[:, bank, c * P:(c + 1) * P], w[:, k, at:at + P], xT[:, k, :],
                                                           start=(k == 0), stop=(k == KD - 1))
                        ins.then_inc(s["gu_psum"], 1)
                    transpose_rows(j + 1)
                    pe.wait_ge(s["y_ready"], j + 1)
                    for c in range(FCH):
                        if c % 2 == 0:
                            pe.wait_ge(s["hid_done"], (j + 1) * (FCH // 2) + c // 2 + 1)
                        ins = nc.tensor.matmul(ps[:, 6, 0:D], hid[:, c, :], w2[:, c, :], start=(c == 0), stop=(c == FCH - 1))
                    ins.then_inc(s["y_psum"], 1)
            pe.wait_ge(s["y_ready"], last + 1)
            pe.wait_ge(s["xT_done"], last + 2)
            pe.wait_ge(s["ld_k"], 16)
            for n in range(8):
                bank = kv_bank()
                ins = nc.tensor.matmul(ps[:, bank, :], ctxT[:, (n // 4) * P:(n // 4 + 1) * P], w_k[:, (n % 4) * HALF:(n % 4 + 1) * HALF], start=True, stop=True)
                ins.then_inc(s["kv_psum"], 1)
            pe.wait_ge(s["wT_done"], 6)
            for n in range(PAIRS):
                if n % 3 == 0:
                    m = n // 3
                    pe.wait_ge(s["counted"], 3 + m)
                    if m:
                        pe.wait_ge(s["spread_done"], 2 + m)
                    spread_diagonals(diag[m], (FCH, FCH, KD)[m], 0)
                pe.wait_ge(s["k_normed"], 1 + n // (PAIRS // 4))
                bank = kv_bank()
                for hd in range(2):
                    for j in range(2):
                        at = (2 * n + hd) * DH
                        ins = nc.tensor.transpose(ps[:, bank, hd * KVT + j * P:hd * KVT + (j + 1) * P], k_raw[:, j, at:at + DH], ident[:, :])
                ins.then_inc(s["kv_psum"], 1)
            pe.wait_ge(s["ld_qT"], 16)
            for n in range(KD * PAIRS):
                bank = kv_bank()
                pair, k = divmod(n, KD)
                pe.wait_ge(s["kv_out"], 3 * PAIRS + 9 + pair)
                for hd in range(2):
                    ins = nc.tensor.matmul(ps[:, bank, hd * KVT:(hd + 1) * KVT], w_qT[:, 2 * pair + hd, k * P:(k + 1) * P], kT[:, 2 * pair + hd, :],
                                           start=True, stop=True)
                ins.then_inc(s["kv_psum"], 1)
            pe.wait_ge(s["kv_out"], kv[0])
            for i in range(TILES):
                pe.wait_ge(s["x1_done"], i + 1)
                for k in range(KD):
                    ins = nc.tensor.transpose(ps[:, 2 * k + i // 4, (i % 4) * P:(i % 4 + 1) * P], x[:, i, k * P:(k + 1) * P], ident[:, :])
                    if i == TILES - 1:
                        ins.then_inc(s["x1T_psum"], 1)
            pe.wait_ge(s["x1T_done"], 2)
            pe.wait_ge(s["ld_q"], 16)

            def scores_of(i, j, b):
                pe.wait_ge(s["x_now_ready"], i + 1)
                pe.wait_ge(s["s_taken"], i + 1)
                for half in range(2):
                    for k in range(KD):
                        ins = nc.tensor.matmul(ps[:, 2 + half, :], x_now[:, j, k, :],
                                               qk[k].rearrange("p b h t -> p b (h t)")[:, b, half * HALF:(half + 1) * HALF],
                                               start=(k == 0), stop=(k == KD - 1))
                ins.then_inc(s["s_psum"], 1)

            def queries_of(i, j, groups):
                for g in groups:
                    pe.wait_ge(s["q_squared"], 4 * i + g + 1)
                    for k in range(KD):
                        ins = nc.tensor.matmul(ps[:, g % 2, :], x_now[:, j, k, :], w_q[:, k, g * HALF:(g + 1) * HALF],
                                               start=(k == 0), stop=(k == KD - 1))
                    ins.then_inc(s["q_psum"], 1)

            def transpose_probs(i, j):
                pe.wait_ge(s["s_soft"], i + 3)
                for half in range(2):
                    pe.wait_ge(s["pT_done"], 2 * i + half + 1)
                    for n in range(4):
                        at = 8 * half + 2 * n
                        ins = nc.tensor.transpose(ps[:, 4 + half, n * P:(n + 1) * P], soft[:, j, at:at + 2, :].rearrange("p a b -> p (a b)"), ident[:, :])
                    ins.then_inc(s["pT_psum"], 1)

            def values_of(i, j, b):
                pe.wait_ge(s["attn_taken"], i + 1)
                for n in range(PAIRS):
                    if n % 4 == 0:
                        pe.wait_ge(s["pT_done"], 2 * i + n // 4 + 3)
                    ins = nc.tensor.matmul(ps[:, 6 + j, 0:D], pT[:, j, n, :], vw[:, n, b, :], start=(n == 0), stop=(n == PAIRS - 1))
                ins.then_inc(s["attn_psum"], 1)

            def transpose_tokens(half):
                pe.wait_ge(s["x_quant"], 4 * half + 4)
                for k in range(KD):
                    for i in range(4):
                        ins = nc.tensor.transpose(ps[:, 2 + 4 * half, (4 * k + i) * P // 2:(4 * k + i + 1) * P // 2].bitcast(BF16),
                                                  qx[:, 4 * half + i, k * P:(k + 1) * P], ident16[:, :])
                ins.then_inc(s["xT8_psum"], 1)

            scores_of(0, 0, 0)
            queries_of(0, 0, range(4))
            with pe.Fori(0, TILES // 2 - 1) as turn:
                for j in range(2):
                    scores_of(2 * turn + j + 1, (j + 1) % 2, turn + (j + 1) // 2)
                    queries_of(2 * turn + j + 1, (j + 1) % 2, (0, 1, 2))
                    transpose_probs(2 * turn + j, j)
                    queries_of(2 * turn + j + 1, (j + 1) % 2, (3,))
                    values_of(2 * turn + j, j, turn)
            scores_of(TILES - 1, 1, BATCH - 1)
            queries_of(TILES - 1, 1, (0, 1, 2))
            transpose_probs(TILES - 2, 0)
            queries_of(TILES - 1, 1, (3,))
            values_of(TILES - 2, 0, BATCH - 1)
            pe.wait_ge(s["s_taken"], TILES + 1)
            transpose_tokens(0)
            transpose_probs(TILES - 1, 1)
            values_of(TILES - 1, 1, BATCH - 1)
            pe.wait_ge(s["xT8_done"], 1)
            pe.wait_ge(s["q_squared"], 4 * TILES + 2)
            def gate_and_up(i):
                pe.wait_ge(s["ff_read"], i + 1)
                for m in range(2):
                    for part in range(2):
                        for k in range(KD):
                            ins = nc.tensor.matmul(ps[:, 2 * m + part, 0:FF // 2], qxT[:, k, bass.ts(i, P)], w_fp8T[m][:, k, part * FF // 2:(part + 1) * FF // 2],
                                                   start=(k == 0), stop=(k == KD - 1))
                ins.then_inc(s["ff_psum"], 1)

            def down(i):
                pe.wait_ge(s["t_done"], i + 1)
                pe.wait_ge(s["tT_done"], i + 1)
                for c in range(FCH):
                    ins = nc.tensor.transpose(ps[:, 4, c * P // 2:(c + 1) * P // 2].bitcast(BF16), t_fp8[:, c * P:(c + 1) * P], ident16[:, :])
                ins.then_inc(s["t_psum"], 1)
                pe.wait_ge(s["tT_done"], i + 2)
                pe.wait_ge(s["y2_read"], i + 1)
                for c in range(FCH):
                    ins = nc.tensor.matmul(ps[:, 5, 0:D], t_fp8T[:, c, :], w_fp8T[2][:, c, :], start=(c == 0), stop=(c == FCH - 1))
                ins.then_inc(s["y2_psum"], 1)

            gate_and_up(0)
            pe.wait_ge(s["attn_taken"], TILES + 1)
            transpose_tokens(1)
            gate_and_up(1)
            pe.wait_ge(s["xT8_done"], 2)
            pe.wait_ge(s["iota_done"], 2)
            with pe.Fori(0, TILES - 2) as i:
                gate_and_up(i + 2)
                down(i)
            down(TILES - 2)
            down(TILES - 1)


def kernel(**inputs):
    import concourse.bacc as bacc
    from concourse.bass_utils import run_bass_kernel_spmd

    def a(name):
        return np.asarray(inputs["L0_attn_" + name])

    def xa(name):
        return np.asarray(inputs["L0_xattn_" + name])

    def ff(name):
        return np.asarray(inputs["L0_ffn_" + name])

    def chunked(w):
        return w.reshape(-1, P, w.shape[1]).transpose(1, 0, 2)

    def index(v):
        return v.view(np.int32)[::2] if v.dtype.itemsize == 8 else v.view(np.int32)

    w_moe = np.zeros((E, P, MOE_W), np.float32)
    for e in range(E):
        for k, name in enumerate(("w1", "w3")):
            at = k * KD * FPAD
            w_moe[e, :, at:at + KD * FPAD].reshape(P, KD, FPAD)[:, :, :FF] = chunked(a(name)[e].T)
        w2 = np.zeros((FPAD, D), np.float32)
        w2[:FF] = a("w2")[e].T
        w_moe[e, :, 2 * KD * FPAD:] = chunked(w2).reshape(P, -1)
    up, down = index(ff("up_reorder_index")), index(ff("down_reorder_index"))
    down_at = np.zeros(FPAD, np.int32)
    down_at[:FF] = down
    lane = [a("conv_w"), a("conv_b")[:, None], a("dt_proj_b")[:, None], a("D_param")[:, None], a("A_log")]
    cols = [chunked(a("ln_in_w")[:, None])[:, :, 0], a("dt_ln_w")[:, None], chunked(a("ln_ff_w")[:, None])[:, :, 0],
            xa("gq")[:, None], xa("gk")[:, None]]
    data = dict(
        x=np.asarray(inputs["x"]), w_in=chunked(a("in_proj_w").T), cols=np.concatenate(cols, 1),
        bc_ln=np.concatenate([a("b_ln_w"), a("c_ln_w")])[:, None], lane=chunked(np.concatenate(lane, 1)),
        w_x=chunked(a("x_proj_w").T), w_dt=a("dt_proj_w").T, w_out=chunked(a("out_proj_w").T), ln_ff=a("ln_ff_w")[None],
        w_router=chunked(a("router_w").T), w_moe=w_moe, ctxT=np.asarray(inputs["ctx_1024"]).reshape(KVT, CTX).T,
        w_q=chunked(xa("Wq")), w_qT=xa("Wq").T.reshape(HEADS, DH, D).transpose(1, 0, 2), w_k=xa("Wk"), w_v=xa("Wv"), w_o=chunked(xa("Wo")),
        w_gate=ff("w_gate"), w_up=ff("w_up"), w_down=chunked(ff("w_down")),
        up_index=up[None], down_index=down[None], down_at=down_at.reshape(FCH, P).T)
    nc = bacc.Bacc("TRN2", target_bir_lowering=False, num_devices=1)
    arrays, inp = {}, {}
    for name, v in data.items():
        v = np.ascontiguousarray(v)
        arrays["in_" + name] = v
        inp[name] = nc.dram_tensor("in_" + name, v.shape, I32 if v.dtype == np.int32 else F32, kind="ExternalInput").ap()
    out = nc.dram_tensor("out", (BATCH, SEQ, D), F32, kind="ExternalOutput").ap()
    build(nc, inp, out)
    return run_bass_kernel_spmd(nc, [arrays], core_ids=[0]).results[0]["out"]
```
